# Optimizing a Trainium2 kernel written in Bass

```python
import numpy as np
import jax
import jax.numpy as jnp

def _softmax(x, axis=-1):
    return jax.nn.softmax(x, axis=axis)

def _gelu(x):
    return jax.nn.gelu(x, approximate=True)

def _silu(x):
    return jax.nn.silu(x)

def _sigmoid(x):
    return jax.nn.sigmoid(x)

def _layernorm(x, axis=-1, eps=1e-05):
    m = jnp.mean(x, axis=axis, keepdims=True)
    v = jnp.var(x, axis=axis, keepdims=True)
    return (x - m) / jnp.sqrt(v + eps)

def _scatter_add(tgt, idx, src, axis=0):
    return tgt.at[idx].add(src)

def _segment_sum(src, seg, n):
    return jax.ops.segment_sum(src, seg, n)
kernel_name = 'mk_adaln_d2_jaxref_r4_6d753e'

def setup_inputs(seed: int=0):
    np.random.seed(seed)
    _w = jnp.asarray

    def _L0_attn_setup():
        import jax, jax.numpy as jnp
        import numpy as np
        B, T, D, H = (2, 512, 256, 16)
        DH = D // H
        ROPE_BASE = 10000.0

        def _rope(Xh, cos, sin):
            x0 = Xh[..., 0::2]
            x1 = Xh[..., 1::2]
            r0 = cos * x0 - sin * x1
            r1 = sin * x0 + cos * x1
            return jnp.stack((r0, r1), axis=-1).reshape(Xh.shape)
        key = jax.random.key(seed)
        ks = jax.random.split(key, 5)
        s = 1.0 / np.sqrt(D)
        return {'X': jax.random.normal(ks[0], (B, T, D), dtype=jnp.float32), 'W_q': jax.random.normal(ks[1], (D, D), dtype=jnp.float32) * s, 'W_k': jax.random.normal(ks[2], (D, D), dtype=jnp.float32) * s, 'W_v': jax.random.normal(ks[3], (D, D), dtype=jnp.float32) * s, 'W_o': jax.random.normal(ks[4], (D, D), dtype=jnp.float32) * s}
    _L0_attn_in = _L0_attn_setup()

    def _L0_ffn_setup():
        import jax, jax.numpy as jnp
        import numpy as np
        B, S, H, E = (2, 2048, 256, 8)
        SCALE = 0.5
        key = jax.random.key(seed)
        k1, k2 = jax.random.split(key)
        x = jax.random.normal(k1, (B, S, H), dtype=jnp.float32)
        gate_w = jax.random.normal(k2, (E, H), dtype=jnp.float32) * 0.02
        coeff = SCALE * (1.0 + 0.05 * jnp.arange(E, dtype=jnp.float32))
        expert_w = coeff[:, None, None] * jnp.eye(H, dtype=jnp.float32)
        return {'x': x, 'gate_w': gate_w, 'expert_w': expert_w}
    _L0_ffn_in = _L0_ffn_setup()
    _L0_c = _w((lambda *s: np.random.randn(*s).astype(np.float32) * 0.05)(2, 256))
    _L0_wmod = _w((lambda *s: np.random.randn(*s).astype(np.float32) * 0.05)(256, 6 * 256) * 256 ** (-0.5))

    def _L1_attn_setup():
        import jax, jax.numpy as jnp
        import numpy as np
        L, B, E, H = (512, 4, 256, 8)
        D1 = 2 * E
        EPS = 1e-08

        def _toeplitz_mix(v, pos, zero, neg):
            b, h, n, d = v.shape
            m = 2 * n
            a = jnp.concatenate([zero, pos[:, :n - 1], jnp.zeros((h, 1), v.dtype), neg[:, :n - 1][:, ::-1]], axis=-1)
            af = jnp.fft.rfft(a, n=m, axis=-1)
            vf = jnp.fft.rfft(v, n=m, axis=-2)
            y = jnp.fft.irfft(af[None, :, :, None] * vf, n=m, axis=-2)
            return y[:, :, :n, :]
        key = jax.random.key(seed)
        ks = jax.random.split(key, 12)
        std = 0.02
        return {'query': jax.random.normal(ks[0], (L, B, E), jnp.float32), 'key': jax.random.normal(ks[1], (L, B, E), jnp.float32), 'value': jax.random.normal(ks[2], (L, B, E), jnp.float32), 'u_w': jax.random.normal(ks[3], (D1, E), jnp.float32) * std, 'u_b': jax.random.normal(ks[4], (D1,), jnp.float32) * std, 'v_w': jax.random.normal(ks[5], (D1, E), jnp.float32) * std, 'v_b': jax.random.normal(ks[6], (D1,), jnp.float32) * std, 'o_w': jax.random.normal(ks[7], (E, D1), jnp.float32) * std, 'o_b': jax.random.normal(ks[8], (E,), jnp.float32) * std, 'pos': jax.random.normal(ks[9], (H, L - 1), jnp.float32) * std, 'zero': jax.random.normal(ks[10], (H, 1), jnp.float32) * std, 'neg': jax.random.normal(ks[11], (H, L - 1), jnp.float32) * std}
    _L1_attn_in = _L1_attn_setup()

    def _L1_ffn_setup():
        import jax, jax.numpy as jnp
        import numpy as np
        E = 8
        K = 2
        key = jax.random.key(seed)
        ks = jax.random.split(key, 6)
        B, S, D, F = (4, 512, 256, 1024)
        s_d = 1.0 / np.sqrt(D).astype(np.float32)
        s_f = 1.0 / np.sqrt(F).astype(np.float32)
        return {'x': jax.random.normal(ks[0], (B, S, D), jnp.float32), 'ln_w': jnp.ones((D,), jnp.float32), 'Wg': jax.random.normal(ks[1], (D, E), jnp.float32) * s_d, 'bg': jnp.zeros((E,), jnp.float32), 'W1a': jax.random.normal(ks[2], (E, D, F), jnp.float32) * s_d, 'b1a': jnp.zeros((E, F), jnp.float32), 'W1b': jax.random.normal(ks[3], (E, D, F), jnp.float32) * s_d, 'b1b': jnp.zeros((E, F), jnp.float32), 'W2': jax.random.normal(ks[4], (E, F, D), jnp.float32) * s_f, 'b2': jnp.zeros((E, D), jnp.float32)}
    _L1_ffn_in = _L1_ffn_setup()
    _L1_c = _w((lambda *s: np.random.randn(*s).astype(np.float32) * 0.05)(2, 256))
    _L1_wmod = _w((lambda *s: np.random.randn(*s).astype(np.float32) * 0.05)(256, 6 * 256) * 256 ** (-0.5))
    _d = {'L0_attn_X': _L0_attn_in['X'], 'L0_attn_W_q': _L0_attn_in['W_q'], 'L0_attn_W_k': _L0_attn_in['W_k'], 'L0_attn_W_v': _L0_attn_in['W_v'], 'L0_attn_W_o': _L0_attn_in['W_o'], 'L0_ffn_gate_w': _L0_ffn_in['gate_w'], 'L0_ffn_expert_w': _L0_ffn_in['expert_w'], 'L0_c': _L0_c, 'L0_wmod': _L0_wmod, 'L1_attn_key': _L1_attn_in['key'], 'L1_attn_value': _L1_attn_in['value'], 'L1_attn_u_w': _L1_attn_in['u_w'], 'L1_attn_u_b': _L1_attn_in['u_b'], 'L1_attn_v_w': _L1_attn_in['v_w'], 'L1_attn_v_b': _L1_attn_in['v_b'], 'L1_attn_o_w': _L1_attn_in['o_w'], 'L1_attn_o_b': _L1_attn_in['o_b'], 'L1_attn_pos': _L1_attn_in['pos'], 'L1_attn_zero': _L1_attn_in['zero'], 'L1_attn_neg': _L1_attn_in['neg'], 'L1_ffn_ln_w': _L1_ffn_in['ln_w'], 'L1_ffn_Wg': _L1_ffn_in['Wg'], 'L1_ffn_bg': _L1_ffn_in['bg'], 'L1_ffn_W1a': _L1_ffn_in['W1a'], 'L1_ffn_b1a': _L1_ffn_in['b1a'], 'L1_ffn_W1b': _L1_ffn_in['W1b'], 'L1_ffn_b1b': _L1_ffn_in['b1b'], 'L1_ffn_W2': _L1_ffn_in['W2'], 'L1_ffn_b2': _L1_ffn_in['b2'], 'L1_c': _L1_c, 'L1_wmod': _L1_wmod}
    _x0 = _d['L0_attn_X']
    _d['L0_attn_X'] = jax.random.normal(jax.random.fold_in(jax.random.key(seed), 1), (2, 2048, 256), dtype=_x0.dtype)
    del _x0
    return _d

def reference(L0_attn_X, L0_attn_W_q, L0_attn_W_k, L0_attn_W_v, L0_attn_W_o, L0_ffn_gate_w, L0_ffn_expert_w, L0_c, L0_wmod, L1_attn_key, L1_attn_value, L1_attn_u_w, L1_attn_u_b, L1_attn_v_w, L1_attn_v_b, L1_attn_o_w, L1_attn_o_b, L1_attn_pos, L1_attn_zero, L1_attn_neg, L1_ffn_ln_w, L1_ffn_Wg, L1_ffn_bg, L1_ffn_W1a, L1_ffn_b1a, L1_ffn_W1b, L1_ffn_b1b, L1_ffn_W2, L1_ffn_b2, L1_c, L1_wmod):

    def _L0_attn_ref(X, W_q, W_k, W_v, W_o):
        import jax, jax.numpy as jnp
        import numpy as np
        B, T, D, H = (2, 512, 256, 16)
        DH = D // H
        ROPE_BASE = 10000.0

        def _rope(Xh, cos, sin):
            x0 = Xh[..., 0::2]
            x1 = Xh[..., 1::2]
            r0 = cos * x0 - sin * x1
            r1 = sin * x0 + cos * x1
            return jnp.stack((r0, r1), axis=-1).reshape(Xh.shape)
        b, t, d = X.shape
        Q = X @ W_q.T
        K = X @ W_k.T
        V = X @ W_v.T
        Qh = Q.reshape(b, t, H, DH).transpose(0, 2, 1, 3)
        Kh = K.reshape(b, t, H, DH).transpose(0, 2, 1, 3)
        Vh = V.reshape(b, t, H, DH).transpose(0, 2, 1, 3)
        theta = ROPE_BASE ** (-2.0 * jnp.arange(DH // 2, dtype=jnp.float32) / DH)
        pos = jnp.arange(t, dtype=jnp.float32)
        angles = pos[:, None] * theta[None, :]
        cos = jnp.cos(angles).astype(Qh.dtype)
        sin = jnp.sin(angles).astype(Qh.dtype)
        Qr = _rope(Qh, cos, sin)
        Kr = _rope(Kh, cos, sin)
        scores = jnp.einsum('bhqd,bhkd->bhqk', Qr, Kr) * DH ** (-0.5)
        causal = jnp.triu(jnp.ones((t, t), dtype=bool), 1)
        neg = jnp.finfo(scores.dtype).min
        scores = jnp.where(causal[None, None], neg, scores)
        pattern = jax.nn.softmax(scores, axis=-1)
        heads = jnp.einsum('bhqk,bhkd->bhqd', pattern, Vh)
        out = heads.transpose(0, 2, 1, 3).reshape(b, t, d)
        return out @ W_o.T

    def _L0_ffn_ref(x, gate_w, expert_w):
        import jax, jax.numpy as jnp
        import numpy as np
        B, S, H, E = (2, 2048, 256, 8)
        SCALE = 0.5
        scores = jnp.einsum('bsh,eh->bse', x, gate_w)
        chosen = jnp.argmax(scores, axis=-1)
        onehot = jax.nn.one_hot(chosen, gate_w.shape[0], dtype=x.dtype)
        expert_out = jnp.einsum('bsh,efh->bsef', x, expert_w)
        return x + jnp.einsum('bsef,bse->bsf', expert_out, onehot)

    def _L1_attn_ref(query, key, value, u_w, u_b, v_w, v_b, o_w, o_b, pos, zero, neg):
        import jax, jax.numpy as jnp
        import numpy as np
        L, B, E, H = (512, 4, 256, 8)
        D1 = 2 * E
        EPS = 1e-08

        def _toeplitz_mix(v, pos, zero, neg):
            b, h, n, d = v.shape
            m = 2 * n
            a = jnp.concatenate([zero, pos[:, :n - 1], jnp.zeros((h, 1), v.dtype), neg[:, :n - 1][:, ::-1]], axis=-1)
            af = jnp.fft.rfft(a, n=m, axis=-1)
            vf = jnp.fft.rfft(v, n=m, axis=-2)
            y = jnp.fft.irfft(af[None, :, :, None] * vf, n=m, axis=-2)
            return y[:, :, :n, :]
        n, b, e = query.shape
        rms = jnp.linalg.norm(query, axis=-1, keepdims=True) * e ** (-0.5)
        x = query / (rms + EPS)
        u = jax.nn.silu(jnp.einsum('nbe,fe->nbf', x, u_w) + u_b)
        v = jax.nn.silu(jnp.einsum('nbe,fe->nbf', x, v_w) + v_b)
        hd = v.shape[-1] // H
        vh = v.reshape(n, b, H, hd).transpose(1, 2, 0, 3)
        y = _toeplitz_mix(vh, pos, zero, neg)
        y = y.transpose(2, 0, 1, 3).reshape(n, b, H * hd)
        out = u * y
        return jnp.einsum('nbf,ef->nbe', out, o_w) + o_b + query

    def _L1_ffn_ref(x, ln_w, Wg, bg, W1a, b1a, W1b, b1b, W2, b2):
        import jax, jax.numpy as jnp
        import numpy as np
        E = 8
        K = 2
        B, S, D = x.shape
        eps = jnp.finfo(x.dtype).eps
        xn = x * jax.lax.rsqrt(jnp.mean(x * x, axis=-1, keepdims=True) + eps) * ln_w
        logits = xn @ Wg + bg
        vals, idx = jax.lax.top_k(logits, K)
        topk_w = jax.nn.softmax(vals, axis=-1)
        we = jnp.sum(jax.nn.one_hot(idx, E, dtype=x.dtype) * topk_w[..., None], axis=-2)
        T = B * S
        xf = xn.reshape(T, D)
        wef = we.reshape(T, E).T

        def step(acc, params):
            W1a_e, b1a_e, W1b_e, b1b_e, W2_e, b2_e, w_e = params
            a = xf @ W1a_e + b1a_e
            b = xf @ W1b_e + b1b_e
            y = jax.nn.silu(a) * b @ W2_e + b2_e
            return (acc + w_e[:, None] * y, None)
        out0 = jnp.zeros_like(xf)
        out, _ = jax.lax.scan(step, out0, (W1a, b1a, W1b, b1b, W2, b2, wef))
        return out.reshape(B, S, D)
    x = L0_attn_X
    mod = (_silu(L0_c) @ L0_wmod).reshape(L0_c.shape[0], 6, 1, -1)
    sa, ca, ga, sb, cb, gb = (mod[:, 0], mod[:, 1], mod[:, 2], mod[:, 3], mod[:, 4], mod[:, 5])
    ga = (2 * (ga >= 0) - 1) * jnp.maximum(jnp.abs(ga), 0.25)
    gb = (2 * (gb >= 0) - 1) * jnp.maximum(jnp.abs(gb), 0.25)
    h = _layernorm(x, axis=-1) * (1 + ca) + sa
    x = x + ga * _L0_attn_ref(h, L0_attn_W_q, L0_attn_W_k, L0_attn_W_v, L0_attn_W_o)
    h = _layernorm(x, axis=-1) * (1 + cb) + sb
    x = x + gb * _L0_ffn_ref(h, L0_ffn_gate_w, L0_ffn_expert_w)
    mod = (_silu(L1_c) @ L1_wmod).reshape(L1_c.shape[0], 6, 1, -1)
    sa, ca, ga, sb, cb, gb = (mod[:, 0], mod[:, 1], mod[:, 2], mod[:, 3], mod[:, 4], mod[:, 5])
    ga = (2 * (ga >= 0) - 1) * jnp.maximum(jnp.abs(ga), 0.25)
    gb = (2 * (gb >= 0) - 1) * jnp.maximum(jnp.abs(gb), 0.25)
    h = _layernorm(x, axis=-1) * (1 + ca) + sa
    x = x + ga * _L1_attn_ref(h, L1_attn_key, L1_attn_value, L1_attn_u_w, L1_attn_u_b, L1_attn_v_w, L1_attn_v_b, L1_attn_o_w, L1_attn_o_b, L1_attn_pos, L1_attn_zero, L1_attn_neg)
    h = _layernorm(x, axis=-1) * (1 + cb) + sb
    x = x + gb * _L1_ffn_ref(h, L1_ffn_ln_w, L1_ffn_Wg, L1_ffn_bg, L1_ffn_W1a, L1_ffn_b1a, L1_ffn_W1b, L1_ffn_b1b, L1_ffn_W2, L1_ffn_b2)
    return x

_drawn_inputs = setup_inputs


def setup_inputs(seed=0):
    import zlib

    import numpy as np

    out = dict(_drawn_inputs(seed))
    spreads = {'L1_ffn_ln_w': (1.0, 0.2),
     'L1_ffn_bg': (0.0, 0.281),
     'L1_ffn_b1a': (0.0, 0.751),
     'L1_ffn_b1b': (0.0, 0.77),
     'L1_ffn_b2': (0.0, 0.472)}
    factors = {'L0_ffn_gate_w': 3.688,
     'L1_attn_u_w': 8.0,
     'L1_attn_u_b': 8.0,
     'L1_attn_v_w': 8.0,
     'L1_attn_v_b': 8.0,
     'L1_attn_o_w': 8.0,
     'L1_attn_o_b': 8.0,
     'L1_attn_pos': 8.0,
     'L1_attn_zero': 8.0,
     'L1_attn_neg': 8.0}
    for name, (base, spread) in spreads.items():
        noise = np.random.default_rng([zlib.crc32(name.encode()), seed]).standard_normal(out[name].shape)
        drawn = base * np.exp(spread * noise) if base else spread * noise
        out[name] = jnp.asarray(drawn.astype(out[name].dtype))
    for name, factor in factors.items():
        out[name] = (out[name] * factor).astype(out[name].dtype)
    return out
```

```python
from contextlib import ExitStack

import numpy as np
import concourse.bass as bass
from concourse import mybir

F32 = mybir.dt.float32
BF16 = mybir.dt.bfloat16
I32 = mybir.dt.int32
U32 = mybir.dt.uint32
F32R = mybir.dt.float32r
ACT = mybir.ActivationFunctionType
ALU = mybir.AluOpType
AX = mybir.AxisListType

B, T, D = 2, 2048, 256
NTOK = B * T
P = 128
KT = D // P
CH = 512
TPC = CH // P
NCH = NTOK // CH
CPS = T // CH
NT = NTOK // P
H0, DH = 16, 16
HG = 4
NS = B * H0 // HG
JT = T // P
VW = 32
SPLIT = 3
Q_PARTS = (0, 0, 1, 1, 0, 2)
K_PARTS = (0, 1, 0, 1, 2, 0)
QROWS = DH * len(Q_PARTS)
EPS = 1e-5
MASKED = -1e30
E0 = 8
F1 = 512
FB1 = F1 // P
E1, FF = 8, 1024
FB = FF // P
ST = 512
SPT = ST // P
NTILES = E1 + (2 * NTOK - E1) // ST
NSLOT = NTILES * ST
ZW = SPT * D


class Count:

    def __init__(self, engine, sem, start=0):
        self.engine, self.sem, self.start, self.n = engine, sem, start, 0

    def add(self, instruction):
        instruction.then_inc(self.sem, 1)
        self.n += 1

    def wait(self):
        self.engine.wait_ge(self.sem, self.start + self.n)

    def step(self, instruction):
        self.add(instruction)
        self.wait()


def first(i):
    return isinstance(i, int) and i == 0


def at(i, step, n):
    return slice(i * step, i * step + n) if isinstance(i, int) else bass.ds(i * step, n)


class Mem:
    def __init__(self, nc, stack):
        self.nc, self.stack = nc, stack

    def sb(self, name, shape, dt=F32):
        return self.stack.enter_context(self.nc.sbuf_tensor(name, shape, dt))

    def ps(self, name, shape, dt=F32):
        return self.stack.enter_context(self.nc.psum_tensor(name, shape, dt))

    def sem(self, name):
        return self.nc.alloc_semaphore(name)


SA, CA, GA, SB_, CB, GB = range(6)


def modulation(nc, a, k):
    with ExitStack() as stack:
        m = Mem(nc, stack)
        wm = m.sb("wm", [P, 2, KT, 6 * D])
        cT = m.sb("cT", [P, 2, KT, B])
        silu_c = m.sb("silu_c", [P, 2, KT, B])
        ones = m.sb("mod_ones", [P, P])
        cb = m.sb("cb", [P, 2, KT, B, P])
        sign = m.sb("gate_sign", [P, B, D])
        mag = m.sb("gate_mag", [P, B, D])
        masks = m.sb("masks_f32", [P, 2, P])
        pm = m.ps("pmod", [P, 2, 2 * D])
        loaded = k.constants_loaded
        c_ready, cb_ready, ones_set = m.sem("silu_c_ready"), m.sem("cb_ready"), m.sem("mod_ones_set")
        product, copied, own = m.sem("mod_product"), m.sem("mod_copied"), m.sem("mod_own")
        x_loaded, stats_done = [m.sem(f"x_loaded{b}") for b in range(B)], m.sem("stats_done")
        LOADS = 6
        with nc.Block() as block:
            @block.gpsimd
            def _(pool):
                for b in range(B):
                    pool.dma_start(k.x[:, b * JT:(b + 1) * JT, :],
                                   a["x"][b * T:(b + 1) * T, :].rearrange("(t p) d -> p t d", p=P)).then_inc(x_loaded[b], 16)

            @block.sync
            def _(sp):
                sp.dma_start(cT[:, 0, :, :], a["cT0"]).then_inc(loaded, 16)
                sp.dma_start(cT[:, 1, :, :], a["cT1"]).then_inc(loaded, 16)
                for layer, name in enumerate(("wmod0", "wmod1")):
                    sp.dma_start(wm[:, layer, :, :], a[name].rearrange("(k p) n -> p k n", p=P)).then_inc(loaded, 16)
                sp.dma_start(k.ident[:, :], a["ident"]).then_inc(loaded, 16)
                sp.dma_start(masks[:, :, :], a["masks"]).then_inc(loaded, 16)
                sp.wait_ge(loaded, 16 * LOADS)

            @block.scalar
            def _(act):
                act.wait_ge(loaded, 16 * LOADS)
                nc.scalar.activation(silu_c[:, :, :, :], cT[:, :, :, :], ACT.Silu).then_inc(c_ready, 1)
                n = 0
                for layer in range(2):
                    for b in range(B):
                        for half in range(3):
                            act.wait_ge(product, n + 1)
                            nc.scalar.activation(
                                k.mods[layer][:, b, 2 * half:2 * half + 2, :],
                                pm[:, n % 2, :].rearrange("p (s d) -> p s d", s=2), ACT.Copy).then_inc(copied, 1)
                            n += 1

            @block.tensor
            def _(pe):
                pe.wait_ge(cb_ready, 2 * KT * B)
                n = 0
                for layer in range(2):
                    for b in range(B):
                        for half in range(3):
                            if n >= 2:
                                pe.wait_ge(copied, n - 1)
                            for kt in range(KT):
                                last = nc.tensor.matmul(
                                    pm[:, n % 2, :], cb[:, layer, kt, b, :],
                                    wm[:, layer, kt, 2 * half * D:(2 * half + 2) * D],
                                    start=kt == 0, stop=kt == KT - 1)
                            last.then_inc(product, 1)
                            n += 1

            @block.vector
            def _(dve):
                nc.vector.memset(ones[:, :], 1.0).then_inc(ones_set, 1)
                dve.wait_ge(ones_set, 1)
                dve.wait_ge(c_ready, 1)
                for layer in range(2):
                    for kt in range(KT):
                        for b in range(B):
                            nc.vector.tensor_scalar(cb[:, layer, kt, b, :], ones[:, :],
                                                    silu_c[:, layer, kt, b:b + 1], None, ALU.mult).then_inc(cb_ready, 1)
                for b in range(B):
                    dve.wait_ge(x_loaded[b], 16)
                    with dve.Fori(b * JT, (b + 1) * JT) as t:
                        nc.vector.bn_stats(out=k.stats[:, at(t, 1, 1), :].rearrange("p o s -> p (o s)"),
                                           in_=k.x[:, at(t, 1, 1), :].rearrange("p o d -> p (o d)")).then_inc(stats_done, 1)
                dve.wait_ge(loaded, 16 * LOADS)
                own_n = Count(dve, own)
                own_n.add(nc.vector.tensor_copy(k.identb[:, :], k.ident[:, :]))
                own_n.add(nc.vector.tensor_copy(k.masks[:, :, :], masks[:, :, :]))
                dve.wait_ge(copied, 6 * B)
                for mods in k.mods:
                    for which in (CA, CB):
                        own_n.add(nc.vector.tensor_scalar(mods[:, :, which, :], mods[:, :, which, :], 1.0, None, ALU.add))
                    for which in (GA, GB):
                        gate = mods[:, :, which, :]
                        own_n.wait()
                        own_n.add(nc.vector.tensor_scalar(sign[:, :, :], gate, 0.0, 2.0, ALU.is_ge, ALU.mult))
                        own_n.step(nc.vector.scalar_tensor_tensor(out=mag[:, :, :], in0=gate, scalar=-1.0, in1=gate,
                                                                  op0=ALU.mult, op1=ALU.max))
                        own_n.step(nc.vector.tensor_scalar(mag[:, :, :], mag[:, :, :], 0.25, None, ALU.max))
                        own_n.step(nc.vector.scalar_tensor_tensor(out=gate, in0=sign[:, :, :], scalar=-1.0,
                                                                  in1=mag[:, :, :], op0=ALU.add, op1=ALU.mult))


NORM_STEPS = TPC + 1
AGGREGATE_STEPS = 6


def aggregate(nc, own, k):
    (mean_e, m2_e), (mean_o, m2_o) = ((k.stats[:, :, i], k.stats[:, :, i + 1]) for i in (1, 4))
    own.add(nc.vector.tensor_tensor(k.mean[:, :], mean_e, mean_o, ALU.add))
    own.add(nc.vector.tensor_tensor(k.spread[:, :], mean_e, mean_o, ALU.subtract))
    own.step(nc.vector.tensor_tensor(k.ve[:, :], m2_e, m2_o, ALU.add))
    own.add(nc.vector.tensor_scalar(k.mean[:, :], k.mean[:, :], 0.5, None, ALU.mult))
    own.add(nc.vector.tensor_scalar(k.ve[:, :], k.ve[:, :], 1.0 / D, EPS, ALU.mult, ALU.add))
    own.step(nc.vector.scalar_tensor_tensor(out=k.spread[:, :], in0=k.spread[:, :], scalar=0.25, in1=k.spread[:, :],
                                            op0=ALU.mult, op1=ALU.mult))
    assert own.n == AGGREGATE_STEPS
    return nc.vector.tensor_tensor(k.ve[:, :], k.ve[:, :], k.spread[:, :], ALU.add)


def row_stats(nc, k, i, done):
    for u in range(TPC):
        t = at(i * TPC + u, 1, 1)
        nc.vector.bn_stats(out=k.stats[:, t, :].rearrange("p o s -> p (o s)"),
                           in_=k.x[:, t, :].rearrange("p o d -> p (o d)")).then_inc(done, 1)


def root(nc, pool, k, power_set, ve_ready, rstd_ready):
    nc.gpsimd.memset(k.neghalf[:, :], -0.5).then_inc(power_set, 1)
    pool.wait_ge(power_set, 1)
    pool.wait_ge(ve_ready, 1)
    nc.gpsimd.tensor_tensor(k.rstd[:, :], k.ve[:, :], k.neghalf[:, :], ALU.pow).then_inc(rstd_ready, 1)


def normalize(nc, k, own, i, h, scale, shift, done):
    for u in range(TPC):
        own.add(nc.vector.tensor_scalar(h[:, u, :], k.x[:, at(i * TPC + u, 1, 1), :].rearrange("p o d -> p (o d)"),
                                        k.mean[:, at(i * TPC + u, 1, 1)], k.rstd[:, at(i * TPC + u, 1, 1)],
                                        ALU.subtract, ALU.mult))
    own.wait()
    own.step(nc.vector.tensor_tensor(h, h, scale, ALU.mult))
    nc.vector.tensor_tensor(h, h, shift, ALU.add).then_inc(done, 1)


def projections(nc, a, k):
    with ExitStack() as stack:
        m = Mem(nc, stack)
        w = m.sb("wqkv", [P, KT, 5 * D])
        trig = m.sb("trig", [P, 2, T])
        h = m.sb("h", [P, TPC, D])
        hT = m.sb("hT", [P, KT, CH])
        rot = m.sb("rot", [P, 2, 2, KT, CH])
        rem = m.sb("rem", [P, 2, KT, CH])
        parts = m.sb("parts", [P, 2, SPLIT, KT, CH], BF16)
        va = m.sb("va", [P, TPC, H0, VW])
        p_t = m.ps("p_t", [P, KT, CH])
        p_qk = m.ps("p_qk", [P, 2, KT, CH])
        p_v = m.ps("p_v", [P, TPC, D])
        w_loaded = m.sem("w_loaded")
        ve_ready, rstd_ready = m.sem("a_ve_ready"), m.sem("a_rstd_ready")
        h_ready, hT_psum, hT_ready = m.sem("a_h_ready"), m.sem("a_hT_psum"), m.sem("a_hT_ready")
        qk_psum, v_psum = m.sem("a_qk_psum"), m.sem("a_v_psum")
        qk_taken, rot_ready = m.sem("a_qk_taken"), m.sem("a_rot_ready")
        part_act, part_dve = m.sem("a_part_act"), m.sem("a_part_dve")
        va_ready, parts_stored, va_stored = m.sem("a_va_ready"), m.sem("a_parts_stored"), m.sem("a_va_stored")
        own, power_set, ones_set = m.sem("a_own"), m.sem("a_power_set"), m.sem("a_ones_set")
        NHG = H0 // HG
        with nc.Block() as block:
            @block.sync
            def _(sp):
                def store(i):
                    b = i // CPS
                    c = i % CPS
                    for qk in range(2):
                        sp.wait_ge(part_dve, 4 * i + 2 * qk + 2)
                        for part in range(SPLIT):
                            sp.dma_start(
                                k.qk_scr[qk, part][at(b, D, D), at(c, CH, CH)].rearrange("(k p) t -> p k t", p=P),
                                parts[:, qk, part, :, :]).then_inc(parts_stored, 16)
                    sp.wait_ge(va_ready, i + 1)
                    for hg in range(NHG):
                        sp.dma_start(
                            k.v_scr[at(b * NHG + hg, 1, 1), :, at(c, TPC, TPC), :].rearrange("s p u n -> (s p) u n"),
                            va[:, :, HG * hg:HG * hg + HG, :].rearrange("p u h n -> p u (h n)")).then_inc(va_stored, 16)

                sp.dma_start(w[:, :, :], a["wqkv"].rearrange("(k p) n -> p k n", p=P)).then_inc(w_loaded, 16)
                sp.dma_start(trig[:, :, :], a["trig"]).then_inc(w_loaded, 16)
                with sp.Fori(0, NCH) as i:
                    store(i)
                sp.wait_ge(parts_stored, 16 * 2 * SPLIT * NCH)
                sp.wait_ge(va_stored, 16 * NHG * NCH)

            @block.gpsimd
            def _(pool):
                root(nc, pool, k, power_set, ve_ready, rstd_ready)

                def add(i, qk):
                    pool.wait_ge(qk_taken, 4 * i + 2 * qk + 2)
                    nc.gpsimd.tensor_tensor(rem[:, qk, :, :], rot[:, qk, 0, :, :], rot[:, qk, 1, :, :],
                                            ALU.add).then_inc(rot_ready, 1)

                with pool.Fori(0, NCH) as i:
                    add(i, 0)
                    add(i, 1)

            @block.vector
            def _(dve):
                nc.vector.memset(va[:, :, :, :], 1.0).then_inc(ones_set, 1)

                def norm(i):
                    c = Count(dve, own, AGGREGATE_STEPS + NORM_STEPS * i)
                    normalize(nc, k, c, i, h[:, :, :], k.mod(0, i // CPS, CA), k.mod(0, i // CPS, SA), h_ready)
                    assert c.n == NORM_STEPS

                def rotate(i, qk):
                    dve.wait_ge(qk_psum, 2 * i + qk + 1)
                    for s in range(2):
                        table = trig[:, s, at(i % CPS, CH, CH)]
                        nc.vector.tensor_tensor(rot[:, qk, s, :, :], p_qk[:, s, :, :],
                                                table.unsqueeze(1).to_broadcast([P, KT, CH]),
                                                ALU.mult).then_inc(qk_taken, 1)

                def split(i, qk):
                    dve.wait_ge(part_act, 4 * i + 2 * qk + 1)
                    nc.vector.tensor_tensor(rem[:, qk, :, :], rem[:, qk, :, :], parts[:, qk, 0, :, :],
                                            ALU.subtract).then_inc(part_dve, 1)
                    dve.wait_ge(part_act, 4 * i + 2 * qk + 2)
                    nc.vector.tensor_tensor(parts[:, qk, 2, :, :], rem[:, qk, :, :], parts[:, qk, 1, :, :],
                                            ALU.subtract).then_inc(part_dve, 1)

                aggregate(nc, Count(dve, own), k).then_inc(ve_ready, 1)
                dve.wait_ge(rstd_ready, 1)
                norm(0)
                dve.wait_ge(w_loaded, 32)
                with dve.Fori(0, NCH - 1) as i:
                    rotate(i, 0)
                    norm(i + 1)
                    split(i, 0)
                    rotate(i, 1)
                    split(i, 1)
                rotate(NCH - 1, 0)
                split(NCH - 1, 0)
                rotate(NCH - 1, 1)
                split(NCH - 1, 1)

            @block.scalar
            def _(act):
                def take_hT(i):
                    act.wait_ge(hT_psum, i + 1)
                    if not first(i):
                        act.wait_ge(qk_psum, 2 * i)
                    nc.scalar.activation(hT[:, :, :], p_t[:, :, :], ACT.Copy).then_inc(hT_ready, 1)

                def take_v(i):
                    act.wait_ge(v_psum, i + 1)
                    if first(i):
                        act.wait_ge(ones_set, 1)
                    else:
                        act.wait_ge(va_stored, 16 * NHG * i)
                    nc.scalar.activation(va[:, :, :, 0:DH], p_v[:, :, :].rearrange("p u (h d) -> p u h d", d=DH),
                                         ACT.Copy).then_inc(va_ready, 1)

                def split(i, qk):
                    act.wait_ge(rot_ready, 2 * i + qk + 1)
                    if not first(i):
                        act.wait_ge(parts_stored, 16 * 2 * SPLIT * i)
                    nc.scalar.activation(parts[:, qk, 0, :, :], rem[:, qk, :, :], ACT.Copy).then_inc(part_act, 1)
                    act.wait_ge(part_dve, 4 * i + 2 * qk + 1)
                    nc.scalar.activation(parts[:, qk, 1, :, :], rem[:, qk, :, :], ACT.Copy).then_inc(part_act, 1)

                take_hT(0)
                take_v(0)
                split(0, 0)
                take_hT(1)
                split(0, 1)
                with act.Fori(1, NCH - 1) as i:
                    take_v(i)
                    split(i, 0)
                    take_hT(i + 1)
                    split(i, 1)
                take_v(NCH - 1)
                split(NCH - 1, 0)
                split(NCH - 1, 1)

            @block.tensor
            def _(pe):
                def product(i, qk):
                    for s in range(2):
                        for mb in range(KT):
                            for kt in range(KT):
                                col = (2 * qk + s) * D + mb * P
                                last = nc.tensor.matmul(p_qk[:, s, mb, :], w[:, kt, col:col + P], hT[:, kt, :],
                                                        start=kt == 0, stop=kt == KT - 1)
                    last.then_inc(qk_psum, 1)

                def chunk(i):
                    pe.wait_ge(h_ready, i + 1)
                    if not first(i):
                        pe.wait_ge(hT_ready, i)
                    for kt in range(KT):
                        for u in range(TPC):
                            last = nc.tensor.transpose(p_t[:, kt, u * P:(u + 1) * P], h[:, u, kt * P:(kt + 1) * P],
                                                       k.ident[:, :])
                    last.then_inc(hT_psum, 1)
                    if first(i):
                        pe.wait_ge(w_loaded, 32)
                    pe.wait_ge(hT_ready, i + 1)
                    if not first(i):
                        pe.wait_ge(qk_taken, 4 * i)
                    product(i, 0)
                    if not first(i):
                        pe.wait_ge(va_ready, i)
                    for u in range(TPC):
                        for kt in range(KT):
                            last = nc.tensor.matmul(p_v[:, u, :], hT[:, kt, u * P:(u + 1) * P], w[:, kt, 4 * D:5 * D],
                                                    start=kt == 0, stop=kt == KT - 1)
                    last.then_inc(v_psum, 1)
                    pe.wait_ge(qk_taken, 4 * i + 2)
                    product(i, 1)

                chunk(0)
                with pe.Fori(1, NCH) as i:
                    chunk(i)


UNITS = sum(TPC * (c + 1) for c in range(CPS))
NBUF = 3


def attention(nc, a, k):
    with ExitStack() as stack:
        m = Mem(nc, stack)
        qa = m.sb("qa", [P, NBUF, HG, T], BF16)
        ka = m.sb("ka", [P, NBUF, HG, T], BF16)
        va = m.sb("va3", [P, NBUF, JT, HG * VW])
        probs = m.sb("probs", [P, 2, HG, CH])
        tile_max = m.sb("tile_max", [P, HG, TPC, CPS])
        row_max = m.sb("row_max", [P, HG, TPC])
        max_rest = m.sb("max_rest", [P, HG, TPC])
        max_parts = m.sb("max_parts", [P, TPC, SPLIT, HG], BF16)
        max_rows = m.sb("max_rows", [SPLIT * HG, 2, CH], BF16)
        o_sb = m.sb("o_sb", [P, 2, CH])
        recip = m.sb("recip", [P, TPC, HG])
        p_s = m.ps("p_s", [P, 2, CH])
        p_m = m.ps("p_m", [P, 2, 2, CH])
        p_o = m.ps("p_o", [P, CH])
        p_misc = m.ps("p_misc", [P, CH])
        stage_loaded = [m.sem(f"stage_loaded{n}") for n in range(NBUF)]
        scores_ready, probs_ready, probs_used = m.sem("scores_ready"), m.sem("probs_ready"), m.sem("probs_used")
        max_scores, max_taken = m.sem("max_scores"), m.sem("max_taken")
        max_parts_ready, max_turned, max_rows_ready = m.sem("max_parts_ready"), m.sem("max_turned"), m.sem("max_rows_ready")
        max_stored, max_placed = m.sem("max_stored"), m.sem("max_placed")
        o_taken, o_turned, att_ready = m.sem("o_taken"), m.sem("o_turned"), m.sem("att_ready")
        ones_set, own, recip_ready = m.sem("ones_set"), m.sem("b_own"), m.sem("recip_ready")
        zeros, zeros_set, slots_zeroed = m.sb("zeros", [P, ZW]), m.sem("zeros_set"), m.sem("slots_zeroed")
        LOADS = 2 * len(Q_PARTS) + 1
        NMAX = 2 * UNITS
        MAX_OWN = 4


        units = [(c, j) for c in range(CPS) for j in range(TPC * (c + 1))]
        max_units = [(c, i, bank, hp) for c in range(CPS) for i in range(TPC) for bank in range(c + 1)
                     for hp in range(HG // 2)]
        assert len(max_units) == NMAX == 2 * len(units)
        AFTER_O, AFTER_MAX_ROWS, AFTER_TURN_O = 0, 2, 3
        LOOPED = (NS - 2) // NBUF

        def ends_chunk(u):
            c, i, bank, hp = max_units[u]
            return (i, bank, hp) == (TPC - 1, c, HG // 2 - 1)

        def all_stages(engine, stage):
            with engine.Fori(0, LOOPED) as turn:
                for n in range(NBUF):
                    stage(NBUF * turn + n, n, True, turn)
            for s in range(NBUF * LOOPED, NS):
                stage(s, s % NBUF, s < NS - 1, s // NBUF)

        with nc.Block() as block:
            @block.gpsimd
            def _(pool):
                nc.gpsimd.memset(ka[QROWS:QROWS + SPLIT, :, :, :], 1.0).then_inc(ones_set, 1)
                for s in range(NS):
                    buf = s % NBUF
                    if s >= NBUF:
                        pool.wait_ge(probs_used, UNITS * (s - NBUF + 1))
                    for g, (qp, kp) in enumerate(zip(Q_PARTS, K_PARTS)):
                        for dst, qk, part in ((qa, 0, qp), (ka, 1, kp)):
                            src = k.qk_scr[qk, part][at(s, HG * DH, HG * DH), :].rearrange("(h d) t -> d h t", h=HG)
                            pool.dma_start(dst[DH * g:DH * (g + 1), buf, :, :], src).then_inc(stage_loaded[buf], 16)
                    pool.dma_start(va[:, buf, :, :], k.v_scr[s, :, :, :]).then_inc(stage_loaded[buf], 16)

            @block.sync
            def _(sp):
                def place(s, buf, c):
                    n = CPS * s + c
                    sp.wait_ge(max_rows_ready, n + 1)
                    sp.dma_start(k.max_scr[c % 2], max_rows[:, c % 2, :]).then_inc(max_stored, 16)
                    sp.wait_ge(max_stored, 16 * n + 16)
                    if not first(n):
                        sp.wait_ge(max_placed, 16 * n)
                    sp.dma_start(qa[QROWS:QROWS + SPLIT, buf, :, c * CH:(c + 1) * CH],
                                 k.max_scr[c % 2].rearrange("(o h) t -> o h t", o=SPLIT)).then_inc(max_placed, 16)

                def stage(s, buf, more, turn):
                    if more:
                        for c in range(CPS):
                            place(s + 1, (buf + 1) % NBUF, c)

                sp.wait_ge(stage_loaded[0], 16 * LOADS)
                for c in range(CPS):
                    place(0, 0, c)
                sp.wait_ge(zeros_set, 1)
                with sp.Fori(0, NTILES) as t:
                    sp.dma_start(k.x_slots[at(t, ST, ST), :].rearrange("(p u) d -> p (u d)", p=P), zeros[:, :]
                                 ).then_inc(slots_zeroed, 16)
                all_stages(sp, stage)
                sp.wait_ge(slots_zeroed, 16 * NTILES)

            @block.tensor
            def _(pe):
                def maximum(s, buf, u):
                    c, i, bank, hp = max_units[u]
                    width = CH if bank < c else P * (i + 1)
                    if u >= 2:
                        pe.wait_ge(max_taken, NMAX * s + u - 1)
                    for hh in range(2):
                        hd = 2 * hp + hh
                        q0 = (c * TPC + i) * P
                        last = nc.tensor.matmul(p_m[:, u % 2, hh, 0:width], qa[0:QROWS, buf, hd, q0:q0 + P],
                                                ka[0:QROWS, buf, hd, bank * CH:bank * CH + width],
                                                start=True, stop=bank < c)
                        if bank == c:
                            last = nc.tensor.matmul(p_m[:, u % 2, hh, width - P:width], k.identb[:, :],
                                                    k.masks[:, 0, :], start=False, stop=True)
                    last.then_inc(max_scores, 1)

                def scores(s, buf, n, h):
                    c, j = units[n]
                    lo = max(0, j - TPC * c) * P
                    if HG * n + h >= 2:
                        pe.wait_ge(probs_ready, HG * (UNITS * s + n) + h - 1)
                    last = nc.tensor.matmul(p_s[:, h % 2, lo:CH], ka[0:QROWS + SPLIT, buf, h, j * P:(j + 1) * P],
                                            qa[0:QROWS + SPLIT, buf, h, c * CH + lo:(c + 1) * CH],
                                            start=True, stop=j < TPC * c)
                    if j >= TPC * c:
                        last = nc.tensor.matmul(p_s[:, h % 2, lo:lo + P], k.identb[:, :], k.masks[:, 1, :],
                                                start=False, stop=True)
                    last.then_inc(scores_ready, 1)

                def values(s, buf, n):
                    c, j = units[n]
                    lo = max(0, j - TPC * c) * P
                    pe.wait_ge(probs_ready, HG * (UNITS * s + n) + HG)
                    if j == 0 and c:
                        pe.wait_ge(o_taken, CPS * s + c)
                    for h in range(HG):
                        last = nc.tensor.matmul(p_o[VW * h:VW * (h + 1), lo:CH], va[:, buf, j, VW * h:VW * (h + 1)],
                                                probs[:, n % 2, h, lo:CH], start=j == 0, stop=j == TPC * (c + 1) - 1)
                    last.then_inc(probs_used, 1)

                def turn_maxima(n):
                    pe.wait_ge(max_parts_ready, n + 1)
                    rows = p_misc[:, :].bitcast(BF16)
                    for i in range(TPC):
                        last = nc.tensor.transpose(rows[0:SPLIT * HG, i * P:(i + 1) * P],
                                                   max_parts[:, i, :, :].rearrange("p s h -> p (s h)"), k.identb[:, :])
                    last.then_inc(max_turned, 1)

                def turn_outputs(n, parity):
                    pe.wait_ge(o_taken, n + 1)
                    for u in range(TPC):
                        last = nc.tensor.transpose(p_misc[:, u * P:(u + 1) * P], o_sb[:, parity, u * P:(u + 1) * P],
                                                   k.ident[:, :])
                    last.then_inc(o_turned, 1)

                def turn_both(s, c, more):
                    if more:
                        pe.wait_ge(att_ready, CPS * s + c + 1)
                        turn_maxima(CPS * (s + 1) + c)

                def turn_o(s, c, more):
                    if more:
                        pe.wait_ge(max_rows_ready, CPS * (s + 1) + c + 1)
                    else:
                        pe.wait_ge(att_ready, CPS * s + c + 1)
                    turn_outputs(CPS * s + c, c % 2)

                def stage(s, buf, more, turn):
                    nbuf = (buf + 1) % NBUF
                    if more:
                        pe.wait_ge(stage_loaded[nbuf], 16 * LOADS * (turn + 1 + (buf + 1) // NBUF))
                    for n, (c, j) in enumerate(units):
                        if j == 0:
                            pe.wait_ge(max_placed, 16 * (CPS * s + c + 1))
                        for h in range(HG):
                            scores(s, buf, n, h)
                            if n and h == 1:
                                values(s, buf, n - 1)
                        if more:
                            maximum(s + 1, nbuf, 2 * n)
                            maximum(s + 1, nbuf, 2 * n + 1)
                        if c and j == AFTER_MAX_ROWS:
                            turn_both(s, c - 1, more)
                        if c and j == AFTER_TURN_O:
                            turn_o(s, c - 1, more)
                    values(s, buf, UNITS - 1)
                    turn_both(s, CPS - 1, more)
                    turn_o(s, CPS - 1, more)

                pe.wait_ge(stage_loaded[0], 16 * LOADS)
                pe.wait_ge(ones_set, 1)
                for u in range(NMAX):
                    maximum(0, 0, u)
                    if ends_chunk(u):
                        c = max_units[u][0]
                        if c:
                            pe.wait_ge(max_rows_ready, c)
                        turn_maxima(c)
                all_stages(pe, stage)

            @block.scalar
            def _(act):
                def exponentials(s, n):
                    c, j = units[n]
                    lo = max(0, j - TPC * c) * P
                    if n >= 2:
                        act.wait_ge(probs_used, UNITS * s + n - 1)
                    for h in range(HG):
                        act.wait_ge(scores_ready, HG * (UNITS * s + n) + h + 1)
                        nc.scalar.activation(probs[:, n % 2, h, lo:CH], p_s[:, h % 2, lo:CH], ACT.Exp,
                                             scale=DH ** -0.5).then_inc(probs_ready, 1)

                def take_o(s, c, n_last):
                    act.wait_ge(probs_used, UNITS * s + n_last + 1)
                    nc.scalar.activation(o_sb[:, c % 2, :], p_o[:, :], ACT.Copy).then_inc(o_taken, 1)

                def take_rows(n, c):
                    act.wait_ge(max_turned, n + 1)
                    if not (isinstance(n, int) and n < 2):
                        act.wait_ge(max_stored, 16 * (n - 1))
                    nc.scalar.activation(max_rows[:, c % 2, :], p_misc[:, :].bitcast(BF16)[0:SPLIT * HG, 0:CH],
                                         ACT.Copy).then_inc(max_rows_ready, 1)

                def stage(s, buf, more, turn):
                    for n, (c, j) in enumerate(units):
                        exponentials(s, n)
                        if c and j == AFTER_O:
                            take_o(s, c - 1, n - 1)
                        if c and j == AFTER_MAX_ROWS and more:
                            take_rows(CPS * (s + 1) + c - 1, c - 1)
                    take_o(s, CPS - 1, UNITS - 1)
                    if more:
                        take_rows(CPS * (s + 1) + CPS - 1, CPS - 1)

                for c in range(CPS):
                    take_rows(c, c)
                all_stages(act, stage)

            @block.vector
            def _(dve):
                def take_max(s, u):
                    c, i, bank, hp = max_units[u]
                    width = CH if bank < c else P * (i + 1)
                    dve.wait_ge(max_scores, NMAX * s + u + 1)
                    nc.vector.tensor_reduce(out=tile_max[:, 2 * hp:2 * hp + 2, i, bank], in_=p_m[:, u % 2, :, 0:width],
                                            op=ALU.max, axis=AX.X).then_inc(max_taken, 1)

                def split_max(s, c):
                    n = CPS * s + c
                    step = Count(dve, own, MAX_OWN * n)
                    dve.wait_ge(max_taken, NMAX * s + sum(ends_chunk(u) * (u + 1) for u in range(NMAX) if max_units[u][0] == c))
                    if not first(n):
                        dve.wait_ge(max_turned, n)
                    part = [max_parts[:, :, q, :].rearrange("p i h -> p h i") for q in range(SPLIT)]
                    step.step(nc.vector.tensor_reduce(out=row_max[:, :, :], in_=tile_max[:, :, :, 0:c + 1],
                                                      op=ALU.max, axis=AX.X))
                    step.step(nc.vector.tensor_scalar(part[0], row_max[:, :, :], -1.0, None, ALU.mult))
                    step.step(nc.vector.scalar_tensor_tensor(out=max_rest[:, :, :], in0=row_max[:, :, :], scalar=-1.0,
                                                             in1=part[0], op0=ALU.mult, op1=ALU.subtract))
                    step.step(nc.vector.tensor_copy(part[1], max_rest[:, :, :]))
                    nc.vector.tensor_tensor(part[2], max_rest[:, :, :], part[1], ALU.subtract).then_inc(max_parts_ready, 1)
                    assert step.n == MAX_OWN

                def divide(s, c):
                    n = CPS * s + c
                    b = s // (H0 // HG)
                    dve.wait_ge(o_turned, n + 1)
                    o = p_misc[:, :].rearrange("p (u h w) -> p u h w", u=TPC, h=HG)
                    nc.vector.reciprocal(recip[:, :, :], o[:, :, :, DH]).then_inc(recip_ready, 1)
                    dve.wait_ge(recip_ready, n + 1)
                    nc.vector.tensor_tensor(
                        k.x[:, at(b * JT + c * TPC, 1, TPC), at(s % (H0 // HG), HG * DH, HG * DH)]
                        .rearrange("p u (h d) -> p u h d", h=HG),
                        o[:, :, :, 0:DH], recip[:, :, :].unsqueeze(3).to_broadcast([P, TPC, HG, DH]),
                        ALU.mult).then_inc(att_ready, 1)

                def stage(s, buf, more, turn):
                    for n, (c, j) in enumerate(units):
                        if more:
                            for u in (2 * n, 2 * n + 1):
                                take_max(s + 1, u)
                                if ends_chunk(u):
                                    split_max(s + 1, c)
                        if c and j == AFTER_TURN_O:
                            divide(s, c - 1)
                    divide(s, CPS - 1)

                nc.vector.memset(zeros[:, :], 0.0).then_inc(zeros_set, 1)
                nc.vector.memset(recip[:, :, :], 0.0).then_inc(att_ready, 1)
                for u in range(NMAX):
                    take_max(0, u)
                    if ends_chunk(u):
                        split_max(0, max_units[u][0])
                all_stages(dve, stage)


def output_projection(nc, a, k):
    with ExitStack() as stack:
        m = Mem(nc, stack)
        w = m.sb("wo", [P, KT, D])
        xin = m.sb("o_xin", [P, 2, TPC, D])
        still = m.sb("o_still", [P, TPC, D])
        aT = m.sb("o_aT", [P, KT, CH])
        gated = m.sb("o_gated", [P, TPC, D])
        p_t = m.ps("o_pt", [P, KT, CH])
        p_o = m.ps("o_po", [P, TPC, D])
        w_loaded, still_ready, stats_done = m.sem("o_w_loaded"), m.sem("o_still_ready"), m.sem("o_stats_done")
        x_loaded = [m.sem(f"o_x_loaded{n}") for n in range(2)]
        turned, aT_ready, product = m.sem("o_turned_"), m.sem("o_aT_ready"), m.sem("o_product")
        scaled, x1_ready = m.sem("o_scaled"), m.sem("o_x1_ready")
        with nc.Block() as block:
            @block.sync
            def _(sp):
                def load(i, par):
                    sp.dma_start(xin[:, par, :, :],
                                 a["x"][at(i, CH, CH), :].rearrange("(u p) d -> p u d", p=P)).then_inc(x_loaded[par], 16)

                sp.dma_start(w[:, :, :], a["woT"].rearrange("(k p) n -> p k n", p=P)).then_inc(w_loaded, 16)
                load(0, 0)
                load(1, 1)
                with sp.Fori(1, NCH // 2) as i:
                    for par in range(2):
                        sp.wait_ge(x1_ready, 2 * i + par - 1)
                        load(2 * i + par, par)

            @block.scalar
            def _(act):
                def chunk(i):
                    if not first(i):
                        act.wait_ge(turned, i)
                    nc.scalar.activation(still[:, :, :], k.x[:, at(i, TPC, TPC), :], ACT.Copy).then_inc(still_ready, 1)
                    act.wait_ge(turned, i + 1)
                    if not first(i):
                        act.wait_ge(product, i)
                    nc.scalar.activation(aT[:, :, :], p_t[:, :, :], ACT.Copy).then_inc(aT_ready, 1)

                chunk(0)
                with act.Fori(1, NCH) as i:
                    chunk(i)

            @block.tensor
            def _(pe):
                def chunk(i):
                    pe.wait_ge(still_ready, i + 1)
                    for kt in range(KT):
                        for u in range(TPC):
                            last = nc.tensor.transpose(p_t[:, kt, u * P:(u + 1) * P], still[:, u, kt * P:(kt + 1) * P],
                                                       k.ident[:, :])
                    last.then_inc(turned, 1)
                    pe.wait_ge(aT_ready, i + 1)
                    if not first(i):
                        pe.wait_ge(scaled, i)
                    for u in range(TPC):
                        for kt in range(KT):
                            last = nc.tensor.matmul(p_o[:, u, :], aT[:, kt, u * P:(u + 1) * P], w[:, kt, :],
                                                    start=kt == 0, stop=kt == KT - 1)
                    last.then_inc(product, 1)

                pe.wait_ge(w_loaded, 16)
                chunk(0)
                with pe.Fori(1, NCH) as i:
                    chunk(i)

            @block.vector
            def _(dve):
                with dve.Fori(0, NCH // 2) as turn:
                    for par in range(2):
                        i = 2 * turn + par
                        dve.wait_ge(product, i + 1)
                        nc.vector.tensor_tensor(gated[:, :, :], p_o[:, :, :], k.mod(0, i // CPS, GA),
                                                ALU.mult).then_inc(scaled, 1)
                        dve.wait_ge(x_loaded[par], 16 * (turn + 1))
                        dve.wait_ge(scaled, i + 1)
                        nc.vector.tensor_tensor(k.x[:, at(i, TPC, TPC), :], gated[:, :, :], xin[:, par, :, :],
                                                ALU.add).then_inc(x1_ready, 1)
                        dve.wait_ge(x1_ready, i + 1)
                        row_stats(nc, k, i, stats_done)


def top1_experts(nc, a, k):
    BANKS = E0 * D // CH
    EPB = E0 // BANKS
    with ExitStack() as stack:
        m = Mem(nc, stack)
        w = m.sb("w_expert", [P, KT, E0 * D])
        gate = m.sb("w_gate0", [P, KT, E0])
        iota = m.sb("iota_e", [P, E0])
        h = m.sb("c_h", [P, 2, D])
        hT = m.sb("c_hT", [P, 2, KT, P])
        top, top_at, same = m.sb("c_top", [P, 1]), m.sb("c_top_at", [P, 1]), m.sb("c_same", [P, E0])
        onehot = m.sb("c_onehot", [P, 2, E0])
        acc = m.sb("c_acc", [P, D])
        p_e = m.ps("p_e", [P, BANKS, CH])
        p_t = m.ps("c_pt", [P, KT, P])
        p_g = m.ps("p_g", [P, E0])
        loaded, power_set = m.sem("c_loaded"), m.sem("c_power_set")
        ve_ready, rstd_ready, h_ready = m.sem("c_ve_ready"), m.sem("c_rstd_ready"), m.sem("c_h_ready")
        turned, hT_ready, gate_psum = m.sem("c_turned"), m.sem("c_hT_ready"), m.sem("c_gate_psum")
        gated, expert_psum, expert_taken = m.sem("c_gated"), m.sem("c_expert_psum"), m.sem("c_expert_taken")
        own, stats_done = m.sem("c_own"), m.sem("c_stats_done")
        LOADS, OWN_NORM, OWN_GATE = 3, 2, 3
        OWN = OWN_NORM + OWN_GATE

        def pairs(engine, tile):
            with engine.Fori(0, NT // 2 - 1) as i:
                tile(2 * i, 0, True)
                tile(2 * i + 1, 1, True)
            tile(NT - 2, 0, True)
            tile(NT - 1, 1, False)

        with nc.Block() as block:
            @block.sync
            def _(sp):
                sp.dma_start(w[:, :, :], a["expertT"].rearrange("(k p) n -> p k n", p=P)).then_inc(loaded, 16)
                sp.dma_start(gate[:, :, :], a["gateT"].rearrange("(k p) n -> p k n", p=P)).then_inc(loaded, 16)
                sp.dma_start(iota[:, :], a["iota8"]).then_inc(loaded, 16)
                sp.wait_ge(loaded, 16 * LOADS)

            @block.gpsimd
            def _(pool):
                root(nc, pool, k, power_set, ve_ready, rstd_ready)

            @block.scalar
            def _(act):
                def take(t, par, skip):
                    act.wait_ge(turned, t + 1)
                    if not skip:
                        act.wait_ge(expert_psum, BANKS * (t - 1))
                    nc.scalar.activation(hT[:, par, :, :], p_t[:, :, :], ACT.Copy).then_inc(hT_ready, 1)

                take(0, 0, True)
                take(1, 1, True)
                with act.Fori(1, NT // 2) as i:
                    take(2 * i, 0, False)
                    take(2 * i + 1, 1, False)

            @block.tensor
            def _(pe):
                def turn(t, par, skip):
                    pe.wait_ge(h_ready, t + 1)
                    if not skip:
                        pe.wait_ge(hT_ready, t)
                    for kt in range(KT):
                        last = nc.tensor.transpose(p_t[:, kt, :], h[:, par, kt * P:(kt + 1) * P], k.ident[:, :])
                    last.then_inc(turned, 1)

                def choose(t, par, skip):
                    pe.wait_ge(hT_ready, t + 1)
                    if not skip:
                        pe.wait_ge(gated, t)
                    for kt in range(KT):
                        last = nc.tensor.matmul(p_g[:, :], hT[:, par, kt, :], gate[:, kt, :], start=kt == 0, stop=kt == KT - 1)
                    last.then_inc(gate_psum, 1)

                def experts(t, par, bank):
                    pe.wait_ge(expert_taken, E0 * t + EPB * (bank + 1))
                    for kt in range(KT):
                        last = nc.tensor.matmul(p_e[:, bank, :], hT[:, par, kt, :], w[:, kt, bank * CH:(bank + 1) * CH],
                                                start=kt == 0, stop=kt == KT - 1)
                    last.then_inc(expert_psum, 1)

                def tile(t, par, more):
                    for bank in range(BANKS - 1):
                        experts(t, par, bank)
                    if more:
                        turn(t + 1, 1 - par, False)
                    experts(t, par, BANKS - 1)
                    if more:
                        choose(t + 1, 1 - par, False)

                pe.wait_ge(loaded, 16 * LOADS)
                turn(0, 0, True)
                choose(0, 0, True)
                pairs(pe, tile)

            @block.vector
            def _(dve):
                def norm(t, par):
                    c = Count(dve, own, AGGREGATE_STEPS + OWN * t)
                    c.step(nc.vector.tensor_scalar(h[:, par, :], k.x[:, at(t, 1, 1), :].rearrange("p o d -> p (o d)"),
                                                   k.mean[:, at(t, 1, 1)], k.rstd[:, at(t, 1, 1)],
                                                   ALU.subtract, ALU.mult))
                    c.step(nc.vector.tensor_tensor(h[:, par, :], h[:, par, :], k.mod1(0, t // JT, CB), ALU.mult))
                    nc.vector.tensor_tensor(h[:, par, :], h[:, par, :], k.mod1(0, t // JT, SB_), ALU.add).then_inc(h_ready, 1)

                def pick(t, par):
                    c = Count(dve, own, AGGREGATE_STEPS + OWN * t + OWN_NORM)
                    dve.wait_ge(gate_psum, t + 1)
                    c.step(nc.vector.tensor_reduce(out=top[:, :], in_=p_g[:, :], op=ALU.max, axis=AX.X))
                    c.step(nc.vector.scalar_tensor_tensor(out=same[:, :], in0=p_g[:, :], scalar=top[:, :], in1=iota[:, :],
                                                          op0=ALU.is_equal, op1=ALU.mult))
                    c.step(nc.vector.tensor_reduce(out=top_at[:, :], in_=same[:, :], op=ALU.min, axis=AX.X))
                    nc.vector.tensor_scalar(onehot[:, par, :], iota[:, :], top_at[:, :], None, ALU.is_equal).then_inc(gated, 1)
                    dve.wait_ge(gated, t + 1)

                def take(t, par, bank):
                    dve.wait_ge(expert_psum, BANKS * t + bank + 1)
                    for e in range(EPB * bank, EPB * (bank + 1)):
                        nc.vector.scalar_tensor_tensor(
                            out=acc[:, :], in0=p_e[:, bank, (e % EPB) * D:(e % EPB + 1) * D],
                            scalar=onehot[:, par, e:e + 1], in1=h[:, par, :] if e == 0 else acc[:, :],
                            op0=ALU.mult, op1=ALU.add).then_inc(expert_taken, 1)
                        dve.wait_ge(expert_taken, E0 * (t + 1) + e + 1)

                def tile(t, par, more):
                    take(t, par, 0)
                    take(t, par, 1)
                    if more:
                        norm(t + 1, 1 - par)
                    take(t, par, 2)
                    take(t, par, 3)
                    x = k.x[:, at(t, 1, 1), :].rearrange("p o d -> p (o d)")
                    nc.vector.tensor_tensor(acc[:, :], acc[:, :], k.mod1(0, t // JT, GB), ALU.mult).then_inc(k.scaled, 1)
                    dve.wait_ge(k.scaled, t + 1)
                    nc.vector.tensor_tensor(x, x, acc[:, :], ALU.add).then_inc(k.x2_ready, 1)
                    dve.wait_ge(k.x2_ready, t + 1)
                    nc.vector.bn_stats(out=k.stats[:, at(t, 1, 1), :].rearrange("p o s -> p (o s)"), in_=x).then_inc(stats_done, 1)
                    if more:
                        pick(t + 1, 1 - par)

                nc.vector.memset(acc[:, :], 0.0).then_inc(expert_taken, E0)
                dve.wait_ge(expert_taken, E0)
                aggregate(nc, Count(dve, own), k).then_inc(ve_ready, 1)
                dve.wait_ge(rstd_ready, 1)
                norm(0, 0)
                dve.wait_ge(loaded, 16 * LOADS)
                pick(0, 0)
                pairs(dve, tile)


def second_norm(nc, a, k, name, shift, scale, h_all, xn_all, xnT_all, weight, logits):
    with ExitStack() as stack:
        m = Mem(nc, stack)
        h = m.sb(name + "h", [P, TPC, D])
        xn = m.sb(name + "xn", [P, TPC, D])
        xnT = m.sb(name + "xnT", [P, KT, CH]) if xnT_all is None else None
        squares = m.sb(name + "squares", [P, D])
        ss, ms, rms, inv = (m.sb(name + n, [P, TPC]) for n in ("ss", "ms", "rms", "inv"))
        power = m.sb(name + "power", [P, TPC])
        p_t = m.ps(name + "pt", [P, KT, CH])
        p_l = m.ps(name + "pl", [P, TPC, E1])
        ve_ready, rstd_ready, h_ready = m.sem(name + "ve_ready"), m.sem(name + "rstd_ready"), m.sem(name + "h_ready")
        squared, ms_ready, rms_ready = m.sem(name + "squared"), m.sem(name + "ms_ready"), m.sem(name + "rms_ready")
        inv_ready, xn_ready, turned = m.sem(name + "inv_ready"), m.sem(name + "xn_ready"), m.sem(name + "turned")
        xnT_ready, h_kept, logit_psum = m.sem(name + "xnT_ready"), m.sem(name + "h_kept"), m.sem(name + "logit_psum")
        logits_taken, own, power_set = m.sem(name + "logits_taken"), m.sem(name + "own"), m.sem(name + "power_set")
        w_loaded, stepped = m.sem(name + "w_loaded"), m.sem(name + "stepped")
        if weight is not None:
            w_rms = m.sb(name + "w_rms", [P, D])
        if h_all is not None:
            o_bias = m.sb(name + "o_bias", [P, D])
        if logits is not None:
            w_l = m.sb(name + "w_l", [P, KT, E1])
            b_l = m.sb(name + "b_l", [P, E1])
        LOADS = (weight is not None) + (h_all is not None) + 2 * (logits is not None)
        with nc.Block() as block:
            @block.sync
            def _(sp):
                if weight is not None:
                    sp.dma_start(w_rms[:, :], weight.partition_broadcast(P)).then_inc(w_loaded, 16)
                if h_all is not None:
                    sp.dma_start(o_bias[:, :], a["o_b"].partition_broadcast(P)).then_inc(w_loaded, 16)
                if logits is not None:
                    sp.dma_start(w_l[:, :, :], a["Wg"].rearrange("(k p) n -> p k n", p=P)).then_inc(w_loaded, 16)
                    sp.dma_start(b_l[:, :], a["bg"].partition_broadcast(P)).then_inc(w_loaded, 16)
                sp.wait_ge(w_loaded, 16 * LOADS)

            @block.gpsimd
            def _(pool):
                root(nc, pool, k, power_set, ve_ready, rstd_ready)
                nc.gpsimd.memset(power[:, :], 0.5 if h_all is not None else -0.5).then_inc(power_set, 1)
                pool.wait_ge(power_set, 2)
                pool.wait_ge(w_loaded, 16 * LOADS)
                with pool.Fori(0, NCH) as i:
                    pool.wait_ge(ms_ready, i + 1)
                    nc.gpsimd.tensor_tensor(rms[:, :], ms[:, :], power[:, :], ALU.pow).then_inc(rms_ready, 1)
                    if h_all is not None:
                        nc.gpsimd.tensor_tensor(h_all[:, at(i, TPC, TPC), :], h[:, :, :],
                                                o_bias[:, :].unsqueeze(1).to_broadcast([P, TPC, D]),
                                                ALU.add).then_inc(h_kept, 1)

            @block.scalar
            def _(act):
                def chunk(i):
                    act.wait_ge(h_ready, i + 1)
                    for u in range(TPC):
                        if u or not first(i):
                            act.wait_ge(squared, TPC * i + u)
                        nc.scalar.activation(squares[:, :], h[:, u, :], ACT.Square, accum_out=ss[:, u:u + 1]).then_inc(squared, 1)
                    act.wait_ge(inv_ready, i + 1)
                    if not first(i):
                        act.wait_ge(turned, i)
                    for u in range(TPC):
                        nc.scalar.activation(xn[:, u, :], h[:, u, :], ACT.Copy, scale=inv[:, u:u + 1]).then_inc(xn_ready, 1)
                    act.wait_ge(turned, i + 1)
                    if xnT_all is not None:
                        dst = xnT_all[:, :, at(i, CH, CH)]
                    else:
                        dst = xnT[:, :, :]
                        if not first(i):
                            act.wait_ge(logit_psum, i)
                    nc.scalar.activation(dst, p_t[:, :, :], ACT.Copy).then_inc(xnT_ready, 1)

                chunk(0)
                with act.Fori(1, NCH) as i:
                    chunk(i)

            @block.tensor
            def _(pe):
                if logits is not None:
                    pe.wait_ge(w_loaded, 16 * LOADS)

                def chunk(i):
                    pe.wait_ge(xn_ready if weight is None else stepped, TPC * i + TPC if weight is None else i + 1)
                    if not first(i):
                        pe.wait_ge(xnT_ready, i)
                    for kt in range(KT):
                        for u in range(TPC):
                            last = nc.tensor.transpose(p_t[:, kt, u * P:(u + 1) * P], xn[:, u, kt * P:(kt + 1) * P],
                                                       k.ident[:, :])
                    last.then_inc(turned, 1)
                    if logits is not None:
                        pe.wait_ge(xnT_ready, i + 1)
                        if not first(i):
                            pe.wait_ge(logits_taken, i)
                        for u in range(TPC):
                            for kt in range(KT):
                                last = nc.tensor.matmul(p_l[:, u, :], xnT[:, kt, u * P:(u + 1) * P], w_l[:, kt, :],
                                                        start=kt == 0, stop=kt == KT - 1)
                        last.then_inc(logit_psum, 1)

                chunk(0)
                with pe.Fori(1, NCH) as i:
                    chunk(i)

            @block.vector
            def _(dve):
                OWN = NORM_STEPS + (1 if h_all is not None else 0)
                dve.wait_ge(w_loaded, 16 * LOADS)
                aggregate(nc, Count(dve, own), k).then_inc(ve_ready, 1)
                dve.wait_ge(rstd_ready, 1)

                def chunk(i):
                    c = Count(dve, own, AGGREGATE_STEPS + OWN * i)
                    if not first(i):
                        dve.wait_ge(xn_ready, TPC * i)
                        if h_all is not None:
                            dve.wait_ge(h_kept, i)
                    b = i // CPS
                    normalize(nc, k, c, i, h[:, :, :], k.mod(1, b, scale), k.mod(1, b, shift), h_ready)
                    dve.wait_ge(squared, TPC * i + TPC)
                    if h_all is not None:
                        nc.vector.tensor_scalar(ms[:, :], ss[:, :], 1.0 / D, None, ALU.mult).then_inc(ms_ready, 1)
                        dve.wait_ge(rms_ready, i + 1)
                        c.step(nc.vector.tensor_scalar(rms[:, :], rms[:, :], 1e-8, None, ALU.add))
                        nc.vector.reciprocal(inv[:, :], rms[:, :]).then_inc(inv_ready, 1)
                    else:
                        nc.vector.tensor_scalar(ms[:, :], ss[:, :], 1.0 / D, float(np.finfo(np.float32).eps),
                                                ALU.mult, ALU.add).then_inc(ms_ready, 1)
                        dve.wait_ge(rms_ready, i + 1)
                        nc.vector.tensor_copy(inv[:, :], rms[:, :]).then_inc(inv_ready, 1)
                    if weight is not None:
                        dve.wait_ge(xn_ready, TPC * i + TPC)
                        nc.vector.tensor_tensor(xn[:, :, :], xn[:, :, :], w_rms[:, :].unsqueeze(1).to_broadcast([P, TPC, D]),
                                                ALU.mult).then_inc(stepped, 1)
                        dve.wait_ge(stepped, i + 1)
                        nc.vector.tensor_copy(xn_all[:, at(i, TPC, TPC), :], xn[:, :, :]).then_inc(h_kept, 1)
                        dve.wait_ge(h_kept, i + 1)
                    if logits is not None:
                        dve.wait_ge(logit_psum, i + 1)
                        nc.vector.tensor_tensor(logits[:, at(i, TPC, TPC), :], p_l[:, :, :],
                                                b_l[:, :].unsqueeze(1).to_broadcast([P, TPC, E1]),
                                                ALU.add).then_inc(logits_taken, 1)
                    assert c.n == OWN

                chunk(0)
                with dve.Fori(1, NCH) as i:
                    chunk(i)


def mix(nc, a, k, h_all, xnT_all):
    with ExitStack() as stack:
        m = Mem(nc, stack)
        w = m.sb("w_uv", [P, KT, 2 * F1])
        wo = m.sb("w_o1", [P, FB1, D])
        bias = m.sb("b_uv", [P, 2 * FB1])
        toep = m.sb("toep", [P, 3, FB1])
        u_sb = m.sb("u_sb", [P, B, FB1, CH])
        v_sb = m.sb("v_sb", [P, B, FB1, CH])
        y_sb = m.sb("y_sb", [P, B, FB1, CH])
        p_uv = m.ps("p_uv", [P, 4, CH])
        p_o = m.ps("d_po", [P, B, TPC, D])
        loaded, uv_psum, uv_ready = m.sem("d_loaded"), m.sem("d_uv_psum"), m.sem("d_uv_ready")
        own, g_ready, product, x3_ready = m.sem("d_own"), m.sem("d_g_ready"), m.sem("d_product"), m.sem("d_x3_ready")
        taken, taken_stats = m.sem("d_taken"), m.sem("d_stats_done")
        LOADS = 4
        NB = 2 * B * FB1
        order = [(1, n, f) for n in range(B) for f in range(FB1)] + [(0, n, f) for n in range(B) for f in range(FB1)]
        OWN = 4 * FB1 + B
        with nc.Block() as block:
            @block.sync
            def _(sp):
                sp.dma_start(w[:, :, :], a["w_uv"].rearrange("(k p) n -> p k n", p=P)).then_inc(loaded, 16)
                sp.dma_start(wo[:, :, :], a["o_wT"].rearrange("(f p) n -> p f n", p=P)).then_inc(loaded, 16)
                sp.dma_start(bias[:, :], a["b_uv"]).then_inc(loaded, 16)
                sp.dma_start(toep[:, :, :], a["toep"]).then_inc(loaded, 16)
                sp.wait_ge(loaded, 16 * LOADS)

            @block.tensor
            def _(pe):
                def chunk(c):
                    for q, (is_v, n, f) in enumerate(order):
                        if q >= 4 or not first(c):
                            pe.wait_ge(uv_ready, NB * c + q - 3)
                        for kt in range(KT):
                            last = nc.tensor.matmul(p_uv[:, q % 4, :], w[:, kt, is_v * F1 + f * P:is_v * F1 + (f + 1) * P],
                                                    xnT_all[:, kt, at(n * CPS + c, CH, CH)],
                                                    start=kt == 0, stop=kt == KT - 1)
                        last.then_inc(uv_psum, 1)
                    for n in range(B):
                        pe.wait_ge(g_ready, B * c + n + 1)
                        if not first(c):
                            pe.wait_ge(taken, B * (c - 1) + n + 1)
                        for u in range(TPC):
                            for f in range(FB1):
                                last = nc.tensor.matmul(p_o[:, n, u, :], y_sb[:, n, f, u * P:(u + 1) * P], wo[:, f, :],
                                                        start=f == 0, stop=f == FB1 - 1)
                        last.then_inc(product, 1)

                pe.wait_ge(loaded, 16 * LOADS)
                chunk(0)
                with pe.Fori(1, CPS) as c:
                    chunk(c)

            @block.scalar
            def _(act):
                def chunk(c):
                    for q, (is_v, n, f) in enumerate(order):
                        act.wait_ge(uv_psum, NB * c + q + 1)
                        if q == 0 and not first(c):
                            act.wait_ge(g_ready, B * c)
                        dst = v_sb if is_v else u_sb
                        nc.scalar.activation(dst[:, n, f, :], p_uv[:, q % 4, :], ACT.Silu,
                                             bias=bias[:, is_v * FB1 + f:is_v * FB1 + f + 1]).then_inc(uv_ready, 1)

                act.wait_ge(loaded, 16 * LOADS)
                chunk(0)
                with act.Fori(1, CPS) as c:
                    chunk(c)

            @block.vector
            def _(dve):
                dve.wait_ge(loaded, 16 * LOADS)

                def chunk(c):
                    cnt = Count(dve, own, OWN * c)
                    dve.wait_ge(uv_ready, NB * c + B * FB1)
                    if not first(c):
                        dve.wait_ge(product, B * c)
                    for f in range(FB1):
                        for n, which in ((0, 2), (1, 1)):
                            cnt.add(nc.vector.tensor_scalar(y_sb[:, n, f, :], v_sb[:, 1 - n, f, :],
                                                            toep[:, which, f:f + 1], None, ALU.mult))
                    cnt.wait()
                    for f in range(FB1):
                        for n in range(B):
                            cnt.add(nc.vector.scalar_tensor_tensor(out=y_sb[:, n, f, :], in0=v_sb[:, n, f, :],
                                                                   scalar=toep[:, 0, f:f + 1], in1=y_sb[:, n, f, :],
                                                                   op0=ALU.mult, op1=ALU.add))
                    cnt.wait()
                    for n in range(B):
                        dve.wait_ge(uv_ready, NB * c + B * FB1 + FB1 * (n + 1))
                        nc.vector.tensor_tensor(y_sb[:, n, :, :], y_sb[:, n, :, :], u_sb[:, n, :, :], ALU.mult).then_inc(g_ready, 1)
                    for n in range(B):
                        hh = h_all[:, at(n * CPS + c, TPC, TPC), :]
                        x = k.x[:, at(n * CPS + c, TPC, TPC), :]
                        dve.wait_ge(product, B * c + n + 1)
                        nc.vector.tensor_tensor(hh, p_o[:, n, :, :], hh, ALU.add).then_inc(taken, 1)
                        dve.wait_ge(taken, B * c + n + 1)
                        cnt.step(nc.vector.tensor_tensor(hh, hh, k.mod(1, n, GA), ALU.mult))
                        nc.vector.tensor_tensor(x, x, hh, ALU.add).then_inc(x3_ready, 1)
                        dve.wait_ge(x3_ready, B * c + n + 1)
                        row_stats(nc, k, n * CPS + c, taken_stats)
                    assert cnt.n == OWN

                chunk(0)
                with dve.Fori(1, CPS) as c:
                    chunk(c)


def route(nc, a, k, logits, xn_all):
    with ExitStack() as stack:
        m = Mem(nc, stack)
        iota, later, ones = m.sb("r_iota", [P, E1]), m.sb("r_later", [P, P]), m.sb("r_ones", [P, P])
        tiles = m.sb("r_tiles", [P, NTILES])
        best = m.sb("r_best", [P, 2, NT])
        same, rest = m.sb("r_same", [P, NT, E1]), m.sb("r_rest", [P, NT, E1])
        first_at = m.sb("r_first_at", [P, NT])
        onehot = m.sb("r_onehot", [P, 2, NT, E1])
        chosen, total = m.sb("r_chosen", [P, NT, E1]), m.sb("r_total", [P, NT, E1])
        run = m.sb("r_run", [P, 2, NT, E1])
        count_i = m.sb("r_count_i", [P, E1], I32)
        ntile, ends = m.sb("r_ntile", [P, E1]), m.sb("r_ends", [P, 2, E1])
        start = m.sb("r_start", [P, E1])
        slot = m.sb("r_slot", [P, NT])
        gap, weight_sum = m.sb("r_gap", [P, NT]), m.sb("r_weight_sum", [P, NT])
        owner, owner_f = m.sb("r_owner", [P, NTILES, E1]), m.sb("r_owner_f", [P, NTILES])
        p_rank, p_total = m.ps("p_rank", [P, NT, E1]), m.ps("p_total", [P, NT, E1])
        loaded, own, chosen_ready, counted = m.sem("r_loaded"), m.sem("r_own"), m.sem("r_chosen_ready"), m.sem("r_counted")
        gap_ready, exp_ready, slots_ready, scattered = (m.sem("r_gap_ready"), m.sem("r_exp_ready"),
                                                        m.sem("r_slots_ready"), m.sem("r_scattered"))
        LOADS = 4
        with nc.Block() as block:
            @block.sync
            def _(sp):
                for dst, src in ((iota, "iota8"), (later, "before"), (ones, "ones"), (tiles, "iota_tiles")):
                    sp.dma_start(dst[:, :], a[src]).then_inc(loaded, 16)
                sp.wait_ge(loaded, 16 * LOADS)

            @block.tensor
            def _(pe):
                pe.wait_ge(loaded, 16 * LOADS)
                pe.wait_ge(chosen_ready, 1)
                nc.tensor.matmul(p_rank[:, :, :], later[:, :], chosen[:, :, :], start=True, stop=True).then_inc(counted, 1)
                nc.tensor.matmul(p_total[:, :, :], ones[:, :], chosen[:, :, :], start=True, stop=True).then_inc(counted, 1)

            @block.scalar
            def _(act):
                act.wait_ge(gap_ready, 1)
                nc.scalar.activation(k.weights[:, 1, :], gap[:, :], ACT.Exp).then_inc(exp_ready, 1)

            @block.vector
            def _(dve):
                dve.wait_ge(loaded, 16 * LOADS)
                c = Count(dve, own)

                def tt(out, x, y, op):
                    c.step(nc.vector.tensor_tensor(out, x, y, op))

                def ts(out, x, s1, s2, op1, op2=None):
                    if op2 is None:
                        c.step(nc.vector.tensor_scalar(out, x, s1, None, op1))
                    else:
                        c.step(nc.vector.tensor_scalar(out, x, s1, s2, op1, op2))

                def wide(x, n=E1):
                    return x.unsqueeze(2).to_broadcast([P, NT, n])

                iota_all = iota[:, :].unsqueeze(1).to_broadcast([P, NT, E1])
                for q in range(2):
                    src = logits[:, :, :] if q == 0 else rest[:, :, :]
                    c.step(nc.vector.tensor_reduce(out=best[:, q, :], in_=src, op=ALU.max, axis=AX.X))
                    tt(same[:, :, :], src, wide(best[:, q, :]), ALU.is_equal)
                    c.step(nc.vector.scalar_tensor_tensor(out=same[:, :, :], in0=iota_all, scalar=0.0,
                                                          in1=same[:, :, :], op0=ALU.add, op1=ALU.mult))
                    c.step(nc.vector.tensor_reduce(out=first_at[:, :], in_=same[:, :, :], op=ALU.min, axis=AX.X))
                    tt(onehot[:, q, :, :], iota_all, wide(first_at[:, :]), ALU.is_equal)
                    if q == 0:
                        c.step(nc.vector.scalar_tensor_tensor(out=rest[:, :, :], in0=onehot[:, 0, :, :], scalar=MASKED,
                                                              in1=logits[:, :, :], op0=ALU.mult, op1=ALU.add))
                nc.vector.tensor_tensor(chosen[:, :, :], onehot[:, 0, :, :], onehot[:, 1, :, :], ALU.add).then_inc(chosen_ready, 1)
                nc.vector.tensor_tensor(gap[:, :], best[:, 1, :], best[:, 0, :], ALU.subtract).then_inc(gap_ready, 1)

                dve.wait_ge(exp_ready, 1)
                ts(weight_sum[:, :], k.weights[:, 1, :], 1.0, None, ALU.add)
                c.step(nc.vector.reciprocal(k.weights[:, 0, :], weight_sum[:, :]))
                tt(k.weights[:, 1, :], k.weights[:, 1, :], k.weights[:, 0, :], ALU.mult)

                dve.wait_ge(counted, 2)
                c.step(nc.vector.tensor_copy(total[:, :, :], p_total[:, :, :]))
                c.step(nc.vector.tensor_copy(run[:, 0, :, :], total[:, :, :]))
                now, step = 0, 1
                while step < NT:
                    c.add(nc.vector.tensor_copy(run[:, 1 - now, 0:step, :], run[:, now, 0:step, :]))
                    tt(run[:, 1 - now, step:NT, :], run[:, now, step:NT, :], run[:, now, 0:NT - step, :], ALU.add)
                    now, step = 1 - now, 2 * step
                ts(ends[:, 0, :], run[:, now, NT - 1, :], float(ST - 1), None, ALU.add)
                c.step(nc.vector.tensor_copy(count_i[:, :], ends[:, 0, :]))
                ts(count_i[:, :], count_i[:, :], ST.bit_length() - 1, None, ALU.logical_shift_right)
                c.step(nc.vector.tensor_copy(ntile[:, :], count_i[:, :]))
                c.step(nc.vector.tensor_copy(ends[:, 0, :], ntile[:, :]))
                at_end, step = 0, 1
                while step < E1:
                    c.add(nc.vector.tensor_copy(ends[:, 1 - at_end, 0:step], ends[:, at_end, 0:step]))
                    tt(ends[:, 1 - at_end, step:E1], ends[:, at_end, step:E1], ends[:, at_end, 0:E1 - step], ALU.add)
                    at_end, step = 1 - at_end, 2 * step
                tt(start[:, :], ends[:, at_end, :], ntile[:, :], ALU.subtract)
                ts(start[:, :], start[:, :], float(ST), None, ALU.mult)
                tt(run[:, now, :, :], run[:, now, :, :], total[:, :, :], ALU.subtract)
                tt(run[:, now, :, :], run[:, now, :, :], p_rank[:, :, :], ALU.add)
                tt(run[:, now, :, :], run[:, now, :, :], start[:, :].unsqueeze(1).to_broadcast([P, NT, E1]), ALU.add)
                for q in range(2):
                    tt(same[:, :, :], onehot[:, q, :, :], run[:, now, :, :], ALU.mult)
                    c.step(nc.vector.tensor_reduce(out=slot[:, :], in_=same[:, :, :], op=ALU.add, axis=AX.X))
                    nc.vector.tensor_copy(k.slots[:, q, :], slot[:, :]).then_inc(slots_ready, 1)
                    dve.wait_ge(slots_ready, q + 1)
                tt(owner[:, :, :], tiles[:, :].unsqueeze(2).to_broadcast([P, NTILES, E1]),
                   ends[:, at_end, :].unsqueeze(1).to_broadcast([P, NTILES, E1]), ALU.is_ge)
                c.step(nc.vector.tensor_reduce(out=owner_f[:, :], in_=owner[:, :, :], op=ALU.add, axis=AX.X))
                ts(owner_f[:, :], owner_f[:, :], float(E1 - 1), None, ALU.min)
                c.step(nc.vector.tensor_copy(k.owners[:, :], owner_f[:, :]))

            @block.gpsimd
            def _(pool):
                for q in range(2):
                    pool.wait_ge(slots_ready, q + 1)
                    for t in range(NT):
                        pool.indirect_dma_start(out=k.x_slots[:, :],
                                                out_offset=bass.IndirectOffsetOnAxis(ap=k.slots[:, q, t:t + 1], axis=0),
                                                in_=xn_all[:, t, :], in_offset=None).then_inc(scattered, 16)
                pool.wait_ge(scattered, 16 * 2 * NT)


HI, LO = 0, 1
PRODUCTS = ((HI, HI), (HI, LO), (LO, HI))


def routed_experts(nc, a, k):
    with ExitStack() as stack:
        m = Mem(nc, stack)
        raw1 = m.sb("f_raw1", [P, 2, 2 * KT, FF])
        raw2 = m.sb("f_raw2", [P, 2, FB, D])
        w1 = m.sb("f_w1", [P, 2, 2 * KT, FF], F32R)
        w2 = m.sb("f_w2", [P, 2, FB, D], F32R)
        b1 = m.sb("f_b1", [P, 2, 2 * FB])
        b2 = m.sb("f_b2", [P, 2, D])
        x = m.sb("f_x", [P, SPT, D])
        xT = m.sb("f_xT", [P, 2, 2, KT, ST], F32R)
        gate = m.sb("f_gate", [P, 2, ST])
        hidden = m.sb("f_hidden", [P, 2, 2, ST], F32R)
        y = m.sb("f_y", [P, SPT, D])
        p_up = m.ps("p_up", [P, 2, 2, ST])
        p_t = m.ps("f_pt", [P, KT, ST])
        p_y = m.ps("p_y", [P, SPT, D])
        x_loaded = m.sem("f_x_loaded")
        w1_loaded, w2_loaded, b_loaded = ([m.sem(f"f_{what}_loaded{n}") for n in range(2)] for what in ("w1", "w2", "b"))
        turned, xT_high, xT_ready = m.sem("f_turned"), m.sem("f_xT_high"), m.sem("f_xT_ready")
        w_high, w_ready = m.sem("f_w_high"), m.sem("f_w_ready")
        up_psum, down_psum = m.sem("f_up_psum"), m.sem("f_down_psum")
        gate_ready, hidden_raw = m.sem("f_gate_ready"), m.sem("f_hidden_raw")
        hidden_high, hidden_ready = m.sem("f_hidden_high"), m.sem("f_hidden_ready")
        y_ready, y_stored = m.sem("f_y_ready"), m.sem("f_y_stored")
        pieces = [(1, 0), (2, 0), (1, 1), (1, 2), (2, 1), (1, 3)]
        PIECES, AHEAD = len(pieces), 3
        F1P, F2P = 2, FB // 2
        TURN_AT, AHEAD_AT = 3, FB - AHEAD

        def piece(q, one, two):
            which, n = pieces[q]
            if which == 1:
                return one[:, :, n * F1P * P:(n + 1) * F1P * P]
            return two[:, n * F2P:(n + 1) * F2P, :]

        def piece_raw(q, par):
            return piece(q, raw1[:, par, :, :], raw2[:, par, :, :])

        def piece_part(q, part):
            return piece(q, w1[:, part, :, :], w2[:, part, :, :])

        def all_tiles(engine, tile):
            tile(0, 0, 0)
            tile(1, 1, 0)
            with engine.Fori(1, NTILES // 2) as i:
                tile(2 * i, 0, i)
                tile(2 * i + 1, 1, i)
            for t in range(NTILES // 2 * 2, NTILES):
                tile(t, t % 2, t // 2)

        def early(t):
            return isinstance(t, int) and t < 2

        def last_tile(t):
            return isinstance(t, int) and t == NTILES - 1

        with nc.Block() as block:
            @block.sync
            def _(sp):
                def load(t, par):
                    if not first(t):
                        sp.wait_ge(turned, t)
                    sp.dma_start(x[:, :, :], k.x_slots[at(t, ST, ST), :].rearrange("(u p) d -> p u d", p=P)
                                 ).then_inc(x_loaded, 16)
                    if not early(t):
                        sp.wait_ge(w_ready, PIECES * (t - 1))
                    e = sp.value_load(k.owners[0:1, at(t, 1, 1)], min_val=0, max_val=E1 - 1)
                    for ab, src in enumerate((a["W1a"], a["W1b"])):
                        sp.dma_start(raw1[:, par, ab * KT:(ab + 1) * KT, :],
                                     src[bass.ds(e, 1), :, :].rearrange("o (k p) f -> p (o k) f", p=P)
                                     ).then_inc(w1_loaded[par], 16)
                    sp.dma_start(raw2[:, par, :, :], a["W2"][bass.ds(e, 1), :, :].rearrange("o (k p) d -> p (o k) d", p=P)
                                 ).then_inc(w2_loaded[par], 16)
                    if not early(t):
                        sp.wait_ge(y_ready, t - 1)
                    sp.dma_start(b1[:, par, :], a["b1"][bass.ds(e, 1), :, :].rearrange("o p f -> (o p) f")
                                 ).then_inc(b_loaded[par], 16)
                    sp.dma_start(b2[:, par, :], a["b2"][bass.ds(e, 1), :].rearrange("o d -> (o d)").partition_broadcast(P)
                                 ).then_inc(b_loaded[par], 16)

                def store(t):
                    sp.wait_ge(y_ready, t + 1)
                    sp.dma_start(k.y_slots[at(t, ST, ST), :].rearrange("(u p) d -> p u d", p=P), y[:, :, :]
                                 ).then_inc(y_stored, 16)

                load(0, 0)
                load(1, 1)
                load(2, 0)
                store(0)
                with sp.Fori(1, NTILES // 2) as i:
                    load(2 * i + 1, 1)
                    store(2 * i - 1)
                    load(2 * i + 2, 0)
                    store(2 * i)
                store(NTILES - 2)
                store(NTILES - 1)
                sp.wait_ge(y_stored, 16 * NTILES)

            @block.tensor
            def _(pe):
                def turn(t):
                    pe.wait_ge(x_loaded, 16 * t + 16)
                    if not first(t):
                        pe.wait_ge(xT_ready, t)
                    for kt in range(KT):
                        for u in range(SPT):
                            last = nc.tensor.transpose(p_t[:, kt, u * P:(u + 1) * P], x[:, u, kt * P:(kt + 1) * P],
                                                       k.ident[:, :])
                    last.then_inc(turned, 1)

                def up(t, par, f):
                    if f % F1P == 0:
                        pe.wait_ge(w_ready, PIECES * t + pieces.index((1, f // F1P)) + 1)
                    if f >= 2 or not first(t):
                        pe.wait_ge(hidden_raw, FB * t + f - 1)
                    for ab in range(2):
                        for kt in range(KT):
                            for wh, xh in PRODUCTS:
                                last = nc.tensor.matmul(
                                    p_up[:, f % 2, ab, :],
                                    w1[:, wh, ab * KT + kt, f * P:(f + 1) * P], xT[:, par, xh, kt, :],
                                    start=(kt, wh, xh) == (0, HI, HI), stop=(kt, wh, xh) == (KT - 1, LO, HI))
                    last.then_inc(up_psum, 1)

                def down(t, par, f):
                    if f % F2P == 0:
                        pe.wait_ge(w_ready, PIECES * t + pieces.index((2, f // F2P)) + 1)
                    pe.wait_ge(hidden_ready, FB * t + f + 1)
                    if f == 0 and not first(t):
                        pe.wait_ge(y_ready, t)
                    for u in range(SPT):
                        for wh, hh in PRODUCTS:
                            last = nc.tensor.matmul(p_y[:, u, :], hidden[:, f % 2, hh, u * P:(u + 1) * P],
                                                    w2[:, wh, f, :],
                                                    start=(f, wh, hh) == (0, HI, HI) and u % 2 == 0,
                                                    stop=(f, wh, hh) == (FB - 1, LO, HI) and u % 2 == 1)
                    last.then_inc(down_psum, 1)

                def tile(t, par, turns):
                    pe.wait_ge(xT_ready, t + 1)
                    for f in range(FB):
                        up(t, par, f)
                        if f == TURN_AT and not last_tile(t):
                            turn(t + 1)
                        if f:
                            down(t, par, f - 1)
                        elif not first(t):
                            down(t - 1, 1 - par, FB - 1)

                turn(0)
                all_tiles(pe, tile)
                down(NTILES - 1, (NTILES - 1) % 2, FB - 1)

            @block.scalar
            def _(act):
                def round_x(t, par):
                    act.wait_ge(turned, t + 1)
                    nc.scalar.activation(xT[:, par, HI, :, :], p_t[:, :, :], ACT.Copy).then_inc(xT_high, 1)

                def round_weights(t, par, q, turns):
                    which, n = pieces[q]
                    if which == 1:
                        if n == 0:
                            act.wait_ge(w1_loaded[par], 16 * 2 * (turns + 1))
                        if not first(t):
                            act.wait_ge(up_psum, FB * (t - 1) + (n + 1) * F1P)
                    else:
                        if n == 0:
                            act.wait_ge(w2_loaded[par], 16 * (turns + 1))
                        if not first(t):
                            act.wait_ge(down_psum, FB * (t - 1) + (n + 1) * F2P)
                    nc.scalar.activation(piece_part(q, HI), piece_raw(q, par), ACT.Copy).then_inc(w_high, 1)

                def tile(t, par, turns):
                    act.wait_ge(b_loaded[par], 16 * 2 * (turns + 1))
                    for f in range(FB):
                        n = FB * t + f + 1
                        act.wait_ge(up_psum, n)
                        if f >= 2 or not first(t):
                            act.wait_ge(hidden_ready, n - 2)
                        nc.scalar.activation(gate[:, f % 2, :], p_up[:, f % 2, 0, :], ACT.Silu,
                                             bias=b1[:, par, f:f + 1]).then_inc(gate_ready, 1)
                        act.wait_ge(hidden_raw, n)
                        if f >= 2 or not first(t):
                            act.wait_ge(down_psum, n - 2)
                        nc.scalar.activation(hidden[:, f % 2, HI, :], gate[:, f % 2, :], ACT.Copy).then_inc(hidden_high, 1)
                        if f == TURN_AT and not last_tile(t):
                            round_x(t + 1, 1 - par)
                        if f < PIECES - AHEAD:
                            round_weights(t, par, AHEAD + f, turns)
                        if f >= AHEAD_AT and not last_tile(t):
                            round_weights(t + 1, 1 - par, f - AHEAD_AT, turns + (1 if par else 0))

                round_x(0, 0)
                for q in range(AHEAD):
                    round_weights(0, 0, q, 0)
                all_tiles(act, tile)

            @block.vector
            def _(dve):
                def rest_of_x(t, par):
                    dve.wait_ge(xT_high, t + 1)
                    nc.vector.tensor_tensor(xT[:, par, LO, :, :], p_t[:, :, :], xT[:, par, HI, :, :],
                                            ALU.subtract).then_inc(xT_ready, 1)

                def hide(t, par, f):
                    n = FB * t + f + 1
                    dve.wait_ge(gate_ready, n)
                    nc.vector.scalar_tensor_tensor(out=gate[:, f % 2, :], in0=p_up[:, f % 2, 1, :],
                                                   scalar=b1[:, par, FB + f:FB + f + 1], in1=gate[:, f % 2, :],
                                                   op0=ALU.add, op1=ALU.mult).then_inc(hidden_raw, 1)
                    dve.wait_ge(hidden_high, n)
                    nc.vector.tensor_tensor(hidden[:, f % 2, LO, :], gate[:, f % 2, :], hidden[:, f % 2, HI, :],
                                            ALU.subtract).then_inc(hidden_ready, 1)

                def take_y(t, par):
                    dve.wait_ge(down_psum, FB * t + FB)
                    if not first(t):
                        dve.wait_ge(y_stored, 16 * t)
                    nc.vector.tensor_tensor(y[:, :, :], p_y[:, :, :],
                                            b2[:, par, :].unsqueeze(1).to_broadcast([P, SPT, D]), ALU.add).then_inc(y_ready, 1)

                def tile(t, par, turns):
                    for f in range(FB):
                        hide(t, par, f)
                        if f == 0 and not first(t):
                            take_y(t - 1, 1 - par)
                        if f == TURN_AT and not last_tile(t):
                            rest_of_x(t + 1, 1 - par)

                rest_of_x(0, 0)
                all_tiles(dve, tile)
                take_y(NTILES - 1, (NTILES - 1) % 2)

            @block.gpsimd
            def _(pool):
                def tile(t, par, turns):
                    for q in range(PIECES):
                        pool.wait_ge(w_high, PIECES * t + q + 1)
                        nc.gpsimd.tensor_tensor(piece_part(q, LO), piece_raw(q, par), piece_part(q, HI),
                                                ALU.subtract).then_inc(w_ready, 1)

                all_tiles(pool, tile)


def combine(nc, a, k, out):
    with ExitStack() as stack:
        m = Mem(nc, stack)
        ys = m.sb("g_ys", [P, 2, 2, TPC, D])
        res = m.sb("g_res", [P, 2, TPC, D])
        gathered = [m.sem(f"g_gathered{n}") for n in range(2)]
        stored = [m.sem(f"g_stored{n}") for n in range(2)]
        done, own = m.sem("g_done"), m.sem("g_own")
        OWN = 2 * TPC + 1
        with nc.Block() as block:
            @block.gpsimd
            def _(pool):
                for i in range(NCH):
                    if i >= 2:
                        pool.wait_ge(done, i - 1)
                    for u in range(TPC):
                        for q in range(2):
                            t = i * TPC + u
                            pool.indirect_dma_start(out=ys[:, i % 2, q, u, :], out_offset=None, in_=k.y_slots[:, :],
                                                    in_offset=bass.IndirectOffsetOnAxis(ap=k.slots[:, q, t:t + 1], axis=0),
                                                    ).then_inc(gathered[i % 2], 16)

            @block.vector
            def _(dve):
                def chunk(i, par, turns, early):
                    c = Count(dve, own, OWN * i)
                    dve.wait_ge(gathered[par], 16 * 2 * TPC * (turns + 1))
                    if not early:
                        dve.wait_ge(stored[par], 16 * turns)
                    for u in range(TPC):
                        c.add(nc.vector.tensor_scalar(res[:, par, u, :], ys[:, par, 0, u, :],
                                                      k.weights[:, 0, at(i * TPC + u, 1, 1)], None, ALU.mult))
                    c.wait()
                    for u in range(TPC):
                        c.add(nc.vector.scalar_tensor_tensor(out=res[:, par, u, :], in0=ys[:, par, 1, u, :],
                                                             scalar=k.weights[:, 1, at(i * TPC + u, 1, 1)],
                                                             in1=res[:, par, u, :], op0=ALU.mult, op1=ALU.add))
                    c.wait()
                    c.step(nc.vector.tensor_tensor(res[:, par, :, :], res[:, par, :, :], k.mod(1, i // CPS, GB), ALU.mult))
                    nc.vector.tensor_tensor(res[:, par, :, :], res[:, par, :, :], k.x[:, at(i, TPC, TPC), :],
                                            ALU.add).then_inc(done, 1)
                    assert c.n == OWN

                chunk(0, 0, 0, True)
                chunk(1, 1, 0, True)
                with dve.Fori(1, NCH // 2) as i:
                    chunk(2 * i, 0, i, False)
                    chunk(2 * i + 1, 1, i, False)

            @block.sync
            def _(sp):
                with sp.Fori(0, NCH // 2) as i:
                    for par in range(2):
                        sp.wait_ge(done, 2 * i + par + 1)
                        sp.dma_start(out[at(2 * i + par, CH, CH), :].rearrange("(u p) d -> p u d", p=P),
                                     res[:, par, :, :]).then_inc(stored[par], 16)
                for par in range(2):
                    sp.wait_ge(stored[par], 16 * (NCH // 2))


class Kept:

    def __init__(self, nc, m):
        self.ident = m.sb("ident", [P, P])
        self.identb = m.sb("identb", [P, P], BF16)
        self.masks = m.sb("masks", [P, 2, P], BF16)
        self.mods = [None, m.sb("mods1", [P, B, 6, D])]
        self.stats = m.sb("stats", [P, NT, 6])
        self.mean, self.ve, self.rstd = m.sb("mean", [P, NT]), m.sb("ve", [P, NT]), m.sb("rstd", [P, NT])
        self.spread, self.neghalf = m.sb("spread", [P, NT]), m.sb("neghalf", [P, NT])
        self.x = m.sb("x", [P, NT, D])
        self.constants_loaded = m.sem("constants_loaded")
        self.scaled, self.x2_ready = m.sem("c_scaled"), m.sem("c_x2_ready")

        self.weights = m.sb("weights", [P, 2, NT])
        self.slots = m.sb("slots", [P, 2, NT], U32)
        self.owners = m.sb("owners", [P, NTILES], I32)

        def dram(name, shape, dt=F32):
            return nc.dram_tensor(name, shape, dt, kind="Internal").ap()

        self.qk_rows = dram("qk_scr", [2 * SPLIT * B * D, T], BF16)
        self.v_scr = dram("v_scr", [NS, P, JT, HG * VW])
        self.x_slots, self.y_slots = dram("x_slots", [NSLOT, D]), dram("y_slots", [NSLOT, D])
        self.max_scr = dram("max_scr", [2, SPLIT * HG, CH], BF16)
        self.qk_scr = {(qk, part): self.qk_rows[(qk * SPLIT + part) * B * D:(qk * SPLIT + part + 1) * B * D, :]
                       for qk in range(2) for part in range(SPLIT)}

    def mod(self, layer, b, which):
        return self.mods[layer][:, at(b, 1, 1), which, :].to_broadcast([P, TPC, D])

    def mod1(self, layer, b, which):
        return self.mods[layer][:, at(b, 1, 1), which, :].rearrange("p o d -> p (o d)")


def program(nc, a, out):
    with ExitStack() as stack:
        m = Mem(nc, stack)
        k = Kept(nc, m)
        with ExitStack() as block0:
            k.mods[0] = Mem(nc, block0).sb("mods0", [P, B, 6, D])
            modulation(nc, a, k)
            projections(nc, a, k)
            attention(nc, a, k)
            output_projection(nc, a, k)
            top1_experts(nc, a, k)
        with ExitStack() as mixing:
            mm = Mem(nc, mixing)
            h_all = mm.sb("h_all", [P, NT, D])
            xnT_all = mm.sb("xnT_all", [P, KT, NTOK])
            second_norm(nc, a, k, "n1_", SA, CA, h_all, None, xnT_all, None, None)
            mix(nc, a, k, h_all, xnT_all)
        with ExitStack() as routing:
            mm = Mem(nc, routing)
            xn_all = mm.sb("xn_all", [P, NT, D])
            logits = mm.sb("logits", [P, NT, E1])
            second_norm(nc, a, k, "n2_", SB_, CB, None, xn_all, None, a["ln_w"], logits)
            route(nc, a, k, logits, xn_all)
        routed_experts(nc, a, k)
        combine(nc, a, k, out)


def lay_out(inputs):
    g = {n: np.asarray(v) for n, v in inputs.items()}
    swap = np.arange(D) ^ 1
    a = {"x": g["L0_attn_X"].reshape(NTOK, D)}
    for n in range(2):
        a[f"cT{n}"] = g[f"L{n}_c"].T.reshape(KT, P, B).transpose(1, 0, 2)
        a[f"wmod{n}"] = g[f"L{n}_wmod"]
    wq, wk, wv = (g[f"L0_attn_W_{c}"] for c in "qkv")
    a["wqkv"] = np.concatenate([wq.T, wq[swap].T, wk.T, wk[swap].T, wv.T], axis=1)
    a["woT"] = g["L0_attn_W_o"].T
    a["expertT"] = g["L0_ffn_expert_w"].transpose(2, 0, 1).reshape(D, E0 * D)
    a["gateT"] = g["L0_ffn_gate_w"].T
    a["iota8"] = np.tile(np.arange(E0, dtype=np.float32) - E0, (P, 1))
    a["w_uv"] = np.concatenate([g["L1_attn_u_w"].T, g["L1_attn_v_w"].T], axis=1)
    a["b_uv"] = np.concatenate([g["L1_attn_u_b"], g["L1_attn_v_b"]]).reshape(2 * FB1, P).T
    a["o_wT"] = g["L1_attn_o_w"].T
    a["o_b"] = g["L1_attn_o_b"]
    heads = np.stack([g["L1_attn_zero"][:, 0], g["L1_attn_pos"][:, 0], g["L1_attn_neg"][:, 0]])
    a["toep"] = np.repeat(heads, F1 // heads.shape[1], axis=1).reshape(3, FB1, P).transpose(2, 0, 1)
    a["ln_w"], a["Wg"], a["bg"] = g["L1_ffn_ln_w"], g["L1_ffn_Wg"], g["L1_ffn_bg"]
    a["W1a"], a["W1b"], a["W2"], a["b2"] = g["L1_ffn_W1a"], g["L1_ffn_W1b"], g["L1_ffn_W2"], g["L1_ffn_b2"]
    b1 = np.concatenate([g["L1_ffn_b1a"], g["L1_ffn_b1b"]], axis=1)
    a["b1"] = b1.reshape(E1, 2 * FB, P).transpose(0, 2, 1)
    a["before"] = np.triu(np.ones((P, P), np.float32), 1)
    a["ones"] = np.ones((P, P), np.float32)
    a["iota_tiles"] = np.tile(np.arange(NTILES, dtype=np.float32), (P, 1))
    theta = np.power(np.float32(10000.0), np.float32(-2.0) * np.arange(DH // 2, dtype=np.float32) / np.float32(DH))
    angle = (np.arange(T, dtype=np.float32)[:, None] * theta[None, :]).T.repeat(2, axis=0)
    sign = np.where(np.arange(DH) % 2 == 0, -1, 1).astype(np.float32)[:, None]
    a["trig"] = np.stack([np.tile(np.cos(angle), (P // DH, 1)), np.tile(sign * np.sin(angle), (P // DH, 1))], axis=1)
    a["ident"] = np.eye(P, dtype=np.float32)
    later = np.triu(np.full((P, P), MASKED, np.float32), 1)
    a["masks"] = np.stack([later, later.T], axis=1)
    return {n: np.ascontiguousarray(v) for n, v in a.items()}


def kernel(**inputs):
    import concourse.bacc as bacc
    from concourse.bass_utils import run_bass_kernel_spmd

    nc = bacc.Bacc("TRN2", target_bir_lowering=False, num_devices=1)
    arrays = lay_out(inputs)
    a = {n: nc.dram_tensor(f"in_{n}", v.shape, mybir.dt.from_np(v.dtype), kind="ExternalInput").ap()
         for n, v in arrays.items()}
    out = nc.dram_tensor("out", [NTOK, D], F32, kind="ExternalOutput").ap()
    program(nc, a, out)
    r = run_bass_kernel_spmd(nc, [{f"in_{n}": v for n, v in arrays.items()}], core_ids=[0])
    return r.results[0]["out"].reshape(B, T, D)
```

```python
from contextlib import ExitStack

import numpy as np
import concourse.bass as bass
from concourse import mybir

F32 = mybir.dt.float32
BF16 = mybir.dt.bfloat16
I32 = mybir.dt.int32
U32 = mybir.dt.uint32
F32R = mybir.dt.float32r
ACT = mybir.ActivationFunctionType
ALU = mybir.AluOpType
AX = mybir.AxisListType

B, T, D = 2, 2048, 256
NTOK = B * T
P = 128
KT = D // P
CH = 512
TPC = CH // P
NCH = NTOK // CH
CPS = T // CH
NT = NTOK // P
H0, DH = 16, 16
HG = 4
NS = B * H0 // HG
JT = T // P
VW = 32
SPLIT = 3
Q_PARTS = (0, 0, 1, 1, 0, 2)
K_PARTS = (0, 1, 0, 1, 2, 0)
QROWS = DH * len(Q_PARTS)
EPS = 1e-5
MASKED = -1e30
E0 = 8
F1 = 512
FB1 = F1 // P
E1, FF = 8, 1024
FB = FF // P
ST = 512
SPT = ST // P
NTILES = E1 + (2 * NTOK - E1) // ST
NSLOT = NTILES * ST
ZW = SPT * D

HI, LO = 0, 1
PRODUCTS = ((HI, HI), (HI, LO), (LO, HI))


class Count:

    def __init__(self, engine, sem, start=0):
        self.engine, self.sem, self.start, self.n = engine, sem, start, 0

    def add(self, instruction):
        instruction.then_inc(self.sem, 1)
        self.n += 1

    def wait(self):
        self.engine.wait_ge(self.sem, self.start + self.n)

    def step(self, instruction):
        self.add(instruction)
        self.wait()


def first(i):
    return isinstance(i, int) and i == 0


def at(i, step, n):
    return slice(i * step, i * step + n) if isinstance(i, int) else bass.ds(i * step, n)


class Mem:
    def __init__(self, nc, stack):
        self.nc, self.stack = nc, stack

    def sb(self, name, shape, dt=F32):
        return self.stack.enter_context(self.nc.sbuf_tensor(name, shape, dt))

    def ps(self, name, shape, dt=F32):
        return self.stack.enter_context(self.nc.psum_tensor(name, shape, dt))

    def sem(self, name):
        return self.nc.alloc_semaphore(name)


SA, CA, GA, SB_, CB, GB = range(6)


def modulation(nc, a, k):
    with ExitStack() as stack:
        m = Mem(nc, stack)
        wm = m.sb("wm", [P, 2, KT, 6 * D])
        cT = m.sb("cT", [P, 2, KT, B])
        silu_c = m.sb("silu_c", [P, 2, KT, B])
        ones = m.sb("mod_ones", [P, P])
        cb = m.sb("cb", [P, 2, KT, B, P])
        sign = m.sb("gate_sign", [P, B, D])
        mag = m.sb("gate_mag", [P, B, D])
        masks = m.sb("masks_f32", [P, 2, P])
        pm = m.ps("pmod", [P, 2, 2 * D])
        loaded = k.constants_loaded
        c_ready, cb_ready, ones_set = m.sem("silu_c_ready"), m.sem("cb_ready"), m.sem("mod_ones_set")
        product, copied, own = m.sem("mod_product"), m.sem("mod_copied"), m.sem("mod_own")
        x_loaded, stats_done = [m.sem(f"x_loaded{b}") for b in range(B)], m.sem("stats_done")
        LOADS = 6
        with nc.Block() as block:
            @block.gpsimd
            def _(pool):
                for b in range(B):
                    pool.dma_start(k.x[:, b * JT:(b + 1) * JT, :],
                                   a["x"][b * T:(b + 1) * T, :].rearrange("(t p) d -> p t d", p=P)).then_inc(x_loaded[b], 16)

            @block.sync
            def _(sp):
                sp.dma_start(cT[:, 0, :, :], a["cT0"]).then_inc(loaded, 16)
                sp.dma_start(cT[:, 1, :, :], a["cT1"]).then_inc(loaded, 16)
                for layer, name in enumerate(("wmod0", "wmod1")):
                    sp.dma_start(wm[:, layer, :, :], a[name].rearrange("(k p) n -> p k n", p=P)).then_inc(loaded, 16)
                sp.dma_start(k.ident[:, :], a["ident"]).then_inc(loaded, 16)
                sp.dma_start(masks[:, :, :], a["masks"]).then_inc(loaded, 16)
                sp.wait_ge(loaded, 16 * LOADS)

            @block.scalar
            def _(act):
                act.wait_ge(loaded, 16 * LOADS)
                nc.scalar.activation(silu_c[:, :, :, :], cT[:, :, :, :], ACT.Silu).then_inc(c_ready, 1)
                n = 0
                for layer in range(2):
                    for b in range(B):
                        for half in range(3):
                            act.wait_ge(product, n + 1)
                            nc.scalar.activation(
                                k.mods[layer][:, b, 2 * half:2 * half + 2, :],
                                pm[:, n % 2, :].rearrange("p (s d) -> p s d", s=2), ACT.Copy).then_inc(copied, 1)
                            n += 1

            @block.tensor
            def _(pe):
                pe.wait_ge(cb_ready, 2 * KT * B)
                n = 0
                for layer in range(2):
                    for b in range(B):
                        for half in range(3):
                            if n >= 2:
                                pe.wait_ge(copied, n - 1)
                            for kt in range(KT):
                                last = nc.tensor.matmul(
                                    pm[:, n % 2, :], cb[:, layer, kt, b, :],
                                    wm[:, layer, kt, 2 * half * D:(2 * half + 2) * D],
                                    start=kt == 0, stop=kt == KT - 1)
                            last.then_inc(product, 1)
                            n += 1

            @block.vector
            def _(dve):
                nc.vector.memset(ones[:, :], 1.0).then_inc(ones_set, 1)
                dve.wait_ge(ones_set, 1)
                dve.wait_ge(c_ready, 1)
                for layer in range(2):
                    for kt in range(KT):
                        for b in range(B):
                            nc.vector.tensor_scalar(cb[:, layer, kt, b, :], ones[:, :],
                                                    silu_c[:, layer, kt, b:b + 1], None, ALU.mult).then_inc(cb_ready, 1)
                for b in range(B):
                    dve.wait_ge(x_loaded[b], 16)
                    with dve.Fori(b * JT, (b + 1) * JT) as t:
                        nc.vector.bn_stats(out=k.stats[:, at(t, 1, 1), :].rearrange("p o s -> p (o s)"),
                                           in_=k.x[:, at(t, 1, 1), :].rearrange("p o d -> p (o d)")).then_inc(stats_done, 1)
                dve.wait_ge(loaded, 16 * LOADS)
                own_n = Count(dve, own)
                own_n.add(nc.vector.tensor_copy(k.identb[:, :], k.ident[:, :]))
                own_n.add(nc.vector.tensor_copy(k.masks[:, :, :], masks[:, :, :]))
                dve.wait_ge(copied, 6 * B)
                for mods in k.mods:
                    for which in (CA, CB):
                        own_n.add(nc.vector.tensor_scalar(mods[:, :, which, :], mods[:, :, which, :], 1.0, None, ALU.add))
                    for which in (GA, GB):
                        gate = mods[:, :, which, :]
                        own_n.wait()
                        own_n.add(nc.vector.tensor_scalar(sign[:, :, :], gate, 0.0, 2.0, ALU.is_ge, ALU.mult))
                        own_n.step(nc.vector.scalar_tensor_tensor(out=mag[:, :, :], in0=gate, scalar=-1.0, in1=gate,
                                                                  op0=ALU.mult, op1=ALU.max))
                        own_n.step(nc.vector.tensor_scalar(mag[:, :, :], mag[:, :, :], 0.25, None, ALU.max))
                        own_n.step(nc.vector.scalar_tensor_tensor(out=gate, in0=sign[:, :, :], scalar=-1.0,
                                                                  in1=mag[:, :, :], op0=ALU.add, op1=ALU.mult))


NORM_STEPS = TPC + 1
AGGREGATE_STEPS = 6


def aggregate(nc, own, k):
    (mean_e, m2_e), (mean_o, m2_o) = ((k.stats[:, :, i], k.stats[:, :, i + 1]) for i in (1, 4))
    own.add(nc.vector.tensor_tensor(k.mean[:, :], mean_e, mean_o, ALU.add))
    own.add(nc.vector.tensor_tensor(k.spread[:, :], mean_e, mean_o, ALU.subtract))
    own.step(nc.vector.tensor_tensor(k.ve[:, :], m2_e, m2_o, ALU.add))
    own.add(nc.vector.tensor_scalar(k.mean[:, :], k.mean[:, :], 0.5, None, ALU.mult))
    own.add(nc.vector.tensor_scalar(k.ve[:, :], k.ve[:, :], 1.0 / D, EPS, ALU.mult, ALU.add))
    own.step(nc.vector.scalar_tensor_tensor(out=k.spread[:, :], in0=k.spread[:, :], scalar=0.25, in1=k.spread[:, :],
                                            op0=ALU.mult, op1=ALU.mult))
    assert own.n == AGGREGATE_STEPS
    return nc.vector.tensor_tensor(k.ve[:, :], k.ve[:, :], k.spread[:, :], ALU.add)


def row_stats(nc, k, i, done):
    for u in range(TPC):
        t = at(i * TPC + u, 1, 1)
        nc.vector.bn_stats(out=k.stats[:, t, :].rearrange("p o s -> p (o s)"),
                           in_=k.x[:, t, :].rearrange("p o d -> p (o d)")).then_inc(done, 1)


def root(nc, pool, k, norm):
    if norm == 0:
        nc.gpsimd.memset(k.neghalf[:, :], -0.5).then_inc(k.power_set, 1)
        pool.wait_ge(k.power_set, 1)
    pool.wait_ge(k.ve_ready, norm + 1)
    nc.gpsimd.tensor_tensor(k.rstd[:, :], k.ve[:, :], k.neghalf[:, :], ALU.pow).then_inc(k.rstd_ready, 1)


def normalize(nc, k, own, i, h, scale, shift, done):
    for u in range(TPC):
        own.add(nc.vector.tensor_scalar(h[:, u, :], k.x[:, at(i * TPC + u, 1, 1), :].rearrange("p o d -> p (o d)"),
                                        k.mean[:, at(i * TPC + u, 1, 1)], k.rstd[:, at(i * TPC + u, 1, 1)],
                                        ALU.subtract, ALU.mult))
    own.wait()
    own.step(nc.vector.tensor_tensor(h, h, scale, ALU.mult))
    nc.vector.tensor_tensor(h, h, shift, ALU.add).then_inc(done, 1)


def projections(nc, a, k):
    with ExitStack() as stack:
        m = Mem(nc, stack)
        w = m.sb("wqkv", [P, KT, 5 * D])
        trig = m.sb("trig", [P, 2, T])
        h = m.sb("h", [P, TPC, D])
        hT = m.sb("hT", [P, KT, CH])
        rot = m.sb("rot", [P, 2, 2, KT, CH])
        rem = m.sb("rem", [P, 2, KT, CH])
        parts = m.sb("parts", [P, 2, SPLIT, KT, CH], BF16)
        va = m.sb("va", [P, TPC, H0, VW])
        p_t = m.ps("p_t", [P, KT, CH])
        p_qk = m.ps("p_qk", [P, 2, KT, CH])
        p_v = m.ps("p_v", [P, TPC, D])
        w_loaded = m.sem("w_loaded")
        h_ready, hT_psum, hT_ready = m.sem("a_h_ready"), m.sem("a_hT_psum"), m.sem("a_hT_ready")
        qk_psum, v_psum = m.sem("a_qk_psum"), m.sem("a_v_psum")
        qk_taken, rot_ready = m.sem("a_qk_taken"), m.sem("a_rot_ready")
        part_act, part_dve = m.sem("a_part_act"), m.sem("a_part_dve")
        va_ready, parts_stored, va_stored = m.sem("a_va_ready"), m.sem("a_parts_stored"), m.sem("a_va_stored")
        own, ones_set = m.sem("a_own"), m.sem("a_ones_set")
        NHG = H0 // HG
        with nc.Block() as block:
            @block.sync
            def _(sp):
                def store(i):
                    b = i // CPS
                    c = i % CPS
                    for qk in range(2):
                        sp.wait_ge(part_dve, 4 * i + 2 * qk + 2)
                        for part in range(SPLIT):
                            sp.dma_start(
                                k.qk_scr[qk, part][at(b, D, D), at(c, CH, CH)].rearrange("(k p) t -> p k t", p=P),
                                parts[:, qk, part, :, :]).then_inc(parts_stored, 16)
                    sp.wait_ge(va_ready, i + 1)
                    for hg in range(NHG):
                        sp.dma_start(
                            k.v_scr[at(b * NHG + hg, 1, 1), :, at(c, TPC, TPC), :].rearrange("s p u n -> (s p) u n"),
                            va[:, :, HG * hg:HG * hg + HG, :].rearrange("p u h n -> p u (h n)")).then_inc(va_stored, 16)

                sp.dma_start(w[:, :, :], a["wqkv"].rearrange("(k p) n -> p k n", p=P)).then_inc(w_loaded, 16)
                sp.dma_start(trig[:, :, :], a["trig"]).then_inc(w_loaded, 16)
                with sp.Fori(0, NCH) as i:
                    store(i)
                sp.wait_ge(parts_stored, 16 * 2 * SPLIT * NCH)
                sp.wait_ge(va_stored, 16 * NHG * NCH)

            @block.gpsimd
            def _(pool):
                root(nc, pool, k, 0)

                def add(i, qk):
                    pool.wait_ge(qk_taken, 4 * i + 2 * qk + 2)
                    nc.gpsimd.tensor_tensor(rem[:, qk, :, :], rot[:, qk, 0, :, :], rot[:, qk, 1, :, :],
                                            ALU.add).then_inc(rot_ready, 1)

                with pool.Fori(0, NCH) as i:
                    add(i, 0)
                    add(i, 1)

            @block.vector
            def _(dve):
                nc.vector.memset(va[:, :, :, :], 1.0).then_inc(ones_set, 1)

                def norm(i):
                    c = Count(dve, own, AGGREGATE_STEPS + NORM_STEPS * i)
                    normalize(nc, k, c, i, h[:, :, :], k.mod(0, i // CPS, CA), k.mod(0, i // CPS, SA), h_ready)
                    assert c.n == NORM_STEPS

                def rotate(i, qk):
                    dve.wait_ge(qk_psum, 2 * i + qk + 1)
                    for s in range(2):
                        table = trig[:, s, at(i % CPS, CH, CH)]
                        nc.vector.tensor_tensor(rot[:, qk, s, :, :], p_qk[:, s, :, :],
                                                table.unsqueeze(1).to_broadcast([P, KT, CH]),
                                                ALU.mult).then_inc(qk_taken, 1)

                def split(i, qk):
                    dve.wait_ge(part_act, 4 * i + 2 * qk + 1)
                    nc.vector.tensor_tensor(rem[:, qk, :, :], rem[:, qk, :, :], parts[:, qk, 0, :, :],
                                            ALU.subtract).then_inc(part_dve, 1)
                    dve.wait_ge(part_act, 4 * i + 2 * qk + 2)
                    nc.vector.tensor_tensor(parts[:, qk, 2, :, :], rem[:, qk, :, :], parts[:, qk, 1, :, :],
                                            ALU.subtract).then_inc(part_dve, 1)

                aggregate(nc, Count(dve, own), k).then_inc(k.ve_ready, 1)
                dve.wait_ge(k.rstd_ready, 1)
                norm(0)
                dve.wait_ge(w_loaded, 32)
                with dve.Fori(0, NCH - 1) as i:
                    rotate(i, 0)
                    norm(i + 1)
                    split(i, 0)
                    rotate(i, 1)
                    split(i, 1)
                rotate(NCH - 1, 0)
                split(NCH - 1, 0)
                rotate(NCH - 1, 1)
                split(NCH - 1, 1)

            @block.scalar
            def _(act):
                def take_hT(i):
                    act.wait_ge(hT_psum, i + 1)
                    if not first(i):
                        act.wait_ge(qk_psum, 2 * i)
                    nc.scalar.activation(hT[:, :, :], p_t[:, :, :], ACT.Copy).then_inc(hT_ready, 1)

                def take_v(i):
                    act.wait_ge(v_psum, i + 1)
                    if first(i):
                        act.wait_ge(ones_set, 1)
                    else:
                        act.wait_ge(va_stored, 16 * NHG * i)
                    nc.scalar.activation(va[:, :, :, 0:DH], p_v[:, :, :].rearrange("p u (h d) -> p u h d", d=DH),
                                         ACT.Copy).then_inc(va_ready, 1)

                def split(i, qk):
                    act.wait_ge(rot_ready, 2 * i + qk + 1)
                    if not first(i):
                        act.wait_ge(parts_stored, 16 * 2 * SPLIT * i)
                    nc.scalar.activation(parts[:, qk, 0, :, :], rem[:, qk, :, :], ACT.Copy).then_inc(part_act, 1)
                    act.wait_ge(part_dve, 4 * i + 2 * qk + 1)
                    nc.scalar.activation(parts[:, qk, 1, :, :], rem[:, qk, :, :], ACT.Copy).then_inc(part_act, 1)

                take_hT(0)
                take_v(0)
                split(0, 0)
                take_hT(1)
                split(0, 1)
                with act.Fori(1, NCH - 1) as i:
                    take_v(i)
                    split(i, 0)
                    take_hT(i + 1)
                    split(i, 1)
                take_v(NCH - 1)
                split(NCH - 1, 0)
                split(NCH - 1, 1)

            @block.tensor
            def _(pe):
                def product(i, qk):
                    for s in range(2):
                        for mb in range(KT):
                            for kt in range(KT):
                                col = (2 * qk + s) * D + mb * P
                                last = nc.tensor.matmul(p_qk[:, s, mb, :], w[:, kt, col:col + P], hT[:, kt, :],
                                                        start=kt == 0, stop=kt == KT - 1)
                    last.then_inc(qk_psum, 1)

                def chunk(i):
                    pe.wait_ge(h_ready, i + 1)
                    if not first(i):
                        pe.wait_ge(hT_ready, i)
                    for kt in range(KT):
                        for u in range(TPC):
                            last = nc.tensor.transpose(p_t[:, kt, u * P:(u + 1) * P], h[:, u, kt * P:(kt + 1) * P],
                                                       k.ident[:, :])
                    last.then_inc(hT_psum, 1)
                    if first(i):
                        pe.wait_ge(w_loaded, 32)
                    pe.wait_ge(hT_ready, i + 1)
                    if not first(i):
                        pe.wait_ge(qk_taken, 4 * i)
                    product(i, 0)
                    if not first(i):
                        pe.wait_ge(va_ready, i)
                    for u in range(TPC):
                        for kt in range(KT):
                            last = nc.tensor.matmul(p_v[:, u, :], hT[:, kt, u * P:(u + 1) * P], w[:, kt, 4 * D:5 * D],
                                                    start=kt == 0, stop=kt == KT - 1)
                    last.then_inc(v_psum, 1)
                    pe.wait_ge(qk_taken, 4 * i + 2)
                    product(i, 1)

                chunk(0)
                with pe.Fori(1, NCH) as i:
                    chunk(i)


UNITS = sum(TPC * (c + 1) for c in range(CPS))
NBUF = 3


def attention(nc, a, k):
    with ExitStack() as stack:
        m = Mem(nc, stack)
        qa = m.sb("qa", [P, NBUF, HG, T], BF16)
        ka = m.sb("ka", [P, NBUF, HG, T], BF16)
        va = m.sb("va3", [P, NBUF, JT, HG * VW])
        probs = m.sb("probs", [P, 2, HG, CH])
        tile_max = m.sb("tile_max", [P, HG, TPC, CPS])
        row_max = m.sb("row_max", [P, HG, TPC])
        max_rest = m.sb("max_rest", [P, HG, TPC])
        max_parts = m.sb("max_parts", [P, TPC, SPLIT, HG], BF16)
        max_rows = m.sb("max_rows", [SPLIT * HG, 2, CH], BF16)
        o_sb = m.sb("o_sb", [P, 2, CH])
        recip = m.sb("recip", [P, TPC, HG])
        p_s = m.ps("p_s", [P, 2, CH])
        p_m = m.ps("p_m", [P, 2, 2, CH])
        p_o = m.ps("p_o", [P, CH])
        p_misc = m.ps("p_misc", [P, CH])
        stage_loaded, stage0_loaded = [m.sem(f"stage_loaded{n}") for n in range(NBUF)], m.sem("stage0_loaded")
        scores_ready, probs_ready, probs_used = m.sem("scores_ready"), m.sem("probs_ready"), m.sem("probs_used")
        max_scores, max_taken = m.sem("max_scores"), m.sem("max_taken")
        max_parts_ready, max_turned, max_rows_ready = m.sem("max_parts_ready"), m.sem("max_turned"), m.sem("max_rows_ready")
        max_stored, max_placed = m.sem("max_stored"), m.sem("max_placed")
        o_taken, o_turned, att_ready = m.sem("o_taken"), m.sem("o_turned"), m.sem("att_ready")
        ones_set, own, recip_ready = m.sem("ones_set"), m.sem("b_own"), m.sem("recip_ready")
        zeros, zeros_set, slots_zeroed = m.sb("zeros", [P, ZW]), m.sem("zeros_set"), m.sem("slots_zeroed")
        LOADS = 2 * len(Q_PARTS) + 1
        NMAX = 2 * UNITS
        MAX_OWN = 4


        units = [(c, j) for c in range(CPS) for j in range(TPC * (c + 1))]
        max_units = [(c, i, bank, hp) for c in range(CPS) for i in range(TPC) for bank in range(c + 1)
                     for hp in range(HG // 2)]
        assert len(max_units) == NMAX == 2 * len(units)
        MAX_LEAD = 22
        TURN_MAXIMA = {5: (2, False), 19: (3, False), 23: (0, True), 31: (1, True)}
        AFTER_O, AFTER_TURN_O = 0, 3
        assert UNITS - MAX_LEAD == 18 and AFTER_TURN_O == TPC - 1
        assert (NS - 2) % NBUF == 0

        def ends_chunk(u):
            c, i, bank, hp = max_units[u]
            return (i, bank, hp) == (TPC - 1, c, HG // 2 - 1)

        def all_stages(engine, stage):
            stage(0, 0, True, 1)
            with engine.Fori(0, (NS - 2) // NBUF) as turn:
                for n in range(1, NBUF + 1):
                    stage(NBUF * turn + n, n % NBUF, True, turn + (n + 1) // NBUF + ((n + 1) % NBUF > 0))
            stage(NS - 1, (NS - 1) % NBUF, False, 0)

        def max_unit(s, n, more):
            if n + MAX_LEAD < UNITS:
                return s, n + MAX_LEAD
            return (s + 1, n + MAX_LEAD - UNITS) if more else None

        def maxima_turned_at(s, n, more):
            c, following = TURN_MAXIMA.get(n, (None, False))
            if c is None or following and not more:
                return None
            return (s + 1 if following else s), c

        def load_stage(engine, s):
            buf = s % NBUF
            loaded = stage_loaded[buf] if s else stage0_loaded
            for g, (qp, kp) in enumerate(zip(Q_PARTS, K_PARTS)):
                for dst, qk, part in ((qa, 0, qp), (ka, 1, kp)):
                    src = k.qk_scr[qk, part][at(s, HG * DH, HG * DH), :].rearrange("(h d) t -> d h t", h=HG)
                    engine.dma_start(dst[DH * g:DH * (g + 1), buf, :, :], src).then_inc(loaded, 16)
            engine.dma_start(va[:, buf, :, :], k.v_scr[s, :, :, :]).then_inc(loaded, 16)

        with nc.Block() as block:
            @block.gpsimd
            def _(pool):
                nc.gpsimd.memset(ka[QROWS:QROWS + SPLIT, :, :, :], 1.0).then_inc(ones_set, 1)
                for s in range(1, NS):
                    if s == 1:
                        pool.wait_ge(stage0_loaded, 16 * LOADS)
                    if s >= NBUF:
                        pool.wait_ge(probs_used, UNITS * (s - NBUF + 1))
                    load_stage(pool, s)

            @block.sync
            def _(sp):
                def place(s, buf, c):
                    n = CPS * s + c
                    sp.wait_ge(max_rows_ready, n + 1)
                    sp.dma_start(k.max_scr[c % 2], max_rows[:, c % 2, :]).then_inc(max_stored, 16)
                    sp.wait_ge(max_stored, 16 * n + 16)
                    if not first(n):
                        sp.wait_ge(max_placed, 16 * n)
                    sp.dma_start(qa[QROWS:QROWS + SPLIT, buf, :, c * CH:(c + 1) * CH],
                                 k.max_scr[c % 2].rearrange("(o h) t -> o h t", o=SPLIT)).then_inc(max_placed, 16)

                def stage(s, buf, more, loads):
                    for n in range(UNITS):
                        turned = maxima_turned_at(s, n, more)
                        if turned:
                            place(turned[0], (buf + TURN_MAXIMA[n][1]) % NBUF, turned[1])

                load_stage(sp, 0)
                for c in range(2):
                    place(0, 0, c)
                sp.wait_ge(zeros_set, 1)
                with sp.Fori(0, NTILES) as t:
                    sp.dma_start(k.x_slots[at(t, ST, ST), :].rearrange("(p u) d -> p (u d)", p=P), zeros[:, :]
                                 ).then_inc(slots_zeroed, 16)
                all_stages(sp, stage)
                sp.wait_ge(slots_zeroed, 16 * NTILES)

            @block.tensor
            def _(pe):
                def maximum(s, buf, u):
                    c, i, bank, hp = max_units[u]
                    width = CH if bank < c else P * (i + 1)
                    if u >= 2 or not first(s):
                        pe.wait_ge(max_taken, NMAX * s + u - 1)
                    for hh in range(2):
                        hd = 2 * hp + hh
                        q0 = (c * TPC + i) * P
                        last = nc.tensor.matmul(p_m[:, u % 2, hh, 0:width], qa[0:QROWS, buf, hd, q0:q0 + P],
                                                ka[0:QROWS, buf, hd, bank * CH:bank * CH + width],
                                                start=True, stop=bank < c)
                        if bank == c:
                            last = nc.tensor.matmul(p_m[:, u % 2, hh, width - P:width], k.identb[:, :],
                                                    k.masks[:, 0, :], start=False, stop=True)
                    last.then_inc(max_scores, 1)

                def scores(s, buf, n, h):
                    c, j = units[n]
                    lo = max(0, j - TPC * c) * P
                    if HG * n + h >= 2 or not first(s):
                        pe.wait_ge(probs_ready, HG * (UNITS * s + n) + h - 1)
                    last = nc.tensor.matmul(p_s[:, h % 2, lo:CH], ka[0:QROWS + SPLIT, buf, h, j * P:(j + 1) * P],
                                            qa[0:QROWS + SPLIT, buf, h, c * CH + lo:(c + 1) * CH],
                                            start=True, stop=j < TPC * c)
                    if j >= TPC * c:
                        last = nc.tensor.matmul(p_s[:, h % 2, lo:lo + P], k.identb[:, :], k.masks[:, 1, :],
                                                start=False, stop=True)
                    last.then_inc(scores_ready, 1)

                def values(s, buf, n):
                    c, j = units[n]
                    lo = max(0, j - TPC * c) * P
                    pe.wait_ge(probs_ready, HG * (UNITS * s + n) + HG)
                    if j == 0 and (c or not first(s)):
                        pe.wait_ge(o_taken, CPS * s + c)
                    for h in range(HG):
                        last = nc.tensor.matmul(p_o[VW * h:VW * (h + 1), lo:CH], va[:, buf, j, VW * h:VW * (h + 1)],
                                                probs[:, n % 2, h, lo:CH], start=j == 0, stop=j == TPC * (c + 1) - 1)
                    last.then_inc(probs_used, 1)

                def turn_maxima(n):
                    pe.wait_ge(max_parts_ready, n + 1)
                    rows = p_misc[:, :].bitcast(BF16)
                    for i in range(TPC):
                        last = nc.tensor.transpose(rows[0:SPLIT * HG, i * P:(i + 1) * P],
                                                   max_parts[:, i, :, :].rearrange("p s h -> p (s h)"), k.identb[:, :])
                    last.then_inc(max_turned, 1)

                def turn_outputs(n, parity):
                    pe.wait_ge(o_taken, n + 1)
                    for u in range(TPC):
                        last = nc.tensor.transpose(p_misc[:, u * P:(u + 1) * P], o_sb[:, parity, u * P:(u + 1) * P],
                                                   k.ident[:, :])
                    last.then_inc(o_turned, 1)

                def turn_m(s, c):
                    if c == 2 and not first(s):
                        pe.wait_ge(att_ready, CPS * s + 1)
                    elif c == 0:
                        pe.wait_ge(max_rows_ready, CPS * s)
                    elif c == 2:
                        pe.wait_ge(max_rows_ready, 2)
                    elif c == 3:
                        pe.wait_ge(att_ready, CPS * s + 3)
                    else:
                        pe.wait_ge(att_ready, CPS * s)
                    turn_maxima(CPS * s + c)

                def turn_o(s, c, more):
                    if c == 1:
                        pe.wait_ge(att_ready, CPS * s + 2)
                    elif c == 0:
                        pe.wait_ge(max_rows_ready, CPS * s + 3)
                    elif c == 2:
                        pe.wait_ge(max_rows_ready, CPS * s + (5 if more else 4))
                    else:
                        pe.wait_ge(max_rows_ready, CPS * s + (6 if more else 4))
                        if not more:
                            pe.wait_ge(att_ready, CPS * s + 4)
                    turn_outputs(CPS * s + c, c % 2)

                def stage(s, buf, more, loads):
                    nbuf = (buf + 1) % NBUF
                    for n, (c, j) in enumerate(units):
                        if j == 0:
                            pe.wait_ge(max_placed, 16 * (CPS * s + c + 1))
                        for h in range(HG):
                            scores(s, buf, n, h)
                            if h == 1:
                                if n:
                                    values(s, buf, n - 1)
                                elif not first(s):
                                    values(s - 1, (buf - 1) % NBUF, UNITS - 1)
                        w = max_unit(s, n, more)
                        if w:
                            own_stage = n + MAX_LEAD < UNITS
                            if w[1] == 0:
                                pe.wait_ge(stage_loaded[nbuf], 16 * LOADS * loads)
                            for u in (2 * w[1], 2 * w[1] + 1):
                                maximum(w[0], buf if own_stage else nbuf, u)
                        turned = maxima_turned_at(s, n, more)
                        if turned:
                            turn_m(*turned)
                        if j == AFTER_TURN_O and c:
                            turn_o(s, c - 1, more)
                        elif j == AFTER_TURN_O and not first(s):
                            turn_o(s - 1, CPS - 1, True)

                pe.wait_ge(stage0_loaded, 16 * LOADS)
                pe.wait_ge(ones_set, 1)
                for u in range(2 * MAX_LEAD):
                    maximum(0, 0, u)
                    if ends_chunk(u):
                        c = max_units[u][0]
                        if c:
                            pe.wait_ge(max_rows_ready, c)
                        turn_maxima(c)
                all_stages(pe, stage)
                values(NS - 1, (NS - 1) % NBUF, UNITS - 1)
                turn_o(NS - 1, CPS - 1, False)

            @block.scalar
            def _(act):
                def exponentials(s, n):
                    c, j = units[n]
                    lo = max(0, j - TPC * c) * P
                    if n >= 2 or not first(s):
                        act.wait_ge(probs_used, UNITS * s + n - 1)
                    for h in range(HG):
                        act.wait_ge(scores_ready, HG * (UNITS * s + n) + h + 1)
                        nc.scalar.activation(probs[:, n % 2, h, lo:CH], p_s[:, h % 2, lo:CH], ACT.Exp,
                                             scale=DH ** -0.5).then_inc(probs_ready, 1)

                def take_o(s, c, n_last):
                    act.wait_ge(probs_used, UNITS * s + n_last + 1)
                    nc.scalar.activation(o_sb[:, c % 2, :], p_o[:, :], ACT.Copy).then_inc(o_taken, 1)

                def take_rows(n, c):
                    act.wait_ge(max_turned, n + 1)
                    if not (isinstance(n, int) and n < 2):
                        act.wait_ge(max_stored, 16 * (n - 1))
                    nc.scalar.activation(max_rows[:, c % 2, :], p_misc[:, :].bitcast(BF16)[0:SPLIT * HG, 0:CH],
                                         ACT.Copy).then_inc(max_rows_ready, 1)

                def stage(s, buf, more, loads):
                    for n, (c, j) in enumerate(units):
                        exponentials(s, n)
                        if j == AFTER_O and c:
                            take_o(s, c - 1, n - 1)
                        elif j == AFTER_O and not first(s):
                            take_o(s - 1, CPS - 1, UNITS - 1)
                        turned = maxima_turned_at(s, n - 1, more)
                        if turned:
                            take_rows(CPS * turned[0] + turned[1], turned[1])

                for c in range(2):
                    take_rows(c, c)
                all_stages(act, stage)
                take_o(NS - 1, CPS - 1, UNITS - 1)

            @block.vector
            def _(dve):
                def take_max(s, u):
                    c, i, bank, hp = max_units[u]
                    width = CH if bank < c else P * (i + 1)
                    dve.wait_ge(max_scores, NMAX * s + u + 1)
                    nc.vector.tensor_reduce(out=tile_max[:, 2 * hp:2 * hp + 2, i, bank], in_=p_m[:, u % 2, :, 0:width],
                                            op=ALU.max, axis=AX.X).then_inc(max_taken, 1)

                def split_max(s, c):
                    n = CPS * s + c
                    step = Count(dve, own, MAX_OWN * n)
                    dve.wait_ge(max_taken, NMAX * s + sum(ends_chunk(u) * (u + 1) for u in range(NMAX) if max_units[u][0] == c))
                    if not first(n):
                        dve.wait_ge(max_turned, n)
                    part = [max_parts[:, :, q, :].rearrange("p i h -> p h i") for q in range(SPLIT)]
                    step.step(nc.vector.tensor_reduce(out=row_max[:, :, :], in_=tile_max[:, :, :, 0:c + 1],
                                                      op=ALU.max, axis=AX.X))
                    step.step(nc.vector.tensor_scalar(part[0], row_max[:, :, :], -1.0, None, ALU.mult))
                    step.step(nc.vector.scalar_tensor_tensor(out=max_rest[:, :, :], in0=row_max[:, :, :], scalar=-1.0,
                                                             in1=part[0], op0=ALU.mult, op1=ALU.subtract))
                    step.step(nc.vector.tensor_copy(part[1], max_rest[:, :, :]))
                    nc.vector.tensor_tensor(part[2], max_rest[:, :, :], part[1], ALU.subtract).then_inc(max_parts_ready, 1)
                    assert step.n == MAX_OWN

                def divide(s, c):
                    n = CPS * s + c
                    b = s // (H0 // HG)
                    dve.wait_ge(o_turned, n + 1)
                    o = p_misc[:, :].rearrange("p (u h w) -> p u h w", u=TPC, h=HG)
                    nc.vector.reciprocal(recip[:, :, :], o[:, :, :, DH]).then_inc(recip_ready, 1)
                    dve.wait_ge(recip_ready, n + 1)
                    nc.vector.tensor_tensor(
                        k.x[:, at(b * JT + c * TPC, 1, TPC), at(s % (H0 // HG), HG * DH, HG * DH)]
                        .rearrange("p u (h d) -> p u h d", h=HG),
                        o[:, :, :, 0:DH], recip[:, :, :].unsqueeze(3).to_broadcast([P, TPC, HG, DH]),
                        ALU.mult).then_inc(att_ready, 1)

                def stage(s, buf, more, loads):
                    for n, (c, j) in enumerate(units):
                        w = max_unit(s, n, more)
                        if w:
                            for u in (2 * w[1], 2 * w[1] + 1):
                                take_max(w[0], u)
                                if ends_chunk(u):
                                    split_max(w[0], max_units[u][0])
                        if j == AFTER_TURN_O and c:
                            divide(s, c - 1)
                        elif j == AFTER_TURN_O and not first(s):
                            divide(s - 1, CPS - 1)

                nc.vector.memset(zeros[:, :], 0.0).then_inc(zeros_set, 1)
                nc.vector.memset(recip[:, :, :], 0.0).then_inc(att_ready, 1)
                for u in range(2 * MAX_LEAD):
                    take_max(0, u)
                    if ends_chunk(u):
                        split_max(0, max_units[u][0])
                all_stages(dve, stage)
                divide(NS - 1, CPS - 1)


def output_projection(nc, a, k):
    with ExitStack() as stack:
        m = Mem(nc, stack)
        w = m.sb("wo", [P, KT, D])
        xin = m.sb("o_xin", [P, 2, TPC, D])
        still = m.sb("o_still", [P, TPC, D])
        aT = m.sb("o_aT", [P, KT, CH])
        gated = m.sb("o_gated", [P, TPC, D])
        p_t = m.ps("o_pt", [P, KT, CH])
        p_o = m.ps("o_po", [P, TPC, D])
        w_loaded, still_ready, stats_done = m.sem("o_w_loaded"), m.sem("o_still_ready"), m.sem("o_stats_done")
        x_loaded = [m.sem(f"o_x_loaded{n}") for n in range(2)]
        turned, aT_ready, product = m.sem("o_turned_"), m.sem("o_aT_ready"), m.sem("o_product")
        scaled, x1_ready = m.sem("o_scaled"), m.sem("o_x1_ready")
        with nc.Block() as block:
            @block.sync
            def _(sp):
                def load(i, par):
                    sp.dma_start(xin[:, par, :, :],
                                 a["x"][at(i, CH, CH), :].rearrange("(u p) d -> p u d", p=P)).then_inc(x_loaded[par], 16)

                sp.dma_start(w[:, :, :], a["woT"].rearrange("(k p) n -> p k n", p=P)).then_inc(w_loaded, 16)
                load(0, 0)
                load(1, 1)
                with sp.Fori(1, NCH // 2) as i:
                    for par in range(2):
                        sp.wait_ge(x1_ready, 2 * i + par - 1)
                        load(2 * i + par, par)

            @block.scalar
            def _(act):
                def chunk(i):
                    if not first(i):
                        act.wait_ge(turned, i)
                    nc.scalar.activation(still[:, :, :], k.x[:, at(i, TPC, TPC), :], ACT.Copy).then_inc(still_ready, 1)
                    act.wait_ge(turned, i + 1)
                    if not first(i):
                        act.wait_ge(product, i)
                    nc.scalar.activation(aT[:, :, :], p_t[:, :, :], ACT.Copy).then_inc(aT_ready, 1)

                chunk(0)
                with act.Fori(1, NCH) as i:
                    chunk(i)

            @block.tensor
            def _(pe):
                def chunk(i):
                    pe.wait_ge(still_ready, i + 1)
                    for kt in range(KT):
                        for u in range(TPC):
                            last = nc.tensor.transpose(p_t[:, kt, u * P:(u + 1) * P], still[:, u, kt * P:(kt + 1) * P],
                                                       k.ident[:, :])
                    last.then_inc(turned, 1)
                    pe.wait_ge(aT_ready, i + 1)
                    if not first(i):
                        pe.wait_ge(scaled, i)
                    for u in range(TPC):
                        for kt in range(KT):
                            last = nc.tensor.matmul(p_o[:, u, :], aT[:, kt, u * P:(u + 1) * P], w[:, kt, :],
                                                    start=kt == 0, stop=kt == KT - 1)
                    last.then_inc(product, 1)

                pe.wait_ge(w_loaded, 16)
                chunk(0)
                with pe.Fori(1, NCH) as i:
                    chunk(i)

            @block.vector
            def _(dve):
                with dve.Fori(0, NCH // 2) as turn:
                    for par in range(2):
                        i = 2 * turn + par
                        dve.wait_ge(product, i + 1)
                        nc.vector.tensor_tensor(gated[:, :, :], p_o[:, :, :], k.mod(0, i // CPS, GA),
                                                ALU.mult).then_inc(scaled, 1)
                        dve.wait_ge(x_loaded[par], 16 * (turn + 1))
                        dve.wait_ge(scaled, i + 1)
                        nc.vector.tensor_tensor(k.x[:, at(i, TPC, TPC), :], gated[:, :, :], xin[:, par, :, :],
                                                ALU.add).then_inc(x1_ready, 1)
                        dve.wait_ge(x1_ready, i + 1)
                        row_stats(nc, k, i, stats_done)


def top1_experts(nc, a, k):
    BANKS = E0 * D // CH
    EPB = E0 // BANKS
    HALF = E0 // 2
    with ExitStack() as stack:
        m = Mem(nc, stack)
        raw, raw_gate = m.sb("c_raw", [P, KT, E0 * D]), m.sb("c_raw_gate", [P, KT, E0])
        w = m.sb("w_expert", [P, 2, KT, E0 * D], F32R)
        gate = m.sb("w_gate0", [P, 2, KT, E0], F32R)
        iota = m.sb("iota_e", [P, E0])
        h = m.sb("c_h", [P, 2, D])
        hT = m.sb("c_hT", [P, 2, 2, KT, P], F32R)
        top, top_at, same = m.sb("c_top", [P, 1]), m.sb("c_top_at", [P, 1]), m.sb("c_same", [P, E0])
        onehot = m.sb("c_onehot", [P, 2, E0])
        acc, terms = m.sb("c_acc", [P, 2, D]), m.sb("c_terms", [P, HALF, D])
        pairs_sum, half_sum = m.sb("c_pairs_sum", [P, HALF // 2, D]), m.sb("c_half_sum", [P, D])
        p_e = m.ps("p_e", [P, BANKS, CH])
        p_t = m.ps("c_pt", [P, KT, P])
        p_g = m.ps("p_g", [P, E0])
        loaded = m.sem("c_loaded")
        w_high, w_ready = m.sem("c_w_high"), m.sem("c_w_ready")
        h_centered, h_scaled, h_ready = m.sem("c_h_centered"), m.sem("c_h_scaled"), m.sem("c_h_ready")
        turned, hT_high, hT_ready, gate_psum = m.sem("c_turned"), m.sem("c_hT_high"), m.sem("c_hT_ready"), m.sem("c_gate_psum")
        picked, onehot_ready, expert_psum = m.sem("c_picked"), m.sem("c_onehot_ready"), m.sem("c_expert_psum")
        taken_dve, taken_act = m.sem("c_taken_dve"), m.sem("c_taken_act")
        paired, half_ready, summed = m.sem("c_paired"), m.sem("c_half_ready"), m.sem("c_summed")
        own, stats_done = m.sem("c_own"), m.sem("c_stats_done")
        LOADS, PICKS = 3, 3

        def all_tiles(engine, tile):
            tile(0, 0, 2)
            tile(1, 1, 2)
            with engine.Fori(1, NT // 2 - 1) as i:
                tile(2 * i, 0, 2)
                tile(2 * i + 1, 1, 2)
            tile(NT - 2, 0, 1)
            tile(NT - 1, 1, 0)

        def bank_of(x, part, bank):
            return x[:, part, :, bank * CH:(bank + 1) * CH]

        with nc.Block() as block:
            @block.sync
            def _(sp):
                sp.dma_start(raw_gate[:, :, :], a["gateT"].rearrange("(k p) n -> p k n", p=P)).then_inc(loaded, 16)
                sp.dma_start(iota[:, :], a["iota8"]).then_inc(loaded, 16)
                sp.dma_start(raw[:, :, :], a["expertT"].rearrange("(k p) n -> p k n", p=P)).then_inc(loaded, 16)
                sp.wait_ge(loaded, 16 * LOADS)

            @block.gpsimd
            def _(pool):
                def scale(t, par):
                    pool.wait_ge(h_centered, t + 1)
                    nc.gpsimd.tensor_tensor(h[:, par, :], h[:, par, :], k.mod1(0, t // JT, CB), ALU.mult).then_inc(h_scaled, 1)
                    pool.wait_ge(h_scaled, t + 1)
                    nc.gpsimd.tensor_tensor(h[:, par, :], h[:, par, :], k.mod1(0, t // JT, SB_), ALU.add).then_inc(h_ready, 1)

                def tile(t, par, more):
                    if more == 2:
                        scale(t + 2, par)
                    if not first(t):
                        pool.wait_ge(half_ready, t)
                    pool.wait_ge(taken_act, HALF * t + HALF)
                    nc.gpsimd.tensor_tensor(pairs_sum[:, :, :], terms[:, 0:HALF // 2, :], terms[:, HALF // 2:HALF, :],
                                            ALU.add).then_inc(paired, 1)
                    pool.wait_ge(paired, t + 1)
                    if not first(t):
                        pool.wait_ge(summed, t)
                    nc.gpsimd.tensor_tensor(half_sum[:, :], pairs_sum[:, 0, :], pairs_sum[:, 1, :], ALU.add
                                            ).then_inc(half_ready, 1)

                root(nc, pool, k, 1)
                scale(0, 0)
                scale(1, 1)
                for n in range(1 + BANKS):
                    pool.wait_ge(w_high, n + 1)
                    if n:
                        nc.gpsimd.tensor_tensor(bank_of(w, LO, n - 1), raw[:, :, (n - 1) * CH:n * CH],
                                                bank_of(w, HI, n - 1), ALU.subtract).then_inc(w_ready, 1)
                    else:
                        nc.gpsimd.tensor_tensor(gate[:, LO, :, :], raw_gate[:, :, :], gate[:, HI, :, :],
                                                ALU.subtract).then_inc(w_ready, 1)
                all_tiles(pool, tile)

            @block.scalar
            def _(act):
                def round_hT(t, par):
                    act.wait_ge(turned, t + 1)
                    nc.scalar.activation(hT[:, par, HI, :, :], p_t[:, :, :], ACT.Copy).then_inc(hT_high, 1)

                def tile(t, par, more):
                    if more:
                        round_hT(t + 1, 1 - par)
                    if not first(t):
                        act.wait_ge(paired, t)
                    act.wait_ge(onehot_ready, t + 1)
                    for e in range(HALF, E0):
                        act.wait_ge(expert_psum, BANKS * t + e // EPB + 1)
                        nc.scalar.activation(terms[:, e - HALF, :], p_e[:, e // EPB, (e % EPB) * D:(e % EPB + 1) * D],
                                             ACT.Copy, scale=onehot[:, par, e:e + 1]).then_inc(taken_act, 1)

                act.wait_ge(loaded, 16 * LOADS)
                nc.scalar.activation(gate[:, HI, :, :], raw_gate[:, :, :], ACT.Copy).then_inc(w_high, 1)
                for bank in range(BANKS):
                    nc.scalar.activation(bank_of(w, HI, bank), raw[:, :, bank * CH:(bank + 1) * CH], ACT.Copy).then_inc(w_high, 1)
                round_hT(0, 0)
                all_tiles(act, tile)

            @block.tensor
            def _(pe):
                def turn(t, par):
                    pe.wait_ge(h_ready, t + 1)
                    if not first(t):
                        pe.wait_ge(hT_ready, t)
                    for kt in range(KT):
                        last = nc.tensor.transpose(p_t[:, kt, :], h[:, par, kt * P:(kt + 1) * P], k.ident[:, :])
                    last.then_inc(turned, 1)

                def product(out, t, par, weights, done):
                    for kt in range(KT):
                        for wp, hp in PRODUCTS:
                            last = nc.tensor.matmul(out, hT[:, par, hp, kt, :], weights(wp, kt),
                                                    start=(kt, wp, hp) == (0, HI, HI), stop=(kt, wp, hp) == (KT - 1, LO, HI))
                    last.then_inc(done, 1)

                def choose(t, par):
                    pe.wait_ge(hT_ready, t + 1)
                    if not first(t):
                        pe.wait_ge(onehot_ready, t)
                    product(p_g[:, :], t, par, lambda part, kt: gate[:, part, kt, :], gate_psum)

                def experts(t, par, bank):
                    if first(t):
                        pe.wait_ge(w_ready, bank + 2)
                    elif bank < BANKS // 2:
                        pe.wait_ge(taken_dve, HALF * (t - 1) + EPB * (bank + 1))
                    else:
                        pe.wait_ge(taken_act, HALF * (t - 1) + EPB * (bank - BANKS // 2 + 1))
                    product(p_e[:, bank, :], t, par, lambda part, kt: w[:, part, kt, bank * CH:(bank + 1) * CH], expert_psum)

                def tile(t, par, more):
                    for bank in range(BANKS):
                        experts(t, par, bank)
                        if more and bank == 1:
                            turn(t + 1, 1 - par)
                    if more:
                        choose(t + 1, 1 - par)

                turn(0, 0)
                pe.wait_ge(w_ready, 1)
                choose(0, 0)
                all_tiles(pe, tile)

            @block.vector
            def _(dve):
                def center(t, par):
                    nc.vector.tensor_scalar(h[:, par, :], k.x[:, at(t, 1, 1), :].rearrange("p o d -> p (o d)"),
                                            k.mean[:, at(t, 1, 1)], k.rstd[:, at(t, 1, 1)],
                                            ALU.subtract, ALU.mult).then_inc(h_centered, 1)

                def rest_of_hT(t, par):
                    dve.wait_ge(hT_high, t + 1)
                    nc.vector.tensor_tensor(hT[:, par, LO, :, :], p_t[:, :, :], hT[:, par, HI, :, :],
                                            ALU.subtract).then_inc(hT_ready, 1)

                def pick(t, par):
                    c = Count(dve, picked, PICKS * t)
                    dve.wait_ge(gate_psum, t + 1)
                    c.step(nc.vector.tensor_reduce(out=top[:, :], in_=p_g[:, :], op=ALU.max, axis=AX.X))
                    c.step(nc.vector.scalar_tensor_tensor(out=same[:, :], in0=p_g[:, :], scalar=top[:, :], in1=iota[:, :],
                                                          op0=ALU.is_equal, op1=ALU.mult))
                    c.step(nc.vector.tensor_reduce(out=top_at[:, :], in_=same[:, :], op=ALU.min, axis=AX.X))
                    nc.vector.tensor_scalar(onehot[:, par, :], iota[:, :], top_at[:, :], None, ALU.is_equal).then_inc(onehot_ready, 1)
                    dve.wait_ge(onehot_ready, t + 1)
                    assert c.n == PICKS

                def finish(t, par):
                    total = acc[:, par, :]
                    dve.wait_ge(half_ready, t + 1)
                    nc.vector.tensor_tensor(total, total, half_sum[:, :], ALU.add).then_inc(summed, 1)
                    dve.wait_ge(summed, t + 1)
                    x = k.x[:, at(t, 1, 1), :].rearrange("p o d -> p (o d)")
                    nc.vector.tensor_tensor(total, total, k.mod1(0, t // JT, GB), ALU.mult).then_inc(k.scaled, 1)
                    dve.wait_ge(k.scaled, t + 1)
                    nc.vector.tensor_tensor(x, x, total, ALU.add).then_inc(k.x2_ready, 1)
                    dve.wait_ge(k.x2_ready, t + 1)
                    nc.vector.bn_stats(out=k.stats[:, at(t, 1, 1), :].rearrange("p o s -> p (o s)"), in_=x).then_inc(stats_done, 1)

                def tile(t, par, more):
                    for e in range(HALF):
                        if e % EPB == 0:
                            dve.wait_ge(expert_psum, BANKS * t + e // EPB + 1)
                        nc.vector.scalar_tensor_tensor(
                            out=acc[:, par, :], in0=p_e[:, e // EPB, (e % EPB) * D:(e % EPB + 1) * D],
                            scalar=onehot[:, par, e:e + 1], in1=h[:, par, :] if e == 0 else acc[:, par, :],
                            op0=ALU.mult, op1=ALU.add).then_inc(taken_dve, 1)
                        dve.wait_ge(taken_dve, HALF * t + e + 1)
                    if more == 2:
                        center(t + 2, par)
                    if more:
                        rest_of_hT(t + 1, 1 - par)
                    if not first(t):
                        finish(t - 1, 1 - par)
                    if more:
                        pick(t + 1, 1 - par)

                aggregate(nc, Count(dve, own), k).then_inc(k.ve_ready, 1)
                dve.wait_ge(k.rstd_ready, 2)
                center(0, 0)
                center(1, 1)
                rest_of_hT(0, 0)
                pick(0, 0)
                all_tiles(dve, tile)
                finish(NT - 1, 1)


def second_norm(nc, a, k, norm, name, shift, scale, h_all, xn_all, xnT_all, weight, logits):
    with ExitStack() as stack:
        m = Mem(nc, stack)
        h = m.sb(name + "h", [P, TPC, D])
        xn = m.sb(name + "xn", [P, TPC, D])
        xnT = m.sb(name + "xnT", [P, KT, CH]) if xnT_all is None else None
        squares = m.sb(name + "squares", [P, D])
        ss, ms, rms, inv = (m.sb(name + n, [P, TPC]) for n in ("ss", "ms", "rms", "inv"))
        power = m.sb(name + "power", [P, TPC])
        p_t = m.ps(name + "pt", [P, KT, CH])
        p_l = m.ps(name + "pl", [P, TPC, E1])
        h_ready = m.sem(name + "h_ready")
        squared, ms_ready, rms_ready = m.sem(name + "squared"), m.sem(name + "ms_ready"), m.sem(name + "rms_ready")
        inv_ready, xn_ready, turned = m.sem(name + "inv_ready"), m.sem(name + "xn_ready"), m.sem(name + "turned")
        xnT_ready, h_kept, logit_psum = m.sem(name + "xnT_ready"), m.sem(name + "h_kept"), m.sem(name + "logit_psum")
        logits_taken, own, power_set = m.sem(name + "logits_taken"), m.sem(name + "own"), m.sem(name + "power_set")
        w_loaded, stepped = m.sem(name + "w_loaded"), m.sem(name + "stepped")
        if weight is not None:
            w_rms = m.sb(name + "w_rms", [P, D])
        if h_all is not None:
            o_bias = m.sb(name + "o_bias", [P, D])
        if logits is not None:
            w_l = m.sb(name + "w_l", [P, KT, E1])
            b_l = m.sb(name + "b_l", [P, E1])
        LOADS = (weight is not None) + (h_all is not None) + 2 * (logits is not None)
        with nc.Block() as block:
            @block.sync
            def _(sp):
                if weight is not None:
                    sp.dma_start(w_rms[:, :], weight.partition_broadcast(P)).then_inc(w_loaded, 16)
                if h_all is not None:
                    sp.dma_start(o_bias[:, :], a["o_b"].partition_broadcast(P)).then_inc(w_loaded, 16)
                if logits is not None:
                    sp.dma_start(w_l[:, :, :], a["Wg"].rearrange("(k p) n -> p k n", p=P)).then_inc(w_loaded, 16)
                    sp.dma_start(b_l[:, :], a["bg"].partition_broadcast(P)).then_inc(w_loaded, 16)
                sp.wait_ge(w_loaded, 16 * LOADS)

            @block.gpsimd
            def _(pool):
                root(nc, pool, k, norm)
                nc.gpsimd.memset(power[:, :], 0.5 if h_all is not None else -0.5).then_inc(power_set, 1)
                pool.wait_ge(power_set, 1)
                pool.wait_ge(w_loaded, 16 * LOADS)
                with pool.Fori(0, NCH) as i:
                    pool.wait_ge(ms_ready, i + 1)
                    nc.gpsimd.tensor_tensor(rms[:, :], ms[:, :], power[:, :], ALU.pow).then_inc(rms_ready, 1)
                    if h_all is not None:
                        nc.gpsimd.tensor_tensor(h_all[:, at(i, TPC, TPC), :], h[:, :, :],
                                                o_bias[:, :].unsqueeze(1).to_broadcast([P, TPC, D]),
                                                ALU.add).then_inc(h_kept, 1)

            @block.scalar
            def _(act):
                def chunk(i):
                    act.wait_ge(h_ready, i + 1)
                    for u in range(TPC):
                        if u or not first(i):
                            act.wait_ge(squared, TPC * i + u)
                        nc.scalar.activation(squares[:, :], h[:, u, :], ACT.Square, accum_out=ss[:, u:u + 1]).then_inc(squared, 1)
                    act.wait_ge(inv_ready, i + 1)
                    if not first(i):
                        act.wait_ge(turned, i)
                    for u in range(TPC):
                        nc.scalar.activation(xn[:, u, :], h[:, u, :], ACT.Copy, scale=inv[:, u:u + 1]).then_inc(xn_ready, 1)
                    act.wait_ge(turned, i + 1)
                    if xnT_all is not None:
                        dst = xnT_all[:, :, at(i, CH, CH)]
                    else:
                        dst = xnT[:, :, :]
                        if not first(i):
                            act.wait_ge(logit_psum, i)
                    nc.scalar.activation(dst, p_t[:, :, :], ACT.Copy).then_inc(xnT_ready, 1)

                chunk(0)
                with act.Fori(1, NCH) as i:
                    chunk(i)

            @block.tensor
            def _(pe):
                if logits is not None:
                    pe.wait_ge(w_loaded, 16 * LOADS)

                def chunk(i):
                    pe.wait_ge(xn_ready if weight is None else stepped, TPC * i + TPC if weight is None else i + 1)
                    if not first(i):
                        pe.wait_ge(xnT_ready, i)
                    for kt in range(KT):
                        for u in range(TPC):
                            last = nc.tensor.transpose(p_t[:, kt, u * P:(u + 1) * P], xn[:, u, kt * P:(kt + 1) * P],
                                                       k.ident[:, :])
                    last.then_inc(turned, 1)
                    if logits is not None:
                        pe.wait_ge(xnT_ready, i + 1)
                        if not first(i):
                            pe.wait_ge(logits_taken, i)
                        for u in range(TPC):
                            for kt in range(KT):
                                last = nc.tensor.matmul(p_l[:, u, :], xnT[:, kt, u * P:(u + 1) * P], w_l[:, kt, :],
                                                        start=kt == 0, stop=kt == KT - 1)
                        last.then_inc(logit_psum, 1)

                chunk(0)
                with pe.Fori(1, NCH) as i:
                    chunk(i)

            @block.vector
            def _(dve):
                OWN = NORM_STEPS + (1 if h_all is not None else 0)
                dve.wait_ge(w_loaded, 16 * LOADS)
                aggregate(nc, Count(dve, own), k).then_inc(k.ve_ready, 1)
                dve.wait_ge(k.rstd_ready, norm + 1)

                def chunk(i):
                    c = Count(dve, own, AGGREGATE_STEPS + OWN * i)
                    if not first(i):
                        dve.wait_ge(xn_ready, TPC * i)
                        if h_all is not None:
                            dve.wait_ge(h_kept, i)
                    b = i // CPS
                    normalize(nc, k, c, i, h[:, :, :], k.mod(1, b, scale), k.mod(1, b, shift), h_ready)
                    dve.wait_ge(squared, TPC * i + TPC)
                    if h_all is not None:
                        nc.vector.tensor_scalar(ms[:, :], ss[:, :], 1.0 / D, None, ALU.mult).then_inc(ms_ready, 1)
                        dve.wait_ge(rms_ready, i + 1)
                        c.step(nc.vector.tensor_scalar(rms[:, :], rms[:, :], 1e-8, None, ALU.add))
                        nc.vector.reciprocal(inv[:, :], rms[:, :]).then_inc(inv_ready, 1)
                    else:
                        nc.vector.tensor_scalar(ms[:, :], ss[:, :], 1.0 / D, float(np.finfo(np.float32).eps),
                                                ALU.mult, ALU.add).then_inc(ms_ready, 1)
                        dve.wait_ge(rms_ready, i + 1)
                        nc.vector.tensor_copy(inv[:, :], rms[:, :]).then_inc(inv_ready, 1)
                    if weight is not None:
                        dve.wait_ge(xn_ready, TPC * i + TPC)
                        nc.vector.tensor_tensor(xn[:, :, :], xn[:, :, :], w_rms[:, :].unsqueeze(1).to_broadcast([P, TPC, D]),
                                                ALU.mult).then_inc(stepped, 1)
                        dve.wait_ge(stepped, i + 1)
                        nc.vector.tensor_copy(xn_all[:, at(i, TPC, TPC), :], xn[:, :, :]).then_inc(h_kept, 1)
                        dve.wait_ge(h_kept, i + 1)
                    if logits is not None:
                        dve.wait_ge(logit_psum, i + 1)
                        nc.vector.tensor_tensor(logits[:, at(i, TPC, TPC), :], p_l[:, :, :],
                                                b_l[:, :].unsqueeze(1).to_broadcast([P, TPC, E1]),
                                                ALU.add).then_inc(logits_taken, 1)
                    assert c.n == OWN

                chunk(0)
                with dve.Fori(1, NCH) as i:
                    chunk(i)


def mix(nc, a, k, h_all, xnT_all):
    with ExitStack() as stack:
        m = Mem(nc, stack)
        w = m.sb("w_uv", [P, KT, 2 * F1])
        wo = m.sb("w_o1", [P, FB1, D])
        bias = m.sb("b_uv", [P, 2 * FB1])
        toep = m.sb("toep", [P, 3, FB1])
        u_sb = m.sb("u_sb", [P, B, FB1, CH])
        v_sb = m.sb("v_sb", [P, B, FB1, CH])
        y_sb = m.sb("y_sb", [P, B, FB1, CH])
        p_uv = m.ps("p_uv", [P, 4, CH])
        p_o = m.ps("d_po", [P, B, TPC, D])
        loaded, uv_psum, uv_ready = m.sem("d_loaded"), m.sem("d_uv_psum"), m.sem("d_uv_ready")
        own, g_ready, product, x3_ready = m.sem("d_own"), m.sem("d_g_ready"), m.sem("d_product"), m.sem("d_x3_ready")
        taken, taken_stats = m.sem("d_taken"), m.sem("d_stats_done")
        LOADS = 4
        NB = 2 * B * FB1
        order = [(1, n, f) for n in range(B) for f in range(FB1)] + [(0, n, f) for n in range(B) for f in range(FB1)]
        OWN = 4 * FB1 + B
        with nc.Block() as block:
            @block.sync
            def _(sp):
                sp.dma_start(w[:, :, :], a["w_uv"].rearrange("(k p) n -> p k n", p=P)).then_inc(loaded, 16)
                sp.dma_start(wo[:, :, :], a["o_wT"].rearrange("(f p) n -> p f n", p=P)).then_inc(loaded, 16)
                sp.dma_start(bias[:, :], a["b_uv"]).then_inc(loaded, 16)
                sp.dma_start(toep[:, :, :], a["toep"]).then_inc(loaded, 16)
                sp.wait_ge(loaded, 16 * LOADS)

            @block.tensor
            def _(pe):
                def chunk(c):
                    for q, (is_v, n, f) in enumerate(order):
                        if q >= 4 or not first(c):
                            pe.wait_ge(uv_ready, NB * c + q - 3)
                        for kt in range(KT):
                            last = nc.tensor.matmul(p_uv[:, q % 4, :], w[:, kt, is_v * F1 + f * P:is_v * F1 + (f + 1) * P],
                                                    xnT_all[:, kt, at(n * CPS + c, CH, CH)],
                                                    start=kt == 0, stop=kt == KT - 1)
                        last.then_inc(uv_psum, 1)
                    for n in range(B):
                        pe.wait_ge(g_ready, B * c + n + 1)
                        if not first(c):
                            pe.wait_ge(taken, B * (c - 1) + n + 1)
                        for u in range(TPC):
                            for f in range(FB1):
                                last = nc.tensor.matmul(p_o[:, n, u, :], y_sb[:, n, f, u * P:(u + 1) * P], wo[:, f, :],
                                                        start=f == 0, stop=f == FB1 - 1)
                        last.then_inc(product, 1)

                pe.wait_ge(loaded, 16 * LOADS)
                chunk(0)
                with pe.Fori(1, CPS) as c:
                    chunk(c)

            @block.scalar
            def _(act):
                def chunk(c):
                    for q, (is_v, n, f) in enumerate(order):
                        act.wait_ge(uv_psum, NB * c + q + 1)
                        if q == 0 and not first(c):
                            act.wait_ge(g_ready, B * c)
                        dst = v_sb if is_v else u_sb
                        nc.scalar.activation(dst[:, n, f, :], p_uv[:, q % 4, :], ACT.Silu,
                                             bias=bias[:, is_v * FB1 + f:is_v * FB1 + f + 1]).then_inc(uv_ready, 1)

                act.wait_ge(loaded, 16 * LOADS)
                chunk(0)
                with act.Fori(1, CPS) as c:
                    chunk(c)

            @block.vector
            def _(dve):
                dve.wait_ge(loaded, 16 * LOADS)

                def chunk(c):
                    cnt = Count(dve, own, OWN * c)
                    dve.wait_ge(uv_ready, NB * c + B * FB1)
                    if not first(c):
                        dve.wait_ge(product, B * c)
                    for f in range(FB1):
                        for n, which in ((0, 2), (1, 1)):
                            cnt.add(nc.vector.tensor_scalar(y_sb[:, n, f, :], v_sb[:, 1 - n, f, :],
                                                            toep[:, which, f:f + 1], None, ALU.mult))
                    cnt.wait()
                    for f in range(FB1):
                        for n in range(B):
                            cnt.add(nc.vector.scalar_tensor_tensor(out=y_sb[:, n, f, :], in0=v_sb[:, n, f, :],
                                                                   scalar=toep[:, 0, f:f + 1], in1=y_sb[:, n, f, :],
                                                                   op0=ALU.mult, op1=ALU.add))
                    cnt.wait()
                    for n in range(B):
                        dve.wait_ge(uv_ready, NB * c + B * FB1 + FB1 * (n + 1))
                        nc.vector.tensor_tensor(y_sb[:, n, :, :], y_sb[:, n, :, :], u_sb[:, n, :, :], ALU.mult).then_inc(g_ready, 1)
                    for n in range(B):
                        hh = h_all[:, at(n * CPS + c, TPC, TPC), :]
                        x = k.x[:, at(n * CPS + c, TPC, TPC), :]
                        dve.wait_ge(product, B * c + n + 1)
                        nc.vector.tensor_tensor(hh, p_o[:, n, :, :], hh, ALU.add).then_inc(taken, 1)
                        dve.wait_ge(taken, B * c + n + 1)
                        cnt.step(nc.vector.tensor_tensor(hh, hh, k.mod(1, n, GA), ALU.mult))
                        nc.vector.tensor_tensor(x, x, hh, ALU.add).then_inc(x3_ready, 1)
                        dve.wait_ge(x3_ready, B * c + n + 1)
                        row_stats(nc, k, n * CPS + c, taken_stats)
                    assert cnt.n == OWN

                chunk(0)
                with dve.Fori(1, CPS) as c:
                    chunk(c)


def route(nc, a, k, logits, xn_all):
    with ExitStack() as stack:
        m = Mem(nc, stack)
        iota, later, ones = m.sb("r_iota", [P, E1]), m.sb("r_later", [P, P]), m.sb("r_ones", [P, P])
        tiles = m.sb("r_tiles", [P, NTILES])
        best = m.sb("r_best", [P, 2, NT])
        same, rest = m.sb("r_same", [P, NT, E1]), m.sb("r_rest", [P, NT, E1])
        first_at = m.sb("r_first_at", [P, NT])
        onehot = m.sb("r_onehot", [P, 2, NT, E1])
        chosen, total = m.sb("r_chosen", [P, NT, E1]), m.sb("r_total", [P, NT, E1])
        run = m.sb("r_run", [P, 2, NT, E1])
        count_i = m.sb("r_count_i", [P, E1], I32)
        ntile, ends = m.sb("r_ntile", [P, E1]), m.sb("r_ends", [P, 2, E1])
        start = m.sb("r_start", [P, E1])
        slot = m.sb("r_slot", [P, NT])
        gap, weight_sum = m.sb("r_gap", [P, NT]), m.sb("r_weight_sum", [P, NT])
        owner, owner_f = m.sb("r_owner", [P, NTILES, E1]), m.sb("r_owner_f", [P, NTILES])
        p_rank, p_total = m.ps("p_rank", [P, NT, E1]), m.ps("p_total", [P, NT, E1])
        loaded, own, chosen_ready, counted = m.sem("r_loaded"), m.sem("r_own"), m.sem("r_chosen_ready"), m.sem("r_counted")
        gap_ready, exp_ready, slots_ready, scattered = (m.sem("r_gap_ready"), m.sem("r_exp_ready"),
                                                        m.sem("r_slots_ready"), m.sem("r_scattered"))
        LOADS = 4
        with nc.Block() as block:
            @block.sync
            def _(sp):
                for dst, src in ((iota, "iota8"), (later, "before"), (ones, "ones"), (tiles, "iota_tiles")):
                    sp.dma_start(dst[:, :], a[src]).then_inc(loaded, 16)
                sp.wait_ge(loaded, 16 * LOADS)

            @block.tensor
            def _(pe):
                pe.wait_ge(loaded, 16 * LOADS)
                pe.wait_ge(chosen_ready, 1)
                nc.tensor.matmul(p_rank[:, :, :], later[:, :], chosen[:, :, :], start=True, stop=True).then_inc(counted, 1)
                nc.tensor.matmul(p_total[:, :, :], ones[:, :], chosen[:, :, :], start=True, stop=True).then_inc(counted, 1)

            @block.scalar
            def _(act):
                act.wait_ge(gap_ready, 1)
                nc.scalar.activation(k.weights[:, 1, :], gap[:, :], ACT.Exp).then_inc(exp_ready, 1)

            @block.vector
            def _(dve):
                dve.wait_ge(loaded, 16 * LOADS)
                c = Count(dve, own)

                def tt(out, x, y, op):
                    c.step(nc.vector.tensor_tensor(out, x, y, op))

                def ts(out, x, s1, s2, op1, op2=None):
                    if op2 is None:
                        c.step(nc.vector.tensor_scalar(out, x, s1, None, op1))
                    else:
                        c.step(nc.vector.tensor_scalar(out, x, s1, s2, op1, op2))

                def wide(x, n=E1):
                    return x.unsqueeze(2).to_broadcast([P, NT, n])

                iota_all = iota[:, :].unsqueeze(1).to_broadcast([P, NT, E1])
                for q in range(2):
                    src = logits[:, :, :] if q == 0 else rest[:, :, :]
                    c.step(nc.vector.tensor_reduce(out=best[:, q, :], in_=src, op=ALU.max, axis=AX.X))
                    tt(same[:, :, :], src, wide(best[:, q, :]), ALU.is_equal)
                    c.step(nc.vector.scalar_tensor_tensor(out=same[:, :, :], in0=iota_all, scalar=0.0,
                                                          in1=same[:, :, :], op0=ALU.add, op1=ALU.mult))
                    c.step(nc.vector.tensor_reduce(out=first_at[:, :], in_=same[:, :, :], op=ALU.min, axis=AX.X))
                    tt(onehot[:, q, :, :], iota_all, wide(first_at[:, :]), ALU.is_equal)
                    if q == 0:
                        c.step(nc.vector.scalar_tensor_tensor(out=rest[:, :, :], in0=onehot[:, 0, :, :], scalar=MASKED,
                                                              in1=logits[:, :, :], op0=ALU.mult, op1=ALU.add))
                nc.vector.tensor_tensor(chosen[:, :, :], onehot[:, 0, :, :], onehot[:, 1, :, :], ALU.add).then_inc(chosen_ready, 1)
                nc.vector.tensor_tensor(gap[:, :], best[:, 1, :], best[:, 0, :], ALU.subtract).then_inc(gap_ready, 1)

                dve.wait_ge(exp_ready, 1)
                ts(weight_sum[:, :], k.weights[:, 1, :], 1.0, None, ALU.add)
                c.step(nc.vector.reciprocal(k.weights[:, 0, :], weight_sum[:, :]))
                tt(k.weights[:, 1, :], k.weights[:, 1, :], k.weights[:, 0, :], ALU.mult)

                dve.wait_ge(counted, 2)
                c.step(nc.vector.tensor_copy(total[:, :, :], p_total[:, :, :]))
                c.step(nc.vector.tensor_copy(run[:, 0, :, :], total[:, :, :]))
                now, step = 0, 1
                while step < NT:
                    c.add(nc.vector.tensor_copy(run[:, 1 - now, 0:step, :], run[:, now, 0:step, :]))
                    tt(run[:, 1 - now, step:NT, :], run[:, now, step:NT, :], run[:, now, 0:NT - step, :], ALU.add)
                    now, step = 1 - now, 2 * step
                ts(ends[:, 0, :], run[:, now, NT - 1, :], float(ST - 1), None, ALU.add)
                c.step(nc.vector.tensor_copy(count_i[:, :], ends[:, 0, :]))
                ts(count_i[:, :], count_i[:, :], ST.bit_length() - 1, None, ALU.logical_shift_right)
                c.step(nc.vector.tensor_copy(ntile[:, :], count_i[:, :]))
                c.step(nc.vector.tensor_copy(ends[:, 0, :], ntile[:, :]))
                at_end, step = 0, 1
                while step < E1:
                    c.add(nc.vector.tensor_copy(ends[:, 1 - at_end, 0:step], ends[:, at_end, 0:step]))
                    tt(ends[:, 1 - at_end, step:E1], ends[:, at_end, step:E1], ends[:, at_end, 0:E1 - step], ALU.add)
                    at_end, step = 1 - at_end, 2 * step
                tt(start[:, :], ends[:, at_end, :], ntile[:, :], ALU.subtract)
                ts(start[:, :], start[:, :], float(ST), None, ALU.mult)
                tt(run[:, now, :, :], run[:, now, :, :], total[:, :, :], ALU.subtract)
                tt(run[:, now, :, :], run[:, now, :, :], p_rank[:, :, :], ALU.add)
                tt(run[:, now, :, :], run[:, now, :, :], start[:, :].unsqueeze(1).to_broadcast([P, NT, E1]), ALU.add)
                for q in range(2):
                    tt(same[:, :, :], onehot[:, q, :, :], run[:, now, :, :], ALU.mult)
                    c.step(nc.vector.tensor_reduce(out=slot[:, :], in_=same[:, :, :], op=ALU.add, axis=AX.X))
                    nc.vector.tensor_copy(k.slots[:, q, :], slot[:, :]).then_inc(slots_ready, 1)
                    dve.wait_ge(slots_ready, q + 1)
                tt(owner[:, :, :], tiles[:, :].unsqueeze(2).to_broadcast([P, NTILES, E1]),
                   ends[:, at_end, :].unsqueeze(1).to_broadcast([P, NTILES, E1]), ALU.is_ge)
                c.step(nc.vector.tensor_reduce(out=owner_f[:, :], in_=owner[:, :, :], op=ALU.add, axis=AX.X))
                ts(owner_f[:, :], owner_f[:, :], float(E1 - 1), None, ALU.min)
                c.step(nc.vector.tensor_copy(k.owners[:, :], owner_f[:, :]))

            @block.gpsimd
            def _(pool):
                for q in range(2):
                    pool.wait_ge(slots_ready, q + 1)
                    for t in range(NT):
                        pool.indirect_dma_start(out=k.x_slots[:, :],
                                                out_offset=bass.IndirectOffsetOnAxis(ap=k.slots[:, q, t:t + 1], axis=0),
                                                in_=xn_all[:, t, :], in_offset=None).then_inc(scattered, 16)
                pool.wait_ge(scattered, 16 * 2 * NT)


def routed_experts(nc, a, k):
    with ExitStack() as stack:
        m = Mem(nc, stack)
        raw1 = m.sb("f_raw1", [P, 2, 2 * KT, FF])
        raw2 = m.sb("f_raw2", [P, 2, FB, D])
        w1 = m.sb("f_w1", [P, 2, 2 * KT, FF], F32R)
        w2 = m.sb("f_w2", [P, 2, FB, D], F32R)
        b1 = m.sb("f_b1", [P, 2, 2 * FB])
        b2 = m.sb("f_b2", [P, 2, D])
        x = m.sb("f_x", [P, SPT, D])
        xT = m.sb("f_xT", [P, 2, 2, KT, ST], F32R)
        gate = m.sb("f_gate", [P, 2, ST])
        hidden = m.sb("f_hidden", [P, 2, 2, ST], F32R)
        y = m.sb("f_y", [P, SPT, D])
        p_up = m.ps("p_up", [P, 2, 2, ST])
        p_t = m.ps("f_pt", [P, KT, ST])
        p_y = m.ps("p_y", [P, SPT, D])
        x_loaded = m.sem("f_x_loaded")
        w1_loaded, w2_loaded, b_loaded = ([m.sem(f"f_{what}_loaded{n}") for n in range(2)] for what in ("w1", "w2", "b"))
        turned, xT_high, xT_ready = m.sem("f_turned"), m.sem("f_xT_high"), m.sem("f_xT_ready")
        w_high, w_ready = m.sem("f_w_high"), m.sem("f_w_ready")
        up_psum, down_psum = m.sem("f_up_psum"), m.sem("f_down_psum")
        gate_ready, hidden_raw = m.sem("f_gate_ready"), m.sem("f_hidden_raw")
        hidden_high, hidden_ready = m.sem("f_hidden_high"), m.sem("f_hidden_ready")
        y_ready, y_stored = m.sem("f_y_ready"), m.sem("f_y_stored")
        pieces = [(1, 0), (2, 0), (1, 1), (1, 2), (2, 1), (1, 3)]
        PIECES, AHEAD = len(pieces), 3
        F1P, F2P = 2, FB // 2
        TURN_AT, AHEAD_AT = 3, FB - AHEAD

        def piece(q, one, two):
            which, n = pieces[q]
            if which == 1:
                return one[:, :, n * F1P * P:(n + 1) * F1P * P]
            return two[:, n * F2P:(n + 1) * F2P, :]

        def piece_raw(q, par):
            return piece(q, raw1[:, par, :, :], raw2[:, par, :, :])

        def piece_part(q, part):
            return piece(q, w1[:, part, :, :], w2[:, part, :, :])

        def all_tiles(engine, tile):
            tile(0, 0, 0)
            tile(1, 1, 0)
            with engine.Fori(1, NTILES // 2) as i:
                tile(2 * i, 0, i)
                tile(2 * i + 1, 1, i)
            for t in range(NTILES // 2 * 2, NTILES):
                tile(t, t % 2, t // 2)

        def early(t):
            return isinstance(t, int) and t < 2

        def last_tile(t):
            return isinstance(t, int) and t == NTILES - 1

        with nc.Block() as block:
            @block.sync
            def _(sp):
                def load(t, par):
                    if not first(t):
                        sp.wait_ge(turned, t)
                    sp.dma_start(x[:, :, :], k.x_slots[at(t, ST, ST), :].rearrange("(u p) d -> p u d", p=P)
                                 ).then_inc(x_loaded, 16)
                    if not early(t):
                        sp.wait_ge(w_ready, PIECES * (t - 1))
                    e = sp.value_load(k.owners[0:1, at(t, 1, 1)], min_val=0, max_val=E1 - 1)
                    for ab, src in enumerate((a["W1a"], a["W1b"])):
                        sp.dma_start(raw1[:, par, ab * KT:(ab + 1) * KT, :],
                                     src[bass.ds(e, 1), :, :].rearrange("o (k p) f -> p (o k) f", p=P)
                                     ).then_inc(w1_loaded[par], 16)
                    sp.dma_start(raw2[:, par, :, :], a["W2"][bass.ds(e, 1), :, :].rearrange("o (k p) d -> p (o k) d", p=P)
                                 ).then_inc(w2_loaded[par], 16)
                    if not early(t):
                        sp.wait_ge(y_ready, t - 1)
                    sp.dma_start(b1[:, par, :], a["b1"][bass.ds(e, 1), :, :].rearrange("o p f -> (o p) f")
                                 ).then_inc(b_loaded[par], 16)
                    sp.dma_start(b2[:, par, :], a["b2"][bass.ds(e, 1), :].rearrange("o d -> (o d)").partition_broadcast(P)
                                 ).then_inc(b_loaded[par], 16)

                def store(t):
                    sp.wait_ge(y_ready, t + 1)
                    sp.dma_start(k.y_slots[at(t, ST, ST), :].rearrange("(u p) d -> p u d", p=P), y[:, :, :]
                                 ).then_inc(y_stored, 16)

                load(0, 0)
                load(1, 1)
                load(2, 0)
                store(0)
                with sp.Fori(1, NTILES // 2) as i:
                    load(2 * i + 1, 1)
                    store(2 * i - 1)
                    load(2 * i + 2, 0)
                    store(2 * i)
                store(NTILES - 2)
                store(NTILES - 1)
                sp.wait_ge(y_stored, 16 * NTILES)

            @block.tensor
            def _(pe):
                def turn(t):
                    pe.wait_ge(x_loaded, 16 * t + 16)
                    if not first(t):
                        pe.wait_ge(xT_ready, t)
                    for kt in range(KT):
                        for u in range(SPT):
                            last = nc.tensor.transpose(p_t[:, kt, u * P:(u + 1) * P], x[:, u, kt * P:(kt + 1) * P],
                                                       k.ident[:, :])
                    last.then_inc(turned, 1)

                def up(t, par, f):
                    if f % F1P == 0:
                        pe.wait_ge(w_ready, PIECES * t + pieces.index((1, f // F1P)) + 1)
                    if f >= 2 or not first(t):
                        pe.wait_ge(hidden_raw, FB * t + f - 1)
                    for ab in range(2):
                        for kt in range(KT):
                            for wh, xh in PRODUCTS:
                                last = nc.tensor.matmul(
                                    p_up[:, f % 2, ab, :],
                                    w1[:, wh, ab * KT + kt, f * P:(f + 1) * P], xT[:, par, xh, kt, :],
                                    start=(kt, wh, xh) == (0, HI, HI), stop=(kt, wh, xh) == (KT - 1, LO, HI))
                    last.then_inc(up_psum, 1)

                def down(t, par, f):
                    if f % F2P == 0:
                        pe.wait_ge(w_ready, PIECES * t + pieces.index((2, f // F2P)) + 1)
                    pe.wait_ge(hidden_ready, FB * t + f + 1)
                    if f == 0 and not first(t):
                        pe.wait_ge(y_ready, t)
                    for u in range(SPT):
                        for wh, hh in PRODUCTS:
                            last = nc.tensor.matmul(p_y[:, u, :], hidden[:, f % 2, hh, u * P:(u + 1) * P],
                                                    w2[:, wh, f, :],
                                                    start=(f, wh, hh) == (0, HI, HI) and u % 2 == 0,
                                                    stop=(f, wh, hh) == (FB - 1, LO, HI) and u % 2 == 1)
                    last.then_inc(down_psum, 1)

                def tile(t, par, turns):
                    pe.wait_ge(xT_ready, t + 1)
                    for f in range(FB):
                        up(t, par, f)
                        if f == TURN_AT and not last_tile(t):
                            turn(t + 1)
                        if f:
                            down(t, par, f - 1)
                        elif not first(t):
                            down(t - 1, 1 - par, FB - 1)

                turn(0)
                all_tiles(pe, tile)
                down(NTILES - 1, (NTILES - 1) % 2, FB - 1)

            @block.scalar
            def _(act):
                def round_x(t, par):
                    act.wait_ge(turned, t + 1)
                    nc.scalar.activation(xT[:, par, HI, :, :], p_t[:, :, :], ACT.Copy).then_inc(xT_high, 1)

                def round_weights(t, par, q, turns):
                    which, n = pieces[q]
                    if which == 1:
                        if n == 0:
                            act.wait_ge(w1_loaded[par], 16 * 2 * (turns + 1))
                        if not first(t):
                            act.wait_ge(up_psum, FB * (t - 1) + (n + 1) * F1P)
                    else:
                        if n == 0:
                            act.wait_ge(w2_loaded[par], 16 * (turns + 1))
                        if not first(t):
                            act.wait_ge(down_psum, FB * (t - 1) + (n + 1) * F2P)
                    nc.scalar.activation(piece_part(q, HI), piece_raw(q, par), ACT.Copy).then_inc(w_high, 1)

                def tile(t, par, turns):
                    act.wait_ge(b_loaded[par], 16 * 2 * (turns + 1))
                    for f in range(FB):
                        n = FB * t + f + 1
                        act.wait_ge(up_psum, n)
                        if f >= 2 or not first(t):
                            act.wait_ge(hidden_ready, n - 2)
                        nc.scalar.activation(gate[:, f % 2, :], p_up[:, f % 2, 0, :], ACT.Silu,
                                             bias=b1[:, par, f:f + 1]).then_inc(gate_ready, 1)
                        act.wait_ge(hidden_raw, n)
                        if f >= 2 or not first(t):
                            act.wait_ge(down_psum, n - 2)
                        nc.scalar.activation(hidden[:, f % 2, HI, :], gate[:, f % 2, :], ACT.Copy).then_inc(hidden_high, 1)
                        if f == TURN_AT and not last_tile(t):
                            round_x(t + 1, 1 - par)
                        if f < PIECES - AHEAD:
                            round_weights(t, par, AHEAD + f, turns)
                        if f >= AHEAD_AT and not last_tile(t):
                            round_weights(t + 1, 1 - par, f - AHEAD_AT, turns + (1 if par else 0))

                round_x(0, 0)
                for q in range(AHEAD):
                    round_weights(0, 0, q, 0)
                all_tiles(act, tile)

            @block.vector
            def _(dve):
                def rest_of_x(t, par):
                    dve.wait_ge(xT_high, t + 1)
                    nc.vector.tensor_tensor(xT[:, par, LO, :, :], p_t[:, :, :], xT[:, par, HI, :, :],
                                            ALU.subtract).then_inc(xT_ready, 1)

                def hide(t, par, f):
                    n = FB * t + f + 1
                    dve.wait_ge(gate_ready, n)
                    nc.vector.scalar_tensor_tensor(out=gate[:, f % 2, :], in0=p_up[:, f % 2, 1, :],
                                                   scalar=b1[:, par, FB + f:FB + f + 1], in1=gate[:, f % 2, :],
                                                   op0=ALU.add, op1=ALU.mult).then_inc(hidden_raw, 1)
                    dve.wait_ge(hidden_high, n)
                    nc.vector.tensor_tensor(hidden[:, f % 2, LO, :], gate[:, f % 2, :], hidden[:, f % 2, HI, :],
                                            ALU.subtract).then_inc(hidden_ready, 1)

                def take_y(t, par):
                    dve.wait_ge(down_psum, FB * t + FB)
                    if not first(t):
                        dve.wait_ge(y_stored, 16 * t)
                    nc.vector.tensor_tensor(y[:, :, :], p_y[:, :, :],
                                            b2[:, par, :].unsqueeze(1).to_broadcast([P, SPT, D]), ALU.add).then_inc(y_ready, 1)

                def tile(t, par, turns):
                    for f in range(FB):
                        hide(t, par, f)
                        if f == 0 and not first(t):
                            take_y(t - 1, 1 - par)
                        if f == TURN_AT and not last_tile(t):
                            rest_of_x(t + 1, 1 - par)

                rest_of_x(0, 0)
                all_tiles(dve, tile)
                take_y(NTILES - 1, (NTILES - 1) % 2)

            @block.gpsimd
            def _(pool):
                def tile(t, par, turns):
                    for q in range(PIECES):
                        pool.wait_ge(w_high, PIECES * t + q + 1)
                        nc.gpsimd.tensor_tensor(piece_part(q, LO), piece_raw(q, par), piece_part(q, HI),
                                                ALU.subtract).then_inc(w_ready, 1)

                all_tiles(pool, tile)


def combine(nc, a, k, out):
    with ExitStack() as stack:
        m = Mem(nc, stack)
        ys = m.sb("g_ys", [P, 2, 2, TPC, D])
        res = m.sb("g_res", [P, 2, TPC, D])
        gathered = [m.sem(f"g_gathered{n}") for n in range(2)]
        stored = [m.sem(f"g_stored{n}") for n in range(2)]
        done, own = m.sem("g_done"), m.sem("g_own")
        OWN = 2 * TPC + 1
        with nc.Block() as block:
            @block.gpsimd
            def _(pool):
                for i in range(NCH):
                    if i >= 2:
                        pool.wait_ge(done, i - 1)
                    for u in range(TPC):
                        for q in range(2):
                            t = i * TPC + u
                            pool.indirect_dma_start(out=ys[:, i % 2, q, u, :], out_offset=None, in_=k.y_slots[:, :],
                                                    in_offset=bass.IndirectOffsetOnAxis(ap=k.slots[:, q, t:t + 1], axis=0),
                                                    ).then_inc(gathered[i % 2], 16)

            @block.vector
            def _(dve):
                def chunk(i, par, turns, early):
                    c = Count(dve, own, OWN * i)
                    dve.wait_ge(gathered[par], 16 * 2 * TPC * (turns + 1))
                    if not early:
                        dve.wait_ge(stored[par], 16 * turns)
                    for u in range(TPC):
                        c.add(nc.vector.tensor_scalar(res[:, par, u, :], ys[:, par, 0, u, :],
                                                      k.weights[:, 0, at(i * TPC + u, 1, 1)], None, ALU.mult))
                    c.wait()
                    for u in range(TPC):
                        c.add(nc.vector.scalar_tensor_tensor(out=res[:, par, u, :], in0=ys[:, par, 1, u, :],
                                                             scalar=k.weights[:, 1, at(i * TPC + u, 1, 1)],
                                                             in1=res[:, par, u, :], op0=ALU.mult, op1=ALU.add))
                    c.wait()
                    c.step(nc.vector.tensor_tensor(res[:, par, :, :], res[:, par, :, :], k.mod(1, i // CPS, GB), ALU.mult))
                    nc.vector.tensor_tensor(res[:, par, :, :], res[:, par, :, :], k.x[:, at(i, TPC, TPC), :],
                                            ALU.add).then_inc(done, 1)
                    assert c.n == OWN

                chunk(0, 0, 0, True)
                chunk(1, 1, 0, True)
                with dve.Fori(1, NCH // 2) as i:
                    chunk(2 * i, 0, i, False)
                    chunk(2 * i + 1, 1, i, False)

            @block.sync
            def _(sp):
                with sp.Fori(0, NCH // 2) as i:
                    for par in range(2):
                        sp.wait_ge(done, 2 * i + par + 1)
                        sp.dma_start(out[at(2 * i + par, CH, CH), :].rearrange("(u p) d -> p u d", p=P),
                                     res[:, par, :, :]).then_inc(stored[par], 16)
                for par in range(2):
                    sp.wait_ge(stored[par], 16 * (NCH // 2))


class Kept:

    def __init__(self, nc, m):
        self.ident = m.sb("ident", [P, P])
        self.identb = m.sb("identb", [P, P], BF16)
        self.masks = m.sb("masks", [P, 2, P], BF16)
        self.mods = [None, m.sb("mods1", [P, B, 6, D])]
        self.stats = m.sb("stats", [P, NT, 6])
        self.mean, self.ve, self.rstd = m.sb("mean", [P, NT]), m.sb("ve", [P, NT]), m.sb("rstd", [P, NT])
        self.spread, self.neghalf = m.sb("spread", [P, NT]), m.sb("neghalf", [P, NT])
        self.x = m.sb("x", [P, NT, D])
        self.constants_loaded = m.sem("constants_loaded")
        self.power_set, self.ve_ready, self.rstd_ready = m.sem("power_set"), m.sem("ve_ready"), m.sem("rstd_ready")
        self.scaled, self.x2_ready = m.sem("c_scaled"), m.sem("c_x2_ready")

        self.weights = m.sb("weights", [P, 2, NT])
        self.slots = m.sb("slots", [P, 2, NT], U32)
        self.owners = m.sb("owners", [P, NTILES], I32)

        def dram(name, shape, dt=F32):
            return nc.dram_tensor(name, shape, dt, kind="Internal").ap()

        self.qk_rows = dram("qk_scr", [2 * SPLIT * B * D, T], BF16)
        self.v_scr = dram("v_scr", [NS, P, JT, HG * VW])
        self.x_slots, self.y_slots = dram("x_slots", [NSLOT, D]), dram("y_slots", [NSLOT, D])
        self.max_scr = dram("max_scr", [2, SPLIT * HG, CH], BF16)
        self.qk_scr = {(qk, part): self.qk_rows[(qk * SPLIT + part) * B * D:(qk * SPLIT + part + 1) * B * D, :]
                       for qk in range(2) for part in range(SPLIT)}

    def mod(self, layer, b, which):
        return self.mods[layer][:, at(b, 1, 1), which, :].to_broadcast([P, TPC, D])

    def mod1(self, layer, b, which):
        return self.mods[layer][:, at(b, 1, 1), which, :].rearrange("p o d -> p (o d)")


def program(nc, a, out):
    with ExitStack() as stack:
        m = Mem(nc, stack)
        k = Kept(nc, m)
        with ExitStack() as block0:
            k.mods[0] = Mem(nc, block0).sb("mods0", [P, B, 6, D])
            modulation(nc, a, k)
            projections(nc, a, k)
            attention(nc, a, k)
            output_projection(nc, a, k)
            top1_experts(nc, a, k)
        with ExitStack() as mixing:
            mm = Mem(nc, mixing)
            h_all = mm.sb("h_all", [P, NT, D])
            xnT_all = mm.sb("xnT_all", [P, KT, NTOK])
            second_norm(nc, a, k, 2, "n1_", SA, CA, h_all, None, xnT_all, None, None)
            mix(nc, a, k, h_all, xnT_all)
        with ExitStack() as routing:
            mm = Mem(nc, routing)
            xn_all = mm.sb("xn_all", [P, NT, D])
            logits = mm.sb("logits", [P, NT, E1])
            second_norm(nc, a, k, 3, "n2_", SB_, CB, None, xn_all, None, a["ln_w"], logits)
            route(nc, a, k, logits, xn_all)
        routed_experts(nc, a, k)
        combine(nc, a, k, out)


def lay_out(inputs):
    g = {n: np.asarray(v) for n, v in inputs.items()}
    swap = np.arange(D) ^ 1
    a = {"x": g["L0_attn_X"].reshape(NTOK, D)}
    for n in range(2):
        a[f"cT{n}"] = g[f"L{n}_c"].T.reshape(KT, P, B).transpose(1, 0, 2)
        a[f"wmod{n}"] = g[f"L{n}_wmod"]
    wq, wk, wv = (g[f"L0_attn_W_{c}"] for c in "qkv")
    a["wqkv"] = np.concatenate([wq.T, wq[swap].T, wk.T, wk[swap].T, wv.T], axis=1)
    a["woT"] = g["L0_attn_W_o"].T
    a["expertT"] = g["L0_ffn_expert_w"].transpose(2, 0, 1).reshape(D, E0 * D)
    a["gateT"] = g["L0_ffn_gate_w"].T
    a["iota8"] = np.tile(np.arange(E0, dtype=np.float32) - E0, (P, 1))
    a["w_uv"] = np.concatenate([g["L1_attn_u_w"].T, g["L1_attn_v_w"].T], axis=1)
    a["b_uv"] = np.concatenate([g["L1_attn_u_b"], g["L1_attn_v_b"]]).reshape(2 * FB1, P).T
    a["o_wT"] = g["L1_attn_o_w"].T
    a["o_b"] = g["L1_attn_o_b"]
    heads = np.stack([g["L1_attn_zero"][:, 0], g["L1_attn_pos"][:, 0], g["L1_attn_neg"][:, 0]])
    a["toep"] = np.repeat(heads, F1 // heads.shape[1], axis=1).reshape(3, FB1, P).transpose(2, 0, 1)
    a["ln_w"], a["Wg"], a["bg"] = g["L1_ffn_ln_w"], g["L1_ffn_Wg"], g["L1_ffn_bg"]
    a["W1a"], a["W1b"], a["W2"], a["b2"] = g["L1_ffn_W1a"], g["L1_ffn_W1b"], g["L1_ffn_W2"], g["L1_ffn_b2"]
    b1 = np.concatenate([g["L1_ffn_b1a"], g["L1_ffn_b1b"]], axis=1)
    a["b1"] = b1.reshape(E1, 2 * FB, P).transpose(0, 2, 1)
    a["before"] = np.triu(np.ones((P, P), np.float32), 1)
    a["ones"] = np.ones((P, P), np.float32)
    a["iota_tiles"] = np.tile(np.arange(NTILES, dtype=np.float32), (P, 1))
    theta = np.power(np.float32(10000.0), np.float32(-2.0) * np.arange(DH // 2, dtype=np.float32) / np.float32(DH))
    angle = (np.arange(T, dtype=np.float32)[:, None] * theta[None, :]).T.repeat(2, axis=0)
    sign = np.where(np.arange(DH) % 2 == 0, -1, 1).astype(np.float32)[:, None]
    a["trig"] = np.stack([np.tile(np.cos(angle), (P // DH, 1)), np.tile(sign * np.sin(angle), (P // DH, 1))], axis=1)
    a["ident"] = np.eye(P, dtype=np.float32)
    later = np.triu(np.full((P, P), MASKED, np.float32), 1)
    a["masks"] = np.stack([later, later.T], axis=1)
    return {n: np.ascontiguousarray(v) for n, v in a.items()}


def kernel(**inputs):
    import concourse.bacc as bacc
    from concourse.bass_utils import run_bass_kernel_spmd

    nc = bacc.Bacc("TRN2", target_bir_lowering=False, num_devices=1)
    arrays = lay_out(inputs)
    a = {n: nc.dram_tensor(f"in_{n}", v.shape, mybir.dt.from_np(v.dtype), kind="ExternalInput").ap()
         for n, v in arrays.items()}
    out = nc.dram_tensor("out", [NTOK, D], F32, kind="ExternalOutput").ap()
    program(nc, a, out)
    r = run_bass_kernel_spmd(nc, [{f"in_{n}": v for n, v in arrays.items()}], core_ids=[0])
    return r.results[0]["out"].reshape(B, T, D)
```

```python
from contextlib import ExitStack

import numpy as np
import concourse.bass as bass
from concourse import mybir

F32 = mybir.dt.float32
BF16 = mybir.dt.bfloat16
I32 = mybir.dt.int32
U32 = mybir.dt.uint32
F32R = mybir.dt.float32r
ACT = mybir.ActivationFunctionType
ALU = mybir.AluOpType
AX = mybir.AxisListType

B, T, D = 2, 2048, 256
NTOK = B * T
P = 128
KT = D // P
CH = 512
TPC = CH // P
NCH = NTOK // CH
CPS = T // CH
NT = NTOK // P
H0, DH = 16, 16
HG = 4
NS = B * H0 // HG
JT = T // P
VW = 32
SPLIT = 3
Q_PARTS = (0, 0, 1, 1, 0, 2)
K_PARTS = (0, 1, 0, 1, 2, 0)
QROWS = DH * len(Q_PARTS)
EPS = 1e-5
MASKED = -1e30
E0 = 8
F1 = 512
FB1 = F1 // P
E1, FF = 8, 1024
FB = FF // P
ST = 512
SPT = ST // P
NTILES = E1 + (2 * NTOK - E1) // ST
NSLOT = NTILES * ST
ZW = SPT * D

HI, LO = 0, 1
PRODUCTS = ((HI, HI), (HI, LO), (LO, HI))


class Count:

    def __init__(self, engine, sem, start=0):
        self.engine, self.sem, self.start, self.n = engine, sem, start, 0

    def add(self, instruction):
        instruction.then_inc(self.sem, 1)
        self.n += 1

    def wait(self):
        self.engine.wait_ge(self.sem, self.start + self.n)

    def step(self, instruction):
        self.add(instruction)
        self.wait()


def first(i):
    return isinstance(i, int) and i == 0


def at(i, step, n):
    return slice(i * step, i * step + n) if isinstance(i, int) else bass.ds(i * step, n)


class Mem:
    def __init__(self, nc, stack):
        self.nc, self.stack = nc, stack

    def sb(self, name, shape, dt=F32):
        return self.stack.enter_context(self.nc.sbuf_tensor(name, shape, dt))

    def ps(self, name, shape, dt=F32):
        return self.stack.enter_context(self.nc.psum_tensor(name, shape, dt))

    def sem(self, name):
        return self.nc.alloc_semaphore(name)


SA, CA, GA, SB_, CB, GB = range(6)


def modulation(nc, a, k):
    with ExitStack() as stack:
        m = Mem(nc, stack)
        wm = m.sb("wm", [P, 2, KT, 6 * D])
        cT = m.sb("cT", [P, 2, KT, B])
        silu_c = m.sb("silu_c", [P, 2, KT, B])
        ones = m.sb("mod_ones", [P, P])
        cb = m.sb("cb", [P, 2, KT, B, P])
        masks = m.sb("masks_f32", [P, 2, P])
        pm = m.ps("pmod", [P, 2, 2 * D])
        loaded = k.constants_loaded
        c_ready, cb_ready, ones_set = m.sem("silu_c_ready"), m.sem("cb_ready"), m.sem("mod_ones_set")
        product, copied, own = m.sem("mod_product"), m.sem("mod_copied"), m.sem("mod_own")
        x_loaded = [m.sem(f"x_loaded{b}") for b in range(B)]
        LOADS = 6
        with nc.Block() as block:
            @block.gpsimd
            def _(pool):
                for b in range(B):
                    pool.dma_start(k.x[:, b * JT:(b + 1) * JT, :],
                                   a["x"][b * T:(b + 1) * T, :].rearrange("(t p) d -> p t d", p=P)).then_inc(x_loaded[b], 16)

            @block.sync
            def _(sp):
                sp.dma_start(cT[:, 0, :, :], a["cT0"]).then_inc(loaded, 16)
                sp.dma_start(cT[:, 1, :, :], a["cT1"]).then_inc(loaded, 16)
                for layer, name in enumerate(("wmod0", "wmod1")):
                    sp.dma_start(wm[:, layer, :, :], a[name].rearrange("(k p) n -> p k n", p=P)).then_inc(loaded, 16)
                sp.dma_start(k.ident[:, :], a["ident"]).then_inc(loaded, 16)
                sp.dma_start(masks[:, :, :], a["masks"]).then_inc(loaded, 16)
                sp.wait_ge(loaded, 16 * LOADS)

            @block.scalar
            def _(act):
                act.wait_ge(loaded, 16 * LOADS)
                nc.scalar.activation(silu_c[:, :, :, :], cT[:, :, :, :], ACT.Silu).then_inc(c_ready, 1)
                n = 0
                for layer in range(2):
                    for b in range(B):
                        for half in range(3):
                            act.wait_ge(product, n + 1)
                            nc.scalar.activation(
                                k.mods[layer][:, b, 2 * half:2 * half + 2, :],
                                pm[:, n % 2, :].rearrange("p (s d) -> p s d", s=2), ACT.Copy).then_inc(copied, 1)
                            n += 1

            @block.tensor
            def _(pe):
                pe.wait_ge(cb_ready, 2 * KT * B)
                n = 0
                for layer in range(2):
                    for b in range(B):
                        for half in range(3):
                            if n >= 2:
                                pe.wait_ge(copied, n - 1)
                            for kt in range(KT):
                                last = nc.tensor.matmul(
                                    pm[:, n % 2, :], cb[:, layer, kt, b, :],
                                    wm[:, layer, kt, 2 * half * D:(2 * half + 2) * D],
                                    start=kt == 0, stop=kt == KT - 1)
                            last.then_inc(product, 1)
                            n += 1

            @block.vector
            def _(dve):
                nc.vector.memset(ones[:, :], 1.0).then_inc(ones_set, 1)
                dve.wait_ge(ones_set, 1)
                dve.wait_ge(c_ready, 1)
                for layer in range(2):
                    for kt in range(KT):
                        for b in range(B):
                            nc.vector.tensor_scalar(cb[:, layer, kt, b, :], ones[:, :],
                                                    silu_c[:, layer, kt, b:b + 1], None, ALU.mult).then_inc(cb_ready, 1)
                for b in range(B):
                    dve.wait_ge(x_loaded[b], 16)
                    with dve.Fori(b * JT, (b + 1) * JT) as t:
                        nc.vector.bn_stats(out=k.stats[:, at(t, 1, 1), :].rearrange("p o s -> p (o s)"),
                                           in_=k.x[:, at(t, 1, 1), :].rearrange("p o d -> p (o d)"))
                dve.wait_ge(loaded, 16 * LOADS)
                own_n = Count(dve, own)
                own_n.add(nc.vector.tensor_copy(k.identb[:, :], k.ident[:, :]))
                own_n.add(nc.vector.tensor_copy(k.masks[:, :, :], masks[:, :, :]))
                dve.wait_ge(copied, 6 * B)
                for mods in k.mods:
                    for which in (CA, CB):
                        own_n.add(nc.vector.tensor_scalar(mods[:, :, which, :], mods[:, :, which, :], 1.0, None, ALU.add))


def guard_gates(nc, k, own, sign, mag):
    for mods in k.mods:
        for which in (GA, GB):
            gate = mods[:, :, which, :]
            own.wait()
            own.add(nc.vector.tensor_scalar(sign, gate, 0.0, 2.0, ALU.is_ge, ALU.mult))
            own.step(nc.vector.scalar_tensor_tensor(out=mag, in0=gate, scalar=-1.0, in1=gate,
                                                    op0=ALU.mult, op1=ALU.max))
            own.step(nc.vector.tensor_scalar(mag, mag, 0.25, None, ALU.max))
            own.step(nc.vector.scalar_tensor_tensor(out=gate, in0=sign, scalar=-1.0, in1=mag,
                                                    op0=ALU.add, op1=ALU.mult))


NORM_STEPS = TPC + 1
AGGREGATE_STEPS = 6


def aggregate(nc, own, k):
    (mean_e, m2_e), (mean_o, m2_o) = ((k.stats[:, :, i], k.stats[:, :, i + 1]) for i in (1, 4))
    own.add(nc.vector.tensor_tensor(k.mean[:, :], mean_e, mean_o, ALU.add))
    own.add(nc.vector.tensor_tensor(k.spread[:, :], mean_e, mean_o, ALU.subtract))
    own.step(nc.vector.tensor_tensor(k.ve[:, :], m2_e, m2_o, ALU.add))
    own.add(nc.vector.tensor_scalar(k.mean[:, :], k.mean[:, :], 0.5, None, ALU.mult))
    own.add(nc.vector.tensor_scalar(k.ve[:, :], k.ve[:, :], 1.0 / D, EPS, ALU.mult, ALU.add))
    own.step(nc.vector.scalar_tensor_tensor(out=k.spread[:, :], in0=k.spread[:, :], scalar=0.25, in1=k.spread[:, :],
                                            op0=ALU.mult, op1=ALU.mult))
    assert own.n == AGGREGATE_STEPS
    return nc.vector.tensor_tensor(k.ve[:, :], k.ve[:, :], k.spread[:, :], ALU.add)


def row_stats(nc, k, i):
    for u in range(TPC):
        t = at(i * TPC + u, 1, 1)
        nc.vector.bn_stats(out=k.stats[:, t, :].rearrange("p o s -> p (o s)"),
                           in_=k.x[:, t, :].rearrange("p o d -> p (o d)"))


def root(nc, pool, k, norm):
    if norm == 0:
        nc.gpsimd.memset(k.neghalf[:, :], -0.5).then_inc(k.power_set, 1)
        pool.wait_ge(k.power_set, 1)
    pool.wait_ge(k.ve_ready, norm + 1)
    nc.gpsimd.tensor_tensor(k.rstd[:, :], k.ve[:, :], k.neghalf[:, :], ALU.pow).then_inc(k.rstd_ready, 1)


def normalize(nc, k, own, i, h, scale, shift, done):
    for u in range(TPC):
        own.add(nc.vector.tensor_scalar(h[:, u, :], k.x[:, at(i * TPC + u, 1, 1), :].rearrange("p o d -> p (o d)"),
                                        k.mean[:, at(i * TPC + u, 1, 1)], k.rstd[:, at(i * TPC + u, 1, 1)],
                                        ALU.subtract, ALU.mult))
    own.wait()
    own.step(nc.vector.tensor_tensor(h, h, scale, ALU.mult))
    nc.vector.tensor_tensor(h, h, shift, ALU.add).then_inc(done, 1)


def projections(nc, a, k):
    with ExitStack() as stack:
        m = Mem(nc, stack)
        raw = m.sb("wqkv_raw", [P, KT, 5 * D])
        w = m.sb("wqkv", [P, 2, KT, 5 * D], F32R)
        trig = m.sb("trig", [P, 2, T])
        h = m.sb("h", [P, TPC, D])
        hT = m.sb("hT", [P, 2, 2, KT, CH], F32R)
        rot = m.sb("rot", [P, 2, 2, KT, CH])
        rem = m.sb("rem", [P, 2, KT, CH])
        parts = m.sb("parts", [P, 2, SPLIT, KT, CH], BF16)
        va = m.sb("va", [P, TPC, H0, VW])
        p_t = m.ps("p_t", [P, KT, CH])
        p_qk = m.ps("p_qk", [P, 2, KT, CH])
        p_v = m.ps("p_v", [P, TPC, D])
        w_loaded, trig_loaded = m.sem("w_loaded"), m.sem("trig_loaded")
        w_high, w_ready = m.sem("a_w_high"), m.sem("a_w_ready")
        h_ready, turned, hT_high, hT_ready = m.sem("a_h_ready"), m.sem("a_turned"), m.sem("a_hT_high"), m.sem("a_hT_ready")
        qk_psum, v_psum = m.sem("a_qk_psum"), m.sem("a_v_psum")
        qk_taken, rot_ready = m.sem("a_qk_taken"), m.sem("a_rot_ready")
        rounded, rem_ready, last_part = m.sem("a_rounded"), m.sem("a_rem_ready"), m.sem("a_last_part")
        va_ready, va_stored = m.sem("a_va_ready"), m.sem("a_va_stored")
        parts_stored = [m.sem(f"a_parts_stored{qk}") for qk in range(2)]
        own, ones_set = m.sem("a_own"), m.sem("a_ones_set")
        NHG = H0 // HG
        columns = [slice(0, 2 * D), slice(2 * D, 4 * D), slice(4 * D, 5 * D)]

        def all_chunks(engine, chunk):
            chunk(0, 0)
            chunk(1, 1)
            with engine.Fori(1, NCH // 2 - 1) as i:
                chunk(2 * i, 0)
                chunk(2 * i + 1, 1)
            chunk(NCH - 2, 0)
            chunk(NCH - 1, 1)

        def last_chunk(i):
            return isinstance(i, int) and i == NCH - 1

        with nc.Block() as block:
            @block.sync
            def _(sp):
                def store(i):
                    b = i // CPS
                    c = i % CPS
                    sp.wait_ge(va_ready, i + 1)
                    for hg in range(NHG):
                        sp.dma_start(
                            k.v_scr[at(b * NHG + hg, 1, 1), :, at(c, TPC, TPC), :].rearrange("s p u n -> (s p) u n"),
                            va[:, :, HG * hg:HG * hg + HG, :].rearrange("p u h n -> p u (h n)")).then_inc(va_stored, 16)
                    for qk in range(2):
                        sp.wait_ge(last_part, 2 * i + qk + 1)
                        for part in range(SPLIT):
                            sp.dma_start(
                                k.qk_scr[qk, part][at(b, D, D), at(c, CH, CH)].rearrange("(k p) t -> p k t", p=P),
                                parts[:, qk, part, :, :]).then_inc(parts_stored[qk], 16)

                sp.dma_start(raw[:, :, :], a["wqkv"].rearrange("(k p) n -> p k n", p=P)).then_inc(w_loaded, 16)
                sp.dma_start(trig[:, :, :], a["trig"]).then_inc(trig_loaded, 16)
                with sp.Fori(0, NCH) as i:
                    store(i)
                for qk in range(2):
                    sp.wait_ge(parts_stored[qk], 16 * SPLIT * NCH)
                sp.wait_ge(va_stored, 16 * NHG * NCH)

            @block.gpsimd
            def _(pool):
                def add(i, qk):
                    pool.wait_ge(qk_taken, 4 * i + 2 * qk + 2)
                    if not first(i):
                        pool.wait_ge(last_part, 2 * i + qk - 1)
                    nc.gpsimd.tensor_tensor(rem[:, qk, :, :], rot[:, qk, 0, :, :], rot[:, qk, 1, :, :],
                                            ALU.add).then_inc(rot_ready, 1)

                def split_off(i, qk):
                    pool.wait_ge(rounded, 4 * i + 2 * qk + 2)
                    nc.gpsimd.tensor_tensor(parts[:, qk, 2, :, :], rem[:, qk, :, :], parts[:, qk, 1, :, :],
                                            ALU.subtract).then_inc(last_part, 1)

                def chunk(i, par):
                    for qk in range(2):
                        add(i, qk)
                        split_off(i, qk)

                root(nc, pool, k, 0)
                for n, cols in enumerate(columns):
                    pool.wait_ge(w_high, n + 1)
                    nc.gpsimd.tensor_tensor(w[:, LO, :, cols], raw[:, :, cols], w[:, HI, :, cols], ALU.subtract
                                            ).then_inc(w_ready, 1)
                all_chunks(pool, chunk)

            @block.vector
            def _(dve):
                nc.vector.memset(va[:, :, :, :], 1.0).then_inc(ones_set, 1)

                def norm(i):
                    c = Count(dve, own, AGGREGATE_STEPS + NORM_STEPS * i)
                    if not first(i):
                        dve.wait_ge(turned, i)
                    normalize(nc, k, c, i, h[:, :, :], k.mod(0, i // CPS, CA), k.mod(0, i // CPS, SA), h_ready)
                    assert c.n == NORM_STEPS

                def rest_of_hT(i, par):
                    dve.wait_ge(hT_high, i + 1)
                    nc.vector.tensor_tensor(hT[:, par, LO, :, :], p_t[:, :, :], hT[:, par, HI, :, :],
                                            ALU.subtract).then_inc(hT_ready, 1)

                def rotate(i, qk):
                    for s in range(2):
                        dve.wait_ge(qk_psum, 4 * i + 2 * qk + s + 1)
                        table = trig[:, s, at(i % CPS, CH, CH)]
                        nc.vector.tensor_tensor(rot[:, qk, s, :, :], p_qk[:, s, :, :],
                                                table.unsqueeze(1).to_broadcast([P, KT, CH]),
                                                ALU.mult).then_inc(qk_taken, 1)

                def split(i, qk):
                    dve.wait_ge(rounded, 4 * i + 2 * qk + 1)
                    nc.vector.tensor_tensor(rem[:, qk, :, :], rem[:, qk, :, :], parts[:, qk, 0, :, :],
                                            ALU.subtract).then_inc(rem_ready, 1)

                def chunk(i, par):
                    if not last_chunk(i):
                        norm(i + 1)
                    if first(i):
                        dve.wait_ge(trig_loaded, 16)
                    else:
                        split(i - 1, 1)
                    rotate(i, 0)
                    if not last_chunk(i):
                        rest_of_hT(i + 1, 1 - par)
                    split(i, 0)
                    rotate(i, 1)

                aggregate(nc, Count(dve, own), k).then_inc(k.ve_ready, 1)
                dve.wait_ge(k.rstd_ready, 1)
                norm(0)
                rest_of_hT(0, 0)
                all_chunks(dve, chunk)
                split(NCH - 1, 1)

            @block.scalar
            def _(act):
                def round_hT(i, par):
                    act.wait_ge(turned, i + 1)
                    nc.scalar.activation(hT[:, par, HI, :, :], p_t[:, :, :], ACT.Copy).then_inc(hT_high, 1)

                def take_v(i):
                    act.wait_ge(v_psum, i + 1)
                    if first(i):
                        act.wait_ge(ones_set, 1)
                    else:
                        act.wait_ge(va_stored, 16 * NHG * i)
                    nc.scalar.activation(va[:, :, :, 0:DH], p_v[:, :, :].rearrange("p u (h d) -> p u h d", d=DH),
                                         ACT.Copy).then_inc(va_ready, 1)

                def split(i, qk):
                    act.wait_ge(rot_ready, 2 * i + qk + 1)
                    if not first(i):
                        act.wait_ge(parts_stored[qk], 16 * SPLIT * i)
                    nc.scalar.activation(parts[:, qk, 0, :, :], rem[:, qk, :, :], ACT.Copy).then_inc(rounded, 1)
                    act.wait_ge(rem_ready, 2 * i + qk + 1)
                    nc.scalar.activation(parts[:, qk, 1, :, :], rem[:, qk, :, :], ACT.Copy).then_inc(rounded, 1)

                def chunk(i, par):
                    if not last_chunk(i):
                        round_hT(i + 1, 1 - par)
                    take_v(i)
                    split(i, 0)
                    split(i, 1)

                act.wait_ge(w_loaded, 16)
                for cols in columns:
                    nc.scalar.activation(w[:, HI, :, cols], raw[:, :, cols], ACT.Copy).then_inc(w_high, 1)
                round_hT(0, 0)
                all_chunks(act, chunk)

            @block.tensor
            def _(pe):
                def turn(i):
                    pe.wait_ge(h_ready, i + 1)
                    if not first(i):
                        pe.wait_ge(hT_ready, i)
                    for kt in range(KT):
                        for u in range(TPC):
                            last = nc.tensor.transpose(p_t[:, kt, u * P:(u + 1) * P], h[:, u, kt * P:(kt + 1) * P],
                                                       k.ident[:, :])
                    last.then_inc(turned, 1)

                def product(i, par, qk):
                    for s in range(2):
                        if not (first(i) and qk == 0):
                            pe.wait_ge(qk_taken, 4 * i + 2 * qk + s - 1)
                        for mb in range(KT):
                            for kt in range(KT):
                                col = (2 * qk + s) * D + mb * P
                                for wp, hp in PRODUCTS:
                                    last = nc.tensor.matmul(p_qk[:, s, mb, :], w[:, wp, kt, col:col + P], hT[:, par, hp, kt, :],
                                                            start=(kt, wp, hp) == (0, HI, HI),
                                                            stop=(kt, wp, hp) == (KT - 1, LO, HI))
                        last.then_inc(qk_psum, 1)

                def chunk(i, par):
                    pe.wait_ge(hT_ready, i + 1)
                    if first(i):
                        pe.wait_ge(w_ready, 3)
                    product(i, par, 0)
                    if not first(i):
                        pe.wait_ge(va_ready, i)
                    for u in range(TPC):
                        for kt in range(KT):
                            for wp, hp in PRODUCTS:
                                last = nc.tensor.matmul(p_v[:, u, :], hT[:, par, hp, kt, u * P:(u + 1) * P],
                                                        w[:, wp, kt, 4 * D:5 * D],
                                                        start=(kt, wp, hp) == (0, HI, HI),
                                                        stop=(kt, wp, hp) == (KT - 1, LO, HI))
                    last.then_inc(v_psum, 1)
                    if not last_chunk(i):
                        turn(i + 1)
                    product(i, par, 1)

                turn(0)
                all_chunks(pe, chunk)


UNITS = sum(TPC * (c + 1) for c in range(CPS))
NBUF = 3


def attention(nc, a, k):
    with ExitStack() as stack:
        m = Mem(nc, stack)
        qa = m.sb("qa", [P, NBUF, HG, T], BF16)
        ka = m.sb("ka", [P, NBUF, HG, T], BF16)
        va = m.sb("va3", [P, NBUF, JT, HG * VW])
        probs = m.sb("probs", [P, 2, HG, CH])
        tile_max = m.sb("tile_max", [P, HG, TPC, CPS])
        row_max = m.sb("row_max", [P, HG, TPC])
        max_rest = m.sb("max_rest", [P, HG, TPC])
        max_parts = m.sb("max_parts", [P, TPC, SPLIT, HG], BF16)
        max_rows = m.sb("max_rows", [SPLIT * HG, 2, CH], BF16)
        o_sb = m.sb("o_sb", [P, 2, CH])
        recip = m.sb("recip", [P, TPC, HG])
        p_s = m.ps("p_s", [P, 2, CH])
        p_m = m.ps("p_m", [P, 2, 2, CH])
        p_o = m.ps("p_o", [P, CH])
        p_misc = m.ps("p_misc", [P, CH])
        stage_loaded, stage0_loaded = [m.sem(f"stage_loaded{n}") for n in range(NBUF)], m.sem("stage0_loaded")
        stage0_rest_loaded = m.sem("stage0_rest_loaded")
        scores_ready, probs_ready, probs_used = m.sem("scores_ready"), m.sem("probs_ready"), m.sem("probs_used")
        max_scores, max_taken = m.sem("max_scores"), m.sem("max_taken")
        max_parts_ready, max_turned, max_rows_ready = m.sem("max_parts_ready"), m.sem("max_turned"), m.sem("max_rows_ready")
        max_stored, max_placed = m.sem("max_stored"), m.sem("max_placed")
        o_taken, o_turned, att_ready = m.sem("o_taken"), m.sem("o_turned"), m.sem("att_ready")
        ones_set, own, recip_ready = m.sem("ones_set"), m.sem("b_own"), m.sem("recip_ready")
        sign, mag = (probs[:, 0, n, :].rearrange("p (b d) -> p b d", b=B) for n in range(2))
        gates_own = m.sem("b_gates_own")
        zeros, zeros_set, slots_zeroed = m.sb("zeros", [P, ZW]), m.sem("zeros_set"), m.sem("slots_zeroed")
        LOADS = 2 * len(Q_PARTS) + 1
        NMAX = 2 * UNITS
        MAX_OWN = 4


        units = [(c, j) for c in range(CPS) for j in range(TPC * (c + 1))]
        max_units = [(c, i, bank, hp) for c in range(CPS) for i in range(TPC) for bank in range(c + 1)
                     for hp in range(HG // 2)]
        assert len(max_units) == NMAX == 2 * len(units)
        MAX_LEAD = 22
        TURN_MAXIMA = {5: (2, False), 19: (3, False), 23: (0, True), 31: (1, True)}
        AFTER_O, AFTER_TURN_O = 0, 3
        assert UNITS - MAX_LEAD == 18 and AFTER_TURN_O == TPC - 1
        assert (NS - 2) % NBUF == 0

        def ends_chunk(u):
            c, i, bank, hp = max_units[u]
            return (i, bank, hp) == (TPC - 1, c, HG // 2 - 1)

        def all_stages(engine, stage):
            stage(0, 0, True, 1)
            with engine.Fori(0, (NS - 2) // NBUF) as turn:
                for n in range(1, NBUF + 1):
                    stage(NBUF * turn + n, n % NBUF, True, turn + (n + 1) // NBUF + ((n + 1) % NBUF > 0))
            stage(NS - 1, (NS - 1) % NBUF, False, 0)

        def max_unit(s, n, more):
            if n + MAX_LEAD < UNITS:
                return s, n + MAX_LEAD
            return (s + 1, n + MAX_LEAD - UNITS) if more else None

        def maxima_turned_at(s, n, more):
            c, following = TURN_MAXIMA.get(n, (None, False))
            if c is None or following and not more:
                return None
            return (s + 1 if following else s), c

        def load_stage(engine, s, columns, loaded):
            for g, (qp, kp) in enumerate(zip(Q_PARTS, K_PARTS)):
                for dst, qk, part in ((qa, 0, qp), (ka, 1, kp)):
                    src = k.qk_scr[qk, part][at(s, HG * DH, HG * DH), columns].rearrange("(h d) t -> d h t", h=HG)
                    engine.dma_start(dst[DH * g:DH * (g + 1), s % NBUF, :, columns], src).then_inc(loaded, 16)

        def load_values(engine, s, loaded):
            engine.dma_start(va[:, s % NBUF, :, :], k.v_scr[s, :, :, :]).then_inc(loaded, 16)

        with nc.Block() as block:
            @block.gpsimd
            def _(pool):
                nc.gpsimd.memset(ka[QROWS:QROWS + SPLIT, :, :, :], 1.0).then_inc(ones_set, 1)
                for s in range(1, NS):
                    if s == 1:
                        pool.wait_ge(stage0_rest_loaded, 16 * LOADS)
                    if s >= NBUF:
                        pool.wait_ge(probs_used, UNITS * (s - NBUF + 1))
                    load_stage(pool, s, slice(0, T), stage_loaded[s % NBUF])
                    load_values(pool, s, stage_loaded[s % NBUF])

            @block.sync
            def _(sp):
                def place(s, buf, c):
                    n = CPS * s + c
                    sp.wait_ge(max_rows_ready, n + 1)
                    sp.dma_start(k.max_scr[c % 2], max_rows[:, c % 2, :]).then_inc(max_stored, 16)
                    sp.wait_ge(max_stored, 16 * n + 16)
                    if not first(n):
                        sp.wait_ge(max_placed, 16 * n)
                    sp.dma_start(qa[QROWS:QROWS + SPLIT, buf, :, c * CH:(c + 1) * CH],
                                 k.max_scr[c % 2].rearrange("(o h) t -> o h t", o=SPLIT)).then_inc(max_placed, 16)

                def stage(s, buf, more, loads):
                    for n in range(UNITS):
                        turned = maxima_turned_at(s, n, more)
                        if turned:
                            place(turned[0], (buf + TURN_MAXIMA[n][1]) % NBUF, turned[1])

                load_stage(sp, 0, slice(0, T // 2), stage0_loaded)
                load_stage(sp, 0, slice(T // 2, T), stage0_rest_loaded)
                load_values(sp, 0, stage0_rest_loaded)
                for c in range(2):
                    place(0, 0, c)
                sp.wait_ge(zeros_set, 1)
                with sp.Fori(0, NTILES) as t:
                    sp.dma_start(k.x_slots[at(t, ST, ST), :].rearrange("(p u) d -> p (u d)", p=P), zeros[:, :]
                                 ).then_inc(slots_zeroed, 16)
                all_stages(sp, stage)
                sp.wait_ge(slots_zeroed, 16 * NTILES)

            @block.tensor
            def _(pe):
                def maximum(s, buf, u):
                    c, i, bank, hp = max_units[u]
                    width = CH if bank < c else P * (i + 1)
                    if u >= 2 or not first(s):
                        pe.wait_ge(max_taken, NMAX * s + u - 1)
                    for hh in range(2):
                        hd = 2 * hp + hh
                        q0 = (c * TPC + i) * P
                        last = nc.tensor.matmul(p_m[:, u % 2, hh, 0:width], qa[0:QROWS, buf, hd, q0:q0 + P],
                                                ka[0:QROWS, buf, hd, bank * CH:bank * CH + width],
                                                start=True, stop=bank < c)
                        if bank == c:
                            last = nc.tensor.matmul(p_m[:, u % 2, hh, width - P:width], k.identb[:, :],
                                                    k.masks[:, 0, :], start=False, stop=True)
                    last.then_inc(max_scores, 1)

                def scores(s, buf, n, h):
                    c, j = units[n]
                    lo = max(0, j - TPC * c) * P
                    if HG * n + h >= 2 or not first(s):
                        pe.wait_ge(probs_ready, HG * (UNITS * s + n) + h - 1)
                    last = nc.tensor.matmul(p_s[:, h % 2, lo:CH], ka[0:QROWS + SPLIT, buf, h, j * P:(j + 1) * P],
                                            qa[0:QROWS + SPLIT, buf, h, c * CH + lo:(c + 1) * CH],
                                            start=True, stop=j < TPC * c)
                    if j >= TPC * c:
                        last = nc.tensor.matmul(p_s[:, h % 2, lo:lo + P], k.identb[:, :], k.masks[:, 1, :],
                                                start=False, stop=True)
                    last.then_inc(scores_ready, 1)

                def values(s, buf, n):
                    c, j = units[n]
                    lo = max(0, j - TPC * c) * P
                    pe.wait_ge(probs_ready, HG * (UNITS * s + n) + HG)
                    if j == 0 and (c or not first(s)):
                        pe.wait_ge(o_taken, CPS * s + c)
                    for h in range(HG):
                        last = nc.tensor.matmul(p_o[VW * h:VW * (h + 1), lo:CH], va[:, buf, j, VW * h:VW * (h + 1)],
                                                probs[:, n % 2, h, lo:CH], start=j == 0, stop=j == TPC * (c + 1) - 1)
                    last.then_inc(probs_used, 1)

                def turn_maxima(n):
                    pe.wait_ge(max_parts_ready, n + 1)
                    rows = p_misc[:, :].bitcast(BF16)
                    for i in range(TPC):
                        last = nc.tensor.transpose(rows[0:SPLIT * HG, i * P:(i + 1) * P],
                                                   max_parts[:, i, :, :].rearrange("p s h -> p (s h)"), k.identb[:, :])
                    last.then_inc(max_turned, 1)

                def turn_outputs(n, parity):
                    pe.wait_ge(o_taken, n + 1)
                    for u in range(TPC):
                        last = nc.tensor.transpose(p_misc[:, u * P:(u + 1) * P], o_sb[:, parity, u * P:(u + 1) * P],
                                                   k.ident[:, :])
                    last.then_inc(o_turned, 1)

                def turn_m(s, c):
                    if c == 2 and not first(s):
                        pe.wait_ge(att_ready, CPS * s + 1)
                    elif c == 0:
                        pe.wait_ge(max_rows_ready, CPS * s)
                    elif c == 2:
                        pe.wait_ge(max_rows_ready, 2)
                    elif c == 3:
                        pe.wait_ge(att_ready, CPS * s + 3)
                    else:
                        pe.wait_ge(att_ready, CPS * s)
                    turn_maxima(CPS * s + c)

                def turn_o(s, c, more):
                    if c == 1:
                        pe.wait_ge(att_ready, CPS * s + 2)
                    elif c == 0:
                        pe.wait_ge(max_rows_ready, CPS * s + 3)
                    elif c == 2:
                        pe.wait_ge(max_rows_ready, CPS * s + (5 if more else 4))
                    else:
                        pe.wait_ge(max_rows_ready, CPS * s + (6 if more else 4))
                        if not more:
                            pe.wait_ge(att_ready, CPS * s + 4)
                    turn_outputs(CPS * s + c, c % 2)

                def stage(s, buf, more, loads):
                    nbuf = (buf + 1) % NBUF
                    for n, (c, j) in enumerate(units):
                        if j == 0:
                            pe.wait_ge(max_placed, 16 * (CPS * s + c + 1))
                        for h in range(HG):
                            scores(s, buf, n, h)
                            if h == 1:
                                if n:
                                    values(s, buf, n - 1)
                                elif not first(s):
                                    values(s - 1, (buf - 1) % NBUF, UNITS - 1)
                        w = max_unit(s, n, more)
                        if w:
                            own_stage = n + MAX_LEAD < UNITS
                            if w[1] == 0:
                                pe.wait_ge(stage_loaded[nbuf], 16 * LOADS * loads)
                            for u in (2 * w[1], 2 * w[1] + 1):
                                maximum(w[0], buf if own_stage else nbuf, u)
                        turned = maxima_turned_at(s, n, more)
                        if turned:
                            turn_m(*turned)
                        if j == AFTER_TURN_O and c:
                            turn_o(s, c - 1, more)
                        elif j == AFTER_TURN_O and not first(s):
                            turn_o(s - 1, CPS - 1, True)

                pe.wait_ge(stage0_loaded, 16 * (LOADS - 1))
                for u in range(2 * MAX_LEAD):
                    if max_units[u][:3] == (CPS // 2, 0, 0) and u % 2 == 0:
                        pe.wait_ge(stage0_rest_loaded, 16 * LOADS)
                    maximum(0, 0, u)
                    if ends_chunk(u):
                        c = max_units[u][0]
                        if c:
                            pe.wait_ge(max_rows_ready, c)
                        turn_maxima(c)
                pe.wait_ge(ones_set, 1)
                all_stages(pe, stage)
                values(NS - 1, (NS - 1) % NBUF, UNITS - 1)
                turn_o(NS - 1, CPS - 1, False)

            @block.scalar
            def _(act):
                def exponentials(s, n):
                    c, j = units[n]
                    lo = max(0, j - TPC * c) * P
                    if n >= 2 or not first(s):
                        act.wait_ge(probs_used, UNITS * s + n - 1)
                    for h in range(HG):
                        act.wait_ge(scores_ready, HG * (UNITS * s + n) + h + 1)
                        nc.scalar.activation(probs[:, n % 2, h, lo:CH], p_s[:, h % 2, lo:CH], ACT.Exp,
                                             scale=DH ** -0.5).then_inc(probs_ready, 1)

                def take_o(s, c, n_last):
                    act.wait_ge(probs_used, UNITS * s + n_last + 1)
                    nc.scalar.activation(o_sb[:, c % 2, :], p_o[:, :], ACT.Copy).then_inc(o_taken, 1)

                def take_rows(n, c):
                    act.wait_ge(max_turned, n + 1)
                    if not (isinstance(n, int) and n < 2):
                        act.wait_ge(max_stored, 16 * (n - 1))
                    nc.scalar.activation(max_rows[:, c % 2, :], p_misc[:, :].bitcast(BF16)[0:SPLIT * HG, 0:CH],
                                         ACT.Copy).then_inc(max_rows_ready, 1)

                def stage(s, buf, more, loads):
                    for n, (c, j) in enumerate(units):
                        exponentials(s, n)
                        if j == AFTER_O and c:
                            take_o(s, c - 1, n - 1)
                        elif j == AFTER_O and not first(s):
                            take_o(s - 1, CPS - 1, UNITS - 1)
                        turned = maxima_turned_at(s, n - 1, more)
                        if turned:
                            take_rows(CPS * turned[0] + turned[1], turned[1])

                for c in range(2):
                    take_rows(c, c)
                all_stages(act, stage)
                take_o(NS - 1, CPS - 1, UNITS - 1)

            @block.vector
            def _(dve):
                def take_max(s, u):
                    c, i, bank, hp = max_units[u]
                    width = CH if bank < c else P * (i + 1)
                    dve.wait_ge(max_scores, NMAX * s + u + 1)
                    nc.vector.tensor_reduce(out=tile_max[:, 2 * hp:2 * hp + 2, i, bank], in_=p_m[:, u % 2, :, 0:width],
                                            op=ALU.max, axis=AX.X).then_inc(max_taken, 1)

                def split_max(s, c):
                    n = CPS * s + c
                    step = Count(dve, own, MAX_OWN * n)
                    dve.wait_ge(max_taken, NMAX * s + sum(ends_chunk(u) * (u + 1) for u in range(NMAX) if max_units[u][0] == c))
                    if not first(n):
                        dve.wait_ge(max_turned, n)
                    part = [max_parts[:, :, q, :].rearrange("p i h -> p h i") for q in range(SPLIT)]
                    step.step(nc.vector.tensor_reduce(out=row_max[:, :, :], in_=tile_max[:, :, :, 0:c + 1],
                                                      op=ALU.max, axis=AX.X))
                    step.step(nc.vector.tensor_scalar(part[0], row_max[:, :, :], -1.0, None, ALU.mult))
                    step.step(nc.vector.scalar_tensor_tensor(out=max_rest[:, :, :], in0=row_max[:, :, :], scalar=-1.0,
                                                             in1=part[0], op0=ALU.mult, op1=ALU.subtract))
                    step.step(nc.vector.tensor_copy(part[1], max_rest[:, :, :]))
                    nc.vector.tensor_tensor(part[2], max_rest[:, :, :], part[1], ALU.subtract).then_inc(max_parts_ready, 1)
                    assert step.n == MAX_OWN

                def divide(s, c):
                    n = CPS * s + c
                    b = s // (H0 // HG)
                    dve.wait_ge(o_turned, n + 1)
                    o = p_misc[:, :].rearrange("p (u h w) -> p u h w", u=TPC, h=HG)
                    nc.vector.reciprocal(recip[:, :, :], o[:, :, :, DH]).then_inc(recip_ready, 1)
                    dve.wait_ge(recip_ready, n + 1)
                    nc.vector.tensor_tensor(
                        k.x[:, at(b * JT + c * TPC, 1, TPC), at(s % (H0 // HG), HG * DH, HG * DH)]
                        .rearrange("p u (h d) -> p u h d", h=HG),
                        o[:, :, :, 0:DH], recip[:, :, :].unsqueeze(3).to_broadcast([P, TPC, HG, DH]),
                        ALU.mult).then_inc(att_ready, 1)

                def stage(s, buf, more, loads):
                    for n, (c, j) in enumerate(units):
                        w = max_unit(s, n, more)
                        if w:
                            for u in (2 * w[1], 2 * w[1] + 1):
                                take_max(w[0], u)
                                if ends_chunk(u):
                                    split_max(w[0], max_units[u][0])
                        if j == AFTER_TURN_O and c:
                            divide(s, c - 1)
                        elif j == AFTER_TURN_O and not first(s):
                            divide(s - 1, CPS - 1)

                nc.vector.memset(zeros[:, :], 0.0).then_inc(zeros_set, 1)
                nc.vector.memset(recip[:, :, :], 0.0).then_inc(att_ready, 1)
                guard_gates(nc, k, Count(dve, gates_own), sign, mag)
                for u in range(2 * MAX_LEAD):
                    take_max(0, u)
                    if ends_chunk(u):
                        split_max(0, max_units[u][0])
                all_stages(dve, stage)
                divide(NS - 1, CPS - 1)


def output_projection(nc, a, k):
    with ExitStack() as stack:
        m = Mem(nc, stack)
        w = m.sb("wo", [P, KT, D])
        xin = m.sb("o_xin", [P, 2, TPC, D])
        still = m.sb("o_still", [P, TPC, D])
        aT = m.sb("o_aT", [P, KT, CH])
        gated = m.sb("o_gated", [P, TPC, D])
        p_t = m.ps("o_pt", [P, KT, CH])
        p_o = m.ps("o_po", [P, TPC, D])
        w_loaded, still_ready = m.sem("o_w_loaded"), m.sem("o_still_ready")
        x_loaded = [m.sem(f"o_x_loaded{n}") for n in range(2)]
        turned, aT_ready, product = m.sem("o_turned_"), m.sem("o_aT_ready"), m.sem("o_product")
        scaled, x1_ready = m.sem("o_scaled"), m.sem("o_x1_ready")
        with nc.Block() as block:
            @block.sync
            def _(sp):
                def load(i, par):
                    sp.dma_start(xin[:, par, :, :],
                                 a["x"][at(i, CH, CH), :].rearrange("(u p) d -> p u d", p=P)).then_inc(x_loaded[par], 16)

                sp.dma_start(w[:, :, :], a["woT"].rearrange("(k p) n -> p k n", p=P)).then_inc(w_loaded, 16)
                load(0, 0)
                load(1, 1)
                with sp.Fori(1, NCH // 2) as i:
                    for par in range(2):
                        sp.wait_ge(x1_ready, 2 * i + par - 1)
                        load(2 * i + par, par)

            @block.scalar
            def _(act):
                def chunk(i):
                    if not first(i):
                        act.wait_ge(turned, i)
                    nc.scalar.activation(still[:, :, :], k.x[:, at(i, TPC, TPC), :], ACT.Copy).then_inc(still_ready, 1)
                    act.wait_ge(turned, i + 1)
                    if not first(i):
                        act.wait_ge(product, i)
                    nc.scalar.activation(aT[:, :, :], p_t[:, :, :], ACT.Copy).then_inc(aT_ready, 1)

                chunk(0)
                with act.Fori(1, NCH) as i:
                    chunk(i)

            @block.tensor
            def _(pe):
                def chunk(i):
                    pe.wait_ge(still_ready, i + 1)
                    for kt in range(KT):
                        for u in range(TPC):
                            last = nc.tensor.transpose(p_t[:, kt, u * P:(u + 1) * P], still[:, u, kt * P:(kt + 1) * P],
                                                       k.ident[:, :])
                    last.then_inc(turned, 1)
                    pe.wait_ge(aT_ready, i + 1)
                    if not first(i):
                        pe.wait_ge(scaled, i)
                    for u in range(TPC):
                        for kt in range(KT):
                            last = nc.tensor.matmul(p_o[:, u, :], aT[:, kt, u * P:(u + 1) * P], w[:, kt, :],
                                                    start=kt == 0, stop=kt == KT - 1)
                    last.then_inc(product, 1)

                pe.wait_ge(w_loaded, 16)
                chunk(0)
                with pe.Fori(1, NCH) as i:
                    chunk(i)

            @block.vector
            def _(dve):
                with dve.Fori(0, NCH // 2) as turn:
                    for par in range(2):
                        i = 2 * turn + par
                        dve.wait_ge(product, i + 1)
                        nc.vector.tensor_tensor(gated[:, :, :], p_o[:, :, :], k.mod(0, i // CPS, GA),
                                                ALU.mult).then_inc(scaled, 1)
                        dve.wait_ge(x_loaded[par], 16 * (turn + 1))
                        dve.wait_ge(scaled, i + 1)
                        nc.vector.tensor_tensor(k.x[:, at(i, TPC, TPC), :], gated[:, :, :], xin[:, par, :, :],
                                                ALU.add).then_inc(x1_ready, 1)
                        dve.wait_ge(x1_ready, i + 1)
                        row_stats(nc, k, i)


def top1_experts(nc, a, k):
    BANKS = E0 * D // CH
    EPB = E0 // BANKS
    HALF = E0 // 2
    with ExitStack() as stack:
        m = Mem(nc, stack)
        raw, raw_gate = m.sb("c_raw", [P, KT, E0 * D]), m.sb("c_raw_gate", [P, KT, E0])
        w = m.sb("w_expert", [P, 2, KT, E0 * D], F32R)
        gate = m.sb("w_gate0", [P, 2, KT, E0], F32R)
        iota = m.sb("iota_e", [P, E0])
        h = m.sb("c_h", [P, 2, D])
        hT = m.sb("c_hT", [P, 2, 2, KT, P], F32R)
        top, top_at, same = m.sb("c_top", [P, 1]), m.sb("c_top_at", [P, 1]), m.sb("c_same", [P, E0])
        onehot = m.sb("c_onehot", [P, 2, E0])
        acc, terms = m.sb("c_acc", [P, 2, D]), m.sb("c_terms", [P, HALF, D])
        pairs_sum, half_sum = m.sb("c_pairs_sum", [P, HALF // 2, D]), m.sb("c_half_sum", [P, D])
        p_e = m.ps("p_e", [P, BANKS, CH])
        p_t = m.ps("c_pt", [P, KT, P])
        p_g = m.ps("p_g", [P, E0])
        loaded = m.sem("c_loaded")
        w_high, w_ready = m.sem("c_w_high"), m.sem("c_w_ready")
        h_centered, h_scaled, h_ready = m.sem("c_h_centered"), m.sem("c_h_scaled"), m.sem("c_h_ready")
        turned, hT_high, hT_ready, gate_psum = m.sem("c_turned"), m.sem("c_hT_high"), m.sem("c_hT_ready"), m.sem("c_gate_psum")
        picked, onehot_ready, expert_psum = m.sem("c_picked"), m.sem("c_onehot_ready"), m.sem("c_expert_psum")
        taken_dve, taken_act = m.sem("c_taken_dve"), m.sem("c_taken_act")
        paired, half_ready, summed = m.sem("c_paired"), m.sem("c_half_ready"), m.sem("c_summed")
        own = m.sem("c_own")
        LOADS, PICKS = 3, 3

        def all_tiles(engine, tile):
            tile(0, 0, 2)
            tile(1, 1, 2)
            with engine.Fori(1, NT // 2 - 1) as i:
                tile(2 * i, 0, 2)
                tile(2 * i + 1, 1, 2)
            tile(NT - 2, 0, 1)
            tile(NT - 1, 1, 0)

        def bank_of(x, part, bank):
            return x[:, part, :, bank * CH:(bank + 1) * CH]

        with nc.Block() as block:
            @block.sync
            def _(sp):
                sp.dma_start(raw_gate[:, :, :], a["gateT"].rearrange("(k p) n -> p k n", p=P)).then_inc(loaded, 16)
                sp.dma_start(iota[:, :], a["iota8"]).then_inc(loaded, 16)
                sp.dma_start(raw[:, :, :], a["expertT"].rearrange("(k p) n -> p k n", p=P)).then_inc(loaded, 16)
                sp.wait_ge(loaded, 16 * LOADS)

            @block.gpsimd
            def _(pool):
                def scale(t, par):
                    pool.wait_ge(h_centered, t + 1)
                    nc.gpsimd.tensor_tensor(h[:, par, :], h[:, par, :], k.mod1(0, t // JT, CB), ALU.mult).then_inc(h_scaled, 1)
                    pool.wait_ge(h_scaled, t + 1)
                    nc.gpsimd.tensor_tensor(h[:, par, :], h[:, par, :], k.mod1(0, t // JT, SB_), ALU.add).then_inc(h_ready, 1)

                def tile(t, par, more):
                    if more == 2:
                        scale(t + 2, par)
                    if not first(t):
                        pool.wait_ge(half_ready, t)
                    pool.wait_ge(taken_act, HALF * t + HALF)
                    nc.gpsimd.tensor_tensor(pairs_sum[:, :, :], terms[:, 0:HALF // 2, :], terms[:, HALF // 2:HALF, :],
                                            ALU.add).then_inc(paired, 1)
                    pool.wait_ge(paired, t + 1)
                    if not first(t):
                        pool.wait_ge(summed, t)
                    nc.gpsimd.tensor_tensor(half_sum[:, :], pairs_sum[:, 0, :], pairs_sum[:, 1, :], ALU.add
                                            ).then_inc(half_ready, 1)

                root(nc, pool, k, 1)
                scale(0, 0)
                scale(1, 1)
                for n in range(1 + BANKS):
                    pool.wait_ge(w_high, n + 1)
                    if n:
                        nc.gpsimd.tensor_tensor(bank_of(w, LO, n - 1), raw[:, :, (n - 1) * CH:n * CH],
                                                bank_of(w, HI, n - 1), ALU.subtract).then_inc(w_ready, 1)
                    else:
                        nc.gpsimd.tensor_tensor(gate[:, LO, :, :], raw_gate[:, :, :], gate[:, HI, :, :],
                                                ALU.subtract).then_inc(w_ready, 1)
                all_tiles(pool, tile)

            @block.scalar
            def _(act):
                def round_hT(t, par):
                    act.wait_ge(turned, t + 1)
                    nc.scalar.activation(hT[:, par, HI, :, :], p_t[:, :, :], ACT.Copy).then_inc(hT_high, 1)

                def tile(t, par, more):
                    if more:
                        round_hT(t + 1, 1 - par)
                    if not first(t):
                        act.wait_ge(paired, t)
                    act.wait_ge(onehot_ready, t + 1)
                    for e in range(HALF, E0):
                        act.wait_ge(expert_psum, BANKS * t + e // EPB + 1)
                        nc.scalar.activation(terms[:, e - HALF, :], p_e[:, e // EPB, (e % EPB) * D:(e % EPB + 1) * D],
                                             ACT.Copy, scale=onehot[:, par, e:e + 1]).then_inc(taken_act, 1)

                act.wait_ge(loaded, 16 * LOADS)
                nc.scalar.activation(gate[:, HI, :, :], raw_gate[:, :, :], ACT.Copy).then_inc(w_high, 1)
                for bank in range(BANKS):
                    nc.scalar.activation(bank_of(w, HI, bank), raw[:, :, bank * CH:(bank + 1) * CH], ACT.Copy).then_inc(w_high, 1)
                round_hT(0, 0)
                all_tiles(act, tile)

            @block.tensor
            def _(pe):
                def turn(t, par):
                    pe.wait_ge(h_ready, t + 1)
                    if not first(t):
                        pe.wait_ge(hT_ready, t)
                    for kt in range(KT):
                        last = nc.tensor.transpose(p_t[:, kt, :], h[:, par, kt * P:(kt + 1) * P], k.ident[:, :])
                    last.then_inc(turned, 1)

                def product(out, t, par, weights, done):
                    for kt in range(KT):
                        for wp, hp in PRODUCTS:
                            last = nc.tensor.matmul(out, hT[:, par, hp, kt, :], weights(wp, kt),
                                                    start=(kt, wp, hp) == (0, HI, HI), stop=(kt, wp, hp) == (KT - 1, LO, HI))
                    last.then_inc(done, 1)

                def choose(t, par):
                    pe.wait_ge(hT_ready, t + 1)
                    if not first(t):
                        pe.wait_ge(onehot_ready, t)
                    product(p_g[:, :], t, par, lambda part, kt: gate[:, part, kt, :], gate_psum)

                def experts(t, par, bank):
                    if first(t):
                        pe.wait_ge(w_ready, bank + 2)
                    elif bank < BANKS // 2:
                        pe.wait_ge(taken_dve, HALF * (t - 1) + EPB * (bank + 1))
                    else:
                        pe.wait_ge(taken_act, HALF * (t - 1) + EPB * (bank - BANKS // 2 + 1))
                    product(p_e[:, bank, :], t, par, lambda part, kt: w[:, part, kt, bank * CH:(bank + 1) * CH], expert_psum)

                def tile(t, par, more):
                    for bank in range(BANKS):
                        experts(t, par, bank)
                        if more and bank == 1:
                            turn(t + 1, 1 - par)
                    if more:
                        choose(t + 1, 1 - par)

                turn(0, 0)
                pe.wait_ge(w_ready, 1)
                choose(0, 0)
                all_tiles(pe, tile)

            @block.vector
            def _(dve):
                def center(t, par):
                    nc.vector.tensor_scalar(h[:, par, :], k.x[:, at(t, 1, 1), :].rearrange("p o d -> p (o d)"),
                                            k.mean[:, at(t, 1, 1)], k.rstd[:, at(t, 1, 1)],
                                            ALU.subtract, ALU.mult).then_inc(h_centered, 1)

                def rest_of_hT(t, par):
                    dve.wait_ge(hT_high, t + 1)
                    nc.vector.tensor_tensor(hT[:, par, LO, :, :], p_t[:, :, :], hT[:, par, HI, :, :],
                                            ALU.subtract).then_inc(hT_ready, 1)

                def pick(t, par):
                    c = Count(dve, picked, PICKS * t)
                    dve.wait_ge(gate_psum, t + 1)
                    c.step(nc.vector.tensor_reduce(out=top[:, :], in_=p_g[:, :], op=ALU.max, axis=AX.X))
                    c.step(nc.vector.scalar_tensor_tensor(out=same[:, :], in0=p_g[:, :], scalar=top[:, :], in1=iota[:, :],
                                                          op0=ALU.is_equal, op1=ALU.mult))
                    c.step(nc.vector.tensor_reduce(out=top_at[:, :], in_=same[:, :], op=ALU.min, axis=AX.X))
                    nc.vector.tensor_scalar(onehot[:, par, :], iota[:, :], top_at[:, :], None, ALU.is_equal).then_inc(onehot_ready, 1)
                    dve.wait_ge(onehot_ready, t + 1)
                    assert c.n == PICKS

                def finish(t, par):
                    total = acc[:, par, :]
                    dve.wait_ge(half_ready, t + 1)
                    nc.vector.tensor_tensor(total, total, half_sum[:, :], ALU.add).then_inc(summed, 1)
                    dve.wait_ge(summed, t + 1)
                    x = k.x[:, at(t, 1, 1), :].rearrange("p o d -> p (o d)")
                    nc.vector.tensor_tensor(total, total, k.mod1(0, t // JT, GB), ALU.mult).then_inc(k.scaled, 1)
                    dve.wait_ge(k.scaled, t + 1)
                    nc.vector.tensor_tensor(x, x, total, ALU.add).then_inc(k.x2_ready, 1)
                    dve.wait_ge(k.x2_ready, t + 1)
                    nc.vector.bn_stats(out=k.stats[:, at(t, 1, 1), :].rearrange("p o s -> p (o s)"), in_=x)

                def tile(t, par, more):
                    for e in range(HALF):
                        if e % EPB == 0:
                            dve.wait_ge(expert_psum, BANKS * t + e // EPB + 1)
                        nc.vector.scalar_tensor_tensor(
                            out=acc[:, par, :], in0=p_e[:, e // EPB, (e % EPB) * D:(e % EPB + 1) * D],
                            scalar=onehot[:, par, e:e + 1], in1=h[:, par, :] if e == 0 else acc[:, par, :],
                            op0=ALU.mult, op1=ALU.add).then_inc(taken_dve, 1)
                        dve.wait_ge(taken_dve, HALF * t + e + 1)
                    if more == 2:
                        center(t + 2, par)
                    if more:
                        rest_of_hT(t + 1, 1 - par)
                    if not first(t):
                        finish(t - 1, 1 - par)
                    if more:
                        pick(t + 1, 1 - par)

                aggregate(nc, Count(dve, own), k).then_inc(k.ve_ready, 1)
                dve.wait_ge(k.rstd_ready, 2)
                center(0, 0)
                center(1, 1)
                rest_of_hT(0, 0)
                pick(0, 0)
                all_tiles(dve, tile)
                finish(NT - 1, 1)


def second_norm(nc, a, k, norm, name, shift, scale, kept, xnT_all, weight, logits):
    before_mix = weight is None
    with ExitStack() as stack:
        m = Mem(nc, stack)
        xn = m.sb(name + "xn", [P, 2, TPC, D])
        xnT = None if before_mix else m.sb(name + "xnT", [P, 2, KT, CH])
        squares = m.sb(name + "squares", [P, D])
        ss, ms, rms, inv = (m.sb(name + n, [P, 2, TPC]) for n in ("ss", "ms", "rms", "inv"))
        power = m.sb(name + "power", [P, TPC])
        on_all = m.sb(name + "on_all", [P, D])
        p_t = m.ps(name + "pt", [P, 2, KT, CH])
        p_l = m.ps(name + "pl", [P, TPC, E1])
        h_ready = m.sem(name + "h_ready")
        squared, ms_ready, rms_ready = m.sem(name + "squared"), m.sem(name + "ms_ready"), m.sem(name + "rms_ready")
        inv_ready, xn_ready, turned = m.sem(name + "inv_ready"), m.sem(name + "xn_ready"), m.sem(name + "turned")
        xnT_ready, row_kept = m.sem(name + "xnT_ready"), m.sem(name + "row_kept")
        own, power_set, w_loaded = m.sem(name + "own"), m.sem(name + "power_set"), m.sem(name + "w_loaded")
        if before_mix:
            rms_guarded = m.sem(name + "rms_guarded")
        else:
            weighted, logit_psum, logits_taken = (m.sem(name + n) for n in ("weighted", "logit_psum", "logits_taken"))
            w_l = m.sb(name + "w_l", [P, KT, E1])
            b_l = m.sb(name + "b_l", [P, E1])
        LOADS = 1 if before_mix else 3

        def turns(engine, turn, after):
            turn(0, 0)
            turn(1, 1)
            with engine.Fori(1, NCH // 2 - 1) as i:
                turn(2 * i, 0)
                turn(2 * i + 1, 1)
            for i in range(NCH - 2, NCH + after):
                turn(i, i % 2)

        def early(i, n):
            return isinstance(i, int) and i < n

        def late(i):
            return isinstance(i, int) and i >= NCH

        def kept_row(i, u):
            return kept[:, at(i * TPC + u, 1, 1), :].rearrange("p o d -> p (o d)")

        with nc.Block() as block:
            @block.sync
            def _(sp):
                src = a["o_b"] if before_mix else weight
                sp.dma_start(on_all[:, :], src.partition_broadcast(P)).then_inc(w_loaded, 16)
                if not before_mix:
                    sp.dma_start(w_l[:, :, :], a["Wg"].rearrange("(k p) n -> p k n", p=P)).then_inc(w_loaded, 16)
                    sp.dma_start(b_l[:, :], a["bg"].partition_broadcast(P)).then_inc(w_loaded, 16)
                sp.wait_ge(w_loaded, 16 * LOADS)

            @block.gpsimd
            def _(pool):
                def turn(i, par):
                    if not late(i):
                        pool.wait_ge(ms_ready, i + 1)
                        nc.gpsimd.tensor_tensor(rms[:, par, :], ms[:, par, :], power[:, :], ALU.pow).then_inc(rms_ready, 1)
                    if before_mix and not early(i, 1):
                        if early(i, 2):
                            pool.wait_ge(w_loaded, 16 * LOADS)
                        pool.wait_ge(xn_ready, TPC * i)
                        rows = kept[:, at(i - 1, TPC, TPC), :]
                        nc.gpsimd.tensor_tensor(rows, rows, on_all[:, :].unsqueeze(1).to_broadcast([P, TPC, D]),
                                                ALU.add).then_inc(row_kept, 1)

                root(nc, pool, k, norm)
                nc.gpsimd.memset(power[:, :], 0.5 if before_mix else -0.5).then_inc(power_set, 1)
                pool.wait_ge(power_set, 1)
                turns(pool, turn, 1 if before_mix else 0)

            @block.scalar
            def _(act):
                def turn(i, par):
                    if not late(i):
                        act.wait_ge(h_ready, i + 1)
                        for u in range(TPC):
                            if u or not first(i):
                                act.wait_ge(squared, TPC * i + u)
                            nc.scalar.activation(squares[:, :], kept_row(i, u), ACT.Square,
                                                 accum_out=ss[:, par, u:u + 1]).then_inc(squared, 1)
                    scaled = not early(i, 1) and not (isinstance(i, int) and i > NCH)
                    if scaled:
                        act.wait_ge(inv_ready, i)
                    if not early(i, 2):
                        act.wait_ge(turned, i - 1)
                        if before_mix:
                            dst = xnT_all[:, :, at(i - 2, CH, CH)]
                        else:
                            dst = xnT[:, par, :, :]
                        nc.scalar.activation(dst, p_t[:, par, :, :], ACT.Copy).then_inc(xnT_ready, 1)
                    if scaled:
                        for u in range(TPC):
                            nc.scalar.activation(xn[:, 1 - par, u, :], kept_row(i - 1, u), ACT.Copy,
                                                 scale=inv[:, 1 - par, u:u + 1]).then_inc(xn_ready, 1)

                turns(act, turn, 2)

            @block.tensor
            def _(pe):
                def turn(i, par):
                    if not late(i):
                        if before_mix:
                            pe.wait_ge(xn_ready, TPC * i + TPC)
                        else:
                            pe.wait_ge(weighted, i + 1)
                        if not early(i, 2):
                            pe.wait_ge(xnT_ready, i - 1)
                        for kt in range(KT):
                            for u in range(TPC):
                                last = nc.tensor.transpose(p_t[:, par, kt, u * P:(u + 1) * P],
                                                           xn[:, par, u, kt * P:(kt + 1) * P], k.ident[:, :])
                        last.then_inc(turned, 1)
                    if not before_mix and not early(i, 1):
                        if early(i, 2):
                            pe.wait_ge(w_loaded, 16 * LOADS)
                        pe.wait_ge(xnT_ready, i)
                        if not early(i, 2):
                            pe.wait_ge(logits_taken, i - 1)
                        for u in range(TPC):
                            for kt in range(KT):
                                last = nc.tensor.matmul(p_l[:, u, :], xnT[:, 1 - par, kt, u * P:(u + 1) * P],
                                                        w_l[:, kt, :], start=kt == 0, stop=kt == KT - 1)
                        last.then_inc(logit_psum, 1)

                turns(pe, turn, 0 if before_mix else 1)

            @block.vector
            def _(dve):
                def layernorm(i):
                    c = Count(dve, own, AGGREGATE_STEPS + NORM_STEPS * i)
                    for u in range(TPC):
                        t = at(i * TPC + u, 1, 1)
                        c.add(nc.vector.tensor_scalar(kept_row(i, u), k.x[:, t, :].rearrange("p o d -> p (o d)"),
                                                      k.mean[:, t], k.rstd[:, t], ALU.subtract, ALU.mult))
                    c.wait()
                    rows = kept[:, at(i, TPC, TPC), :]
                    c.step(nc.vector.tensor_tensor(rows, rows, k.mod(1, i // CPS, scale), ALU.mult))
                    nc.vector.tensor_tensor(rows, rows, k.mod(1, i // CPS, shift), ALU.add).then_inc(h_ready, 1)
                    assert c.n == NORM_STEPS

                def mean_square(i, par):
                    dve.wait_ge(squared, TPC * i + TPC)
                    if before_mix:
                        nc.vector.tensor_scalar(ms[:, par, :], ss[:, par, :], 1.0 / D, None, ALU.mult).then_inc(ms_ready, 1)
                    else:
                        nc.vector.tensor_scalar(ms[:, par, :], ss[:, par, :], 1.0 / D, float(np.finfo(np.float32).eps),
                                                ALU.mult, ALU.add).then_inc(ms_ready, 1)

                def inverse(i, par):
                    dve.wait_ge(rms_ready, i + 1)
                    if before_mix:
                        nc.vector.tensor_scalar(rms[:, par, :], rms[:, par, :], 1e-8, None, ALU.add).then_inc(rms_guarded, 1)
                        dve.wait_ge(rms_guarded, i + 1)
                        nc.vector.reciprocal(inv[:, par, :], rms[:, par, :]).then_inc(inv_ready, 1)
                    else:
                        nc.vector.tensor_copy(inv[:, par, :], rms[:, par, :]).then_inc(inv_ready, 1)

                def weigh(i, par):
                    if first(i):
                        dve.wait_ge(w_loaded, 16 * LOADS)
                    dve.wait_ge(xn_ready, TPC * i + TPC)
                    nc.vector.tensor_tensor(xn[:, par, :, :], xn[:, par, :, :],
                                            on_all[:, :].unsqueeze(1).to_broadcast([P, TPC, D]), ALU.mult).then_inc(weighted, 1)
                    dve.wait_ge(weighted, i + 1)
                    nc.vector.tensor_copy(kept[:, at(i, TPC, TPC), :], xn[:, par, :, :]).then_inc(row_kept, 1)
                    dve.wait_ge(row_kept, i + 1)

                def take_logits(i, par):
                    dve.wait_ge(logit_psum, i + 1)
                    nc.vector.tensor_tensor(logits[:, at(i, TPC, TPC), :], p_l[:, :, :],
                                            b_l[:, :].unsqueeze(1).to_broadcast([P, TPC, E1]),
                                            ALU.add).then_inc(logits_taken, 1)

                def turn(i, par):
                    if not (isinstance(i, int) and i >= NCH - 1):
                        layernorm(i + 1)
                    if not late(i):
                        mean_square(i, par)
                    if not before_mix:
                        if not early(i, 1) and not (isinstance(i, int) and i > NCH):
                            weigh(i - 1, 1 - par)
                        if not early(i, 2):
                            take_logits(i - 2, par)
                    if not late(i):
                        inverse(i, par)

                aggregate(nc, Count(dve, own), k).then_inc(k.ve_ready, 1)
                dve.wait_ge(k.rstd_ready, norm + 1)
                layernorm(0)
                turns(dve, turn, 0 if before_mix else 2)


def mix(nc, a, k, h_all, xnT_all):
    with ExitStack() as stack:
        m = Mem(nc, stack)
        w = m.sb("w_uv", [P, KT, 2 * F1])
        wo = m.sb("w_o1", [P, FB1, D])
        bias = m.sb("b_uv", [P, 2 * FB1])
        toep = m.sb("toep", [P, 3, FB1])
        u_sb = m.sb("u_sb", [P, B, FB1, CH])
        v_sb = m.sb("v_sb", [P, B, FB1, CH])
        y_sb = m.sb("y_sb", [P, B, FB1, CH])
        p_uv = m.ps("p_uv", [P, 4, CH])
        p_o = m.ps("d_po", [P, B, TPC, D])
        loaded, uv_psum, uv_ready = m.sem("d_loaded"), m.sem("d_uv_psum"), m.sem("d_uv_ready")
        own, g_ready, product, x3_ready = m.sem("d_own"), m.sem("d_g_ready"), m.sem("d_product"), m.sem("d_x3_ready")
        taken = m.sem("d_taken")
        LOADS = 4
        NB = 2 * B * FB1
        order = [(1, n, f) for n in range(B) for f in range(FB1)] + [(0, n, f) for n in range(B) for f in range(FB1)]
        OWN = 4 * FB1 + B
        with nc.Block() as block:
            @block.sync
            def _(sp):
                sp.dma_start(w[:, :, :], a["w_uv"].rearrange("(k p) n -> p k n", p=P)).then_inc(loaded, 16)
                sp.dma_start(wo[:, :, :], a["o_wT"].rearrange("(f p) n -> p f n", p=P)).then_inc(loaded, 16)
                sp.dma_start(bias[:, :], a["b_uv"]).then_inc(loaded, 16)
                sp.dma_start(toep[:, :, :], a["toep"]).then_inc(loaded, 16)
                sp.wait_ge(loaded, 16 * LOADS)

            @block.tensor
            def _(pe):
                def chunk(c):
                    for q, (is_v, n, f) in enumerate(order):
                        if q >= 4 or not first(c):
                            pe.wait_ge(uv_ready, NB * c + q - 3)
                        for kt in range(KT):
                            last = nc.tensor.matmul(p_uv[:, q % 4, :], w[:, kt, is_v * F1 + f * P:is_v * F1 + (f + 1) * P],
                                                    xnT_all[:, kt, at(n * CPS + c, CH, CH)],
                                                    start=kt == 0, stop=kt == KT - 1)
                        last.then_inc(uv_psum, 1)
                    for n in range(B):
                        pe.wait_ge(g_ready, B * c + n + 1)
                        if not first(c):
                            pe.wait_ge(taken, B * (c - 1) + n + 1)
                        for u in range(TPC):
                            for f in range(FB1):
                                last = nc.tensor.matmul(p_o[:, n, u, :], y_sb[:, n, f, u * P:(u + 1) * P], wo[:, f, :],
                                                        start=f == 0, stop=f == FB1 - 1)
                        last.then_inc(product, 1)

                pe.wait_ge(loaded, 16 * LOADS)
                chunk(0)
                with pe.Fori(1, CPS) as c:
                    chunk(c)

            @block.scalar
            def _(act):
                def chunk(c):
                    for q, (is_v, n, f) in enumerate(order):
                        act.wait_ge(uv_psum, NB * c + q + 1)
                        if q == 0 and not first(c):
                            act.wait_ge(g_ready, B * c)
                        dst = v_sb if is_v else u_sb
                        nc.scalar.activation(dst[:, n, f, :], p_uv[:, q % 4, :], ACT.Silu,
                                             bias=bias[:, is_v * FB1 + f:is_v * FB1 + f + 1]).then_inc(uv_ready, 1)

                act.wait_ge(loaded, 16 * LOADS)
                chunk(0)
                with act.Fori(1, CPS) as c:
                    chunk(c)

            @block.vector
            def _(dve):
                dve.wait_ge(loaded, 16 * LOADS)

                def chunk(c):
                    cnt = Count(dve, own, OWN * c)
                    dve.wait_ge(uv_ready, NB * c + B * FB1)
                    if not first(c):
                        dve.wait_ge(product, B * c)
                    for f in range(FB1):
                        for n, which in ((0, 2), (1, 1)):
                            cnt.add(nc.vector.tensor_scalar(y_sb[:, n, f, :], v_sb[:, 1 - n, f, :],
                                                            toep[:, which, f:f + 1], None, ALU.mult))
                    cnt.wait()
                    for f in range(FB1):
                        for n in range(B):
                            cnt.add(nc.vector.scalar_tensor_tensor(out=y_sb[:, n, f, :], in0=v_sb[:, n, f, :],
                                                                   scalar=toep[:, 0, f:f + 1], in1=y_sb[:, n, f, :],
                                                                   op0=ALU.mult, op1=ALU.add))
                    cnt.wait()
                    for n in range(B):
                        dve.wait_ge(uv_ready, NB * c + B * FB1 + FB1 * (n + 1))
                        nc.vector.tensor_tensor(y_sb[:, n, :, :], y_sb[:, n, :, :], u_sb[:, n, :, :], ALU.mult).then_inc(g_ready, 1)
                    for n in range(B):
                        hh = h_all[:, at(n * CPS + c, TPC, TPC), :]
                        x = k.x[:, at(n * CPS + c, TPC, TPC), :]
                        dve.wait_ge(product, B * c + n + 1)
                        nc.vector.tensor_tensor(hh, p_o[:, n, :, :], hh, ALU.add).then_inc(taken, 1)
                        dve.wait_ge(taken, B * c + n + 1)
                        cnt.step(nc.vector.tensor_tensor(hh, hh, k.mod(1, n, GA), ALU.mult))
                        nc.vector.tensor_tensor(x, x, hh, ALU.add).then_inc(x3_ready, 1)
                        dve.wait_ge(x3_ready, B * c + n + 1)
                        row_stats(nc, k, n * CPS + c)
                    assert cnt.n == OWN

                chunk(0)
                with dve.Fori(1, CPS) as c:
                    chunk(c)


def route(nc, a, k, logits, xn_all):
    with ExitStack() as stack:
        m = Mem(nc, stack)
        iota, later, ones = m.sb("r_iota", [P, E1]), m.sb("r_later", [P, P]), m.sb("r_ones", [P, P])
        tiles = m.sb("r_tiles", [P, NTILES])
        best = m.sb("r_best", [P, 2, NT])
        same, rest = m.sb("r_same", [P, NT, E1]), m.sb("r_rest", [P, NT, E1])
        first_at = m.sb("r_first_at", [P, NT])
        onehot = m.sb("r_onehot", [P, 2, NT, E1])
        chosen, total = m.sb("r_chosen", [P, NT, E1]), m.sb("r_total", [P, NT, E1])
        run = m.sb("r_run", [P, 2, NT, E1])
        count_i = m.sb("r_count_i", [P, E1], I32)
        ntile, ends = m.sb("r_ntile", [P, E1]), m.sb("r_ends", [P, 2, E1])
        start = m.sb("r_start", [P, E1])
        slot = m.sb("r_slot", [P, NT])
        gap, weight_sum = m.sb("r_gap", [P, NT]), m.sb("r_weight_sum", [P, NT])
        owner, owner_f = m.sb("r_owner", [P, NTILES, E1]), m.sb("r_owner_f", [P, NTILES])
        p_rank, p_total = m.ps("p_rank", [P, NT, E1]), m.ps("p_total", [P, NT, E1])
        loaded, own, chosen_ready, counted = m.sem("r_loaded"), m.sem("r_own"), m.sem("r_chosen_ready"), m.sem("r_counted")
        gap_ready, exp_ready, slots_ready, scattered = (m.sem("r_gap_ready"), m.sem("r_exp_ready"),
                                                        m.sem("r_slots_ready"), m.sem("r_scattered"))
        LOADS = 4
        with nc.Block() as block:
            @block.sync
            def _(sp):
                for dst, src in ((iota, "iota8"), (later, "before"), (ones, "ones"), (tiles, "iota_tiles")):
                    sp.dma_start(dst[:, :], a[src]).then_inc(loaded, 16)
                sp.wait_ge(loaded, 16 * LOADS)

            @block.tensor
            def _(pe):
                pe.wait_ge(loaded, 16 * LOADS)
                pe.wait_ge(chosen_ready, 1)
                nc.tensor.matmul(p_rank[:, :, :], later[:, :], chosen[:, :, :], start=True, stop=True).then_inc(counted, 1)
                nc.tensor.matmul(p_total[:, :, :], ones[:, :], chosen[:, :, :], start=True, stop=True).then_inc(counted, 1)

            @block.scalar
            def _(act):
                act.wait_ge(gap_ready, 1)
                nc.scalar.activation(k.weights[:, 1, :], gap[:, :], ACT.Exp).then_inc(exp_ready, 1)

            @block.vector
            def _(dve):
                dve.wait_ge(loaded, 16 * LOADS)
                c = Count(dve, own)

                def tt(out, x, y, op):
                    c.step(nc.vector.tensor_tensor(out, x, y, op))

                def ts(out, x, s1, s2, op1, op2=None):
                    if op2 is None:
                        c.step(nc.vector.tensor_scalar(out, x, s1, None, op1))
                    else:
                        c.step(nc.vector.tensor_scalar(out, x, s1, s2, op1, op2))

                def wide(x, n=E1):
                    return x.unsqueeze(2).to_broadcast([P, NT, n])

                iota_all = iota[:, :].unsqueeze(1).to_broadcast([P, NT, E1])
                for q in range(2):
                    src = logits[:, :, :] if q == 0 else rest[:, :, :]
                    c.step(nc.vector.tensor_reduce(out=best[:, q, :], in_=src, op=ALU.max, axis=AX.X))
                    tt(same[:, :, :], src, wide(best[:, q, :]), ALU.is_equal)
                    c.step(nc.vector.scalar_tensor_tensor(out=same[:, :, :], in0=iota_all, scalar=0.0,
                                                          in1=same[:, :, :], op0=ALU.add, op1=ALU.mult))
                    c.step(nc.vector.tensor_reduce(out=first_at[:, :], in_=same[:, :, :], op=ALU.min, axis=AX.X))
                    tt(onehot[:, q, :, :], iota_all, wide(first_at[:, :]), ALU.is_equal)
                    if q == 0:
                        c.step(nc.vector.scalar_tensor_tensor(out=rest[:, :, :], in0=onehot[:, 0, :, :], scalar=MASKED,
                                                              in1=logits[:, :, :], op0=ALU.mult, op1=ALU.add))
                nc.vector.tensor_tensor(chosen[:, :, :], onehot[:, 0, :, :], onehot[:, 1, :, :], ALU.add).then_inc(chosen_ready, 1)
                nc.vector.tensor_tensor(gap[:, :], best[:, 1, :], best[:, 0, :], ALU.subtract).then_inc(gap_ready, 1)

                dve.wait_ge(exp_ready, 1)
                ts(weight_sum[:, :], k.weights[:, 1, :], 1.0, None, ALU.add)
                c.step(nc.vector.reciprocal(k.weights[:, 0, :], weight_sum[:, :]))
                tt(k.weights[:, 1, :], k.weights[:, 1, :], k.weights[:, 0, :], ALU.mult)

                dve.wait_ge(counted, 2)
                c.step(nc.vector.tensor_copy(total[:, :, :], p_total[:, :, :]))
                c.step(nc.vector.tensor_copy(run[:, 0, :, :], total[:, :, :]))
                now, step = 0, 1
                while step < NT:
                    c.add(nc.vector.tensor_copy(run[:, 1 - now, 0:step, :], run[:, now, 0:step, :]))
                    tt(run[:, 1 - now, step:NT, :], run[:, now, step:NT, :], run[:, now, 0:NT - step, :], ALU.add)
                    now, step = 1 - now, 2 * step
                ts(ends[:, 0, :], run[:, now, NT - 1, :], float(ST - 1), None, ALU.add)
                c.step(nc.vector.tensor_copy(count_i[:, :], ends[:, 0, :]))
                ts(count_i[:, :], count_i[:, :], ST.bit_length() - 1, None, ALU.logical_shift_right)
                c.step(nc.vector.tensor_copy(ntile[:, :], count_i[:, :]))
                c.step(nc.vector.tensor_copy(ends[:, 0, :], ntile[:, :]))
                at_end, step = 0, 1
                while step < E1:
                    c.add(nc.vector.tensor_copy(ends[:, 1 - at_end, 0:step], ends[:, at_end, 0:step]))
                    tt(ends[:, 1 - at_end, step:E1], ends[:, at_end, step:E1], ends[:, at_end, 0:E1 - step], ALU.add)
                    at_end, step = 1 - at_end, 2 * step
                tt(start[:, :], ends[:, at_end, :], ntile[:, :], ALU.subtract)
                ts(start[:, :], start[:, :], float(ST), None, ALU.mult)
                tt(run[:, now, :, :], run[:, now, :, :], total[:, :, :], ALU.subtract)
                tt(run[:, now, :, :], run[:, now, :, :], p_rank[:, :, :], ALU.add)
                tt(run[:, now, :, :], run[:, now, :, :], start[:, :].unsqueeze(1).to_broadcast([P, NT, E1]), ALU.add)
                for q in range(2):
                    tt(same[:, :, :], onehot[:, q, :, :], run[:, now, :, :], ALU.mult)
                    c.step(nc.vector.tensor_reduce(out=slot[:, :], in_=same[:, :, :], op=ALU.add, axis=AX.X))
                    nc.vector.tensor_copy(k.slots[:, q, :], slot[:, :]).then_inc(slots_ready, 1)
                    dve.wait_ge(slots_ready, q + 1)
                tt(owner[:, :, :], tiles[:, :].unsqueeze(2).to_broadcast([P, NTILES, E1]),
                   ends[:, at_end, :].unsqueeze(1).to_broadcast([P, NTILES, E1]), ALU.is_ge)
                c.step(nc.vector.tensor_reduce(out=owner_f[:, :], in_=owner[:, :, :], op=ALU.add, axis=AX.X))
                ts(owner_f[:, :], owner_f[:, :], float(E1 - 1), None, ALU.min)
                c.step(nc.vector.tensor_copy(k.owners[:, :], owner_f[:, :]))

            @block.gpsimd
            def _(pool):
                for q in range(2):
                    pool.wait_ge(slots_ready, q + 1)
                    for t in range(NT):
                        pool.indirect_dma_start(out=k.x_slots[:, :],
                                                out_offset=bass.IndirectOffsetOnAxis(ap=k.slots[:, q, t:t + 1], axis=0),
                                                in_=xn_all[:, t, :], in_offset=None).then_inc(scattered, 16)
                pool.wait_ge(scattered, 16 * 2 * NT)


def routed_experts(nc, a, k):
    with ExitStack() as stack:
        m = Mem(nc, stack)
        raw1 = m.sb("f_raw1", [P, 2, 2 * KT, FF])
        raw2 = m.sb("f_raw2", [P, 2, FB, D])
        w1 = m.sb("f_w1", [P, 2, 2 * KT, FF], F32R)
        w2 = m.sb("f_w2", [P, 2, FB, D], F32R)
        b1 = m.sb("f_b1", [P, 2, 2 * FB])
        b2 = m.sb("f_b2", [P, 2, D])
        x = m.sb("f_x", [P, SPT, D])
        xT = m.sb("f_xT", [P, 2, 2, KT, ST], F32R)
        gate = m.sb("f_gate", [P, 2, ST])
        hidden = m.sb("f_hidden", [P, 2, 2, ST], F32R)
        y = m.sb("f_y", [P, SPT, D])
        p_up = m.ps("p_up", [P, 2, 2, ST])
        p_t = m.ps("f_pt", [P, KT, ST])
        p_y = m.ps("p_y", [P, SPT, D])
        x_loaded = m.sem("f_x_loaded")
        w1_loaded, w2_loaded, b_loaded = ([m.sem(f"f_{what}_loaded{n}") for n in range(2)] for what in ("w1", "w2", "b"))
        turned, xT_high, xT_ready = m.sem("f_turned"), m.sem("f_xT_high"), m.sem("f_xT_ready")
        w_high, w_ready = m.sem("f_w_high"), m.sem("f_w_ready")
        up_psum, down_psum = m.sem("f_up_psum"), m.sem("f_down_psum")
        gate_ready, hidden_raw = m.sem("f_gate_ready"), m.sem("f_hidden_raw")
        hidden_high, hidden_ready = m.sem("f_hidden_high"), m.sem("f_hidden_ready")
        y_ready, y_stored = m.sem("f_y_ready"), m.sem("f_y_stored")
        pieces = [(1, 0), (2, 0), (1, 1), (1, 2), (2, 1), (1, 3)]
        PIECES, AHEAD = len(pieces), 3
        F1P, F2P = 2, FB // 2
        TURN_AT, AHEAD_AT = 3, FB - AHEAD

        def piece(q, one, two):
            which, n = pieces[q]
            if which == 1:
                return one[:, :, n * F1P * P:(n + 1) * F1P * P]
            return two[:, n * F2P:(n + 1) * F2P, :]

        def piece_raw(q, par):
            return piece(q, raw1[:, par, :, :], raw2[:, par, :, :])

        def piece_part(q, part):
            return piece(q, w1[:, part, :, :], w2[:, part, :, :])

        def all_tiles(engine, tile):
            tile(0, 0, 0)
            tile(1, 1, 0)
            with engine.Fori(1, NTILES // 2) as i:
                tile(2 * i, 0, i)
                tile(2 * i + 1, 1, i)
            for t in range(NTILES // 2 * 2, NTILES):
                tile(t, t % 2, t // 2)

        def early(t):
            return isinstance(t, int) and t < 2

        def last_tile(t):
            return isinstance(t, int) and t == NTILES - 1

        with nc.Block() as block:
            @block.sync
            def _(sp):
                def load(t, par):
                    if not first(t):
                        sp.wait_ge(turned, t)
                    sp.dma_start(x[:, :, :], k.x_slots[at(t, ST, ST), :].rearrange("(u p) d -> p u d", p=P)
                                 ).then_inc(x_loaded, 16)
                    if not early(t):
                        sp.wait_ge(w_ready, PIECES * (t - 1))
                    e = sp.value_load(k.owners[0:1, at(t, 1, 1)], min_val=0, max_val=E1 - 1)
                    for ab, src in enumerate((a["W1a"], a["W1b"])):
                        sp.dma_start(raw1[:, par, ab * KT:(ab + 1) * KT, :],
                                     src[bass.ds(e, 1), :, :].rearrange("o (k p) f -> p (o k) f", p=P)
                                     ).then_inc(w1_loaded[par], 16)
                    sp.dma_start(raw2[:, par, :, :], a["W2"][bass.ds(e, 1), :, :].rearrange("o (k p) d -> p (o k) d", p=P)
                                 ).then_inc(w2_loaded[par], 16)
                    if not early(t):
                        sp.wait_ge(y_ready, t - 1)
                    sp.dma_start(b1[:, par, :], a["b1"][bass.ds(e, 1), :, :].rearrange("o p f -> (o p) f")
                                 ).then_inc(b_loaded[par], 16)
                    sp.dma_start(b2[:, par, :], a["b2"][bass.ds(e, 1), :].rearrange("o d -> (o d)").partition_broadcast(P)
                                 ).then_inc(b_loaded[par], 16)

                def store(t):
                    sp.wait_ge(y_ready, t + 1)
                    sp.dma_start(k.y_slots[at(t, ST, ST), :].rearrange("(u p) d -> p u d", p=P), y[:, :, :]
                                 ).then_inc(y_stored, 16)

                load(0, 0)
                load(1, 1)
                load(2, 0)
                store(0)
                with sp.Fori(1, NTILES // 2) as i:
                    load(2 * i + 1, 1)
                    store(2 * i - 1)
                    load(2 * i + 2, 0)
                    store(2 * i)
                store(NTILES - 2)
                store(NTILES - 1)
                sp.wait_ge(y_stored, 16 * NTILES)

            @block.tensor
            def _(pe):
                def turn(t):
                    pe.wait_ge(x_loaded, 16 * t + 16)
                    if not first(t):
                        pe.wait_ge(xT_ready, t)
                    for kt in range(KT):
                        for u in range(SPT):
                            last = nc.tensor.transpose(p_t[:, kt, u * P:(u + 1) * P], x[:, u, kt * P:(kt + 1) * P],
                                                       k.ident[:, :])
                    last.then_inc(turned, 1)

                def up(t, par, f):
                    if f % F1P == 0:
                        pe.wait_ge(w_ready, PIECES * t + pieces.index((1, f // F1P)) + 1)
                    if f >= 2 or not first(t):
                        pe.wait_ge(hidden_raw, FB * t + f - 1)
                    for ab in range(2):
                        for kt in range(KT):
                            for wh, xh in PRODUCTS:
                                last = nc.tensor.matmul(
                                    p_up[:, f % 2, ab, :],
                                    w1[:, wh, ab * KT + kt, f * P:(f + 1) * P], xT[:, par, xh, kt, :],
                                    start=(kt, wh, xh) == (0, HI, HI), stop=(kt, wh, xh) == (KT - 1, LO, HI))
                    last.then_inc(up_psum, 1)

                def down(t, par, f):
                    if f % F2P == 0:
                        pe.wait_ge(w_ready, PIECES * t + pieces.index((2, f // F2P)) + 1)
                    pe.wait_ge(hidden_ready, FB * t + f + 1)
                    if f == 0 and not first(t):
                        pe.wait_ge(y_ready, t)
                    for u in range(SPT):
                        for wh, hh in PRODUCTS:
                            last = nc.tensor.matmul(p_y[:, u, :], hidden[:, f % 2, hh, u * P:(u + 1) * P],
                                                    w2[:, wh, f, :],
                                                    start=(f, wh, hh) == (0, HI, HI) and u % 2 == 0,
                                                    stop=(f, wh, hh) == (FB - 1, LO, HI) and u % 2 == 1)
                    last.then_inc(down_psum, 1)

                def tile(t, par, turns):
                    pe.wait_ge(xT_ready, t + 1)
                    for f in range(FB):
                        up(t, par, f)
                        if f == TURN_AT and not last_tile(t):
                            turn(t + 1)
                        if f:
                            down(t, par, f - 1)
                        elif not first(t):
                            down(t - 1, 1 - par, FB - 1)

                turn(0)
                all_tiles(pe, tile)
                down(NTILES - 1, (NTILES - 1) % 2, FB - 1)

            @block.scalar
            def _(act):
                def round_x(t, par):
                    act.wait_ge(turned, t + 1)
                    nc.scalar.activation(xT[:, par, HI, :, :], p_t[:, :, :], ACT.Copy).then_inc(xT_high, 1)

                def round_weights(t, par, q, turns):
                    which, n = pieces[q]
                    if which == 1:
                        if n == 0:
                            act.wait_ge(w1_loaded[par], 16 * 2 * (turns + 1))
                        if not first(t):
                            act.wait_ge(up_psum, FB * (t - 1) + (n + 1) * F1P)
                    else:
                        if n == 0:
                            act.wait_ge(w2_loaded[par], 16 * (turns + 1))
                        if not first(t):
                            act.wait_ge(down_psum, FB * (t - 1) + (n + 1) * F2P)
                    nc.scalar.activation(piece_part(q, HI), piece_raw(q, par), ACT.Copy).then_inc(w_high, 1)

                def tile(t, par, turns):
                    act.wait_ge(b_loaded[par], 16 * 2 * (turns + 1))
                    for f in range(FB):
                        n = FB * t + f + 1
                        act.wait_ge(up_psum, n)
                        if f >= 2 or not first(t):
                            act.wait_ge(hidden_ready, n - 2)
                        nc.scalar.activation(gate[:, f % 2, :], p_up[:, f % 2, 0, :], ACT.Silu,
                                             bias=b1[:, par, f:f + 1]).then_inc(gate_ready, 1)
                        act.wait_ge(hidden_raw, n)
                        if f >= 2 or not first(t):
                            act.wait_ge(down_psum, n - 2)
                        nc.scalar.activation(hidden[:, f % 2, HI, :], gate[:, f % 2, :], ACT.Copy).then_inc(hidden_high, 1)
                        if f == TURN_AT and not last_tile(t):
                            round_x(t + 1, 1 - par)
                        if f < PIECES - AHEAD:
                            round_weights(t, par, AHEAD + f, turns)
                        if f >= AHEAD_AT and not last_tile(t):
                            round_weights(t + 1, 1 - par, f - AHEAD_AT, turns + (1 if par else 0))

                round_x(0, 0)
                for q in range(AHEAD):
                    round_weights(0, 0, q, 0)
                all_tiles(act, tile)

            @block.vector
            def _(dve):
                def rest_of_x(t, par):
                    dve.wait_ge(xT_high, t + 1)
                    nc.vector.tensor_tensor(xT[:, par, LO, :, :], p_t[:, :, :], xT[:, par, HI, :, :],
                                            ALU.subtract).then_inc(xT_ready, 1)

                def hide(t, par, f):
                    n = FB * t + f + 1
                    dve.wait_ge(gate_ready, n)
                    nc.vector.scalar_tensor_tensor(out=gate[:, f % 2, :], in0=p_up[:, f % 2, 1, :],
                                                   scalar=b1[:, par, FB + f:FB + f + 1], in1=gate[:, f % 2, :],
                                                   op0=ALU.add, op1=ALU.mult).then_inc(hidden_raw, 1)
                    dve.wait_ge(hidden_high, n)
                    nc.vector.tensor_tensor(hidden[:, f % 2, LO, :], gate[:, f % 2, :], hidden[:, f % 2, HI, :],
                                            ALU.subtract).then_inc(hidden_ready, 1)

                def take_y(t, par):
                    dve.wait_ge(down_psum, FB * t + FB)
                    if not first(t):
                        dve.wait_ge(y_stored, 16 * t)
                    nc.vector.tensor_tensor(y[:, :, :], p_y[:, :, :],
                                            b2[:, par, :].unsqueeze(1).to_broadcast([P, SPT, D]), ALU.add).then_inc(y_ready, 1)

                def tile(t, par, turns):
                    for f in range(FB):
                        hide(t, par, f)
                        if f == 0 and not first(t):
                            take_y(t - 1, 1 - par)
                        if f == TURN_AT and not last_tile(t):
                            rest_of_x(t + 1, 1 - par)

                rest_of_x(0, 0)
                all_tiles(dve, tile)
                take_y(NTILES - 1, (NTILES - 1) % 2)

            @block.gpsimd
            def _(pool):
                def tile(t, par, turns):
                    for q in range(PIECES):
                        pool.wait_ge(w_high, PIECES * t + q + 1)
                        nc.gpsimd.tensor_tensor(piece_part(q, LO), piece_raw(q, par), piece_part(q, HI),
                                                ALU.subtract).then_inc(w_ready, 1)

                all_tiles(pool, tile)


def combine(nc, a, k, out):
    with ExitStack() as stack:
        m = Mem(nc, stack)
        ys = m.sb("g_ys", [P, 2, 2, TPC, D])
        res = m.sb("g_res", [P, 2, TPC, D])
        gathered = [m.sem(f"g_gathered{n}") for n in range(2)]
        stored = [m.sem(f"g_stored{n}") for n in range(2)]
        done, own = m.sem("g_done"), m.sem("g_own")
        OWN = 2 * TPC + 1
        with nc.Block() as block:
            @block.gpsimd
            def _(pool):
                for i in range(NCH):
                    if i >= 2:
                        pool.wait_ge(done, i - 1)
                    for u in range(TPC):
                        for q in range(2):
                            t = i * TPC + u
                            pool.indirect_dma_start(out=ys[:, i % 2, q, u, :], out_offset=None, in_=k.y_slots[:, :],
                                                    in_offset=bass.IndirectOffsetOnAxis(ap=k.slots[:, q, t:t + 1], axis=0),
                                                    ).then_inc(gathered[i % 2], 16)

            @block.vector
            def _(dve):
                def chunk(i, par, turns, early):
                    c = Count(dve, own, OWN * i)
                    dve.wait_ge(gathered[par], 16 * 2 * TPC * (turns + 1))
                    if not early:
                        dve.wait_ge(stored[par], 16 * turns)
                    for u in range(TPC):
                        c.add(nc.vector.tensor_scalar(res[:, par, u, :], ys[:, par, 0, u, :],
                                                      k.weights[:, 0, at(i * TPC + u, 1, 1)], None, ALU.mult))
                    c.wait()
                    for u in range(TPC):
                        c.add(nc.vector.scalar_tensor_tensor(out=res[:, par, u, :], in0=ys[:, par, 1, u, :],
                                                             scalar=k.weights[:, 1, at(i * TPC + u, 1, 1)],
                                                             in1=res[:, par, u, :], op0=ALU.mult, op1=ALU.add))
                    c.wait()
                    c.step(nc.vector.tensor_tensor(res[:, par, :, :], res[:, par, :, :], k.mod(1, i // CPS, GB), ALU.mult))
                    nc.vector.tensor_tensor(res[:, par, :, :], res[:, par, :, :], k.x[:, at(i, TPC, TPC), :],
                                            ALU.add).then_inc(done, 1)
                    assert c.n == OWN

                chunk(0, 0, 0, True)
                chunk(1, 1, 0, True)
                with dve.Fori(1, NCH // 2) as i:
                    chunk(2 * i, 0, i, False)
                    chunk(2 * i + 1, 1, i, False)

            @block.sync
            def _(sp):
                with sp.Fori(0, NCH // 2) as i:
                    for par in range(2):
                        sp.wait_ge(done, 2 * i + par + 1)
                        sp.dma_start(out[at(2 * i + par, CH, CH), :].rearrange("(u p) d -> p u d", p=P),
                                     res[:, par, :, :]).then_inc(stored[par], 16)
                for par in range(2):
                    sp.wait_ge(stored[par], 16 * (NCH // 2))


class Kept:

    def __init__(self, nc, m):
        self.ident = m.sb("ident", [P, P])
        self.identb = m.sb("identb", [P, P], BF16)
        self.masks = m.sb("masks", [P, 2, P], BF16)
        self.mods = [None, m.sb("mods1", [P, B, 6, D])]
        self.stats = m.sb("stats", [P, NT, 6])
        self.mean, self.ve, self.rstd = m.sb("mean", [P, NT]), m.sb("ve", [P, NT]), m.sb("rstd", [P, NT])
        self.spread, self.neghalf = m.sb("spread", [P, NT]), m.sb("neghalf", [P, NT])
        self.x = m.sb("x", [P, NT, D])
        self.constants_loaded = m.sem("constants_loaded")
        self.power_set, self.ve_ready, self.rstd_ready = m.sem("power_set"), m.sem("ve_ready"), m.sem("rstd_ready")
        self.scaled, self.x2_ready = m.sem("c_scaled"), m.sem("c_x2_ready")

        self.weights = m.sb("weights", [P, 2, NT])
        self.slots = m.sb("slots", [P, 2, NT], U32)
        self.owners = m.sb("owners", [P, NTILES], I32)

        def dram(name, shape, dt=F32):
            return nc.dram_tensor(name, shape, dt, kind="Internal").ap()

        self.qk_rows = dram("qk_scr", [2 * SPLIT * B * D, T], BF16)
        self.v_scr = dram("v_scr", [NS, P, JT, HG * VW])
        self.x_slots, self.y_slots = dram("x_slots", [NSLOT, D]), dram("y_slots", [NSLOT, D])
        self.max_scr = dram("max_scr", [2, SPLIT * HG, CH], BF16)
        self.qk_scr = {(qk, part): self.qk_rows[(qk * SPLIT + part) * B * D:(qk * SPLIT + part + 1) * B * D, :]
                       for qk in range(2) for part in range(SPLIT)}

    def mod(self, layer, b, which):
        return self.mods[layer][:, at(b, 1, 1), which, :].to_broadcast([P, TPC, D])

    def mod1(self, layer, b, which):
        return self.mods[layer][:, at(b, 1, 1), which, :].rearrange("p o d -> p (o d)")


def program(nc, a, out):
    with ExitStack() as stack:
        m = Mem(nc, stack)
        k = Kept(nc, m)
        with ExitStack() as block0:
            k.mods[0] = Mem(nc, block0).sb("mods0", [P, B, 6, D])
            modulation(nc, a, k)
            projections(nc, a, k)
            attention(nc, a, k)
            output_projection(nc, a, k)
            top1_experts(nc, a, k)
        with ExitStack() as mixing:
            mm = Mem(nc, mixing)
            h_all = mm.sb("h_all", [P, NT, D])
            xnT_all = mm.sb("xnT_all", [P, KT, NTOK])
            second_norm(nc, a, k, 2, "n1_", SA, CA, h_all, xnT_all, None, None)
            mix(nc, a, k, h_all, xnT_all)
        with ExitStack() as routing:
            mm = Mem(nc, routing)
            xn_all = mm.sb("xn_all", [P, NT, D])
            logits = mm.sb("logits", [P, NT, E1])
            second_norm(nc, a, k, 3, "n2_", SB_, CB, xn_all, None, a["ln_w"], logits)
            route(nc, a, k, logits, xn_all)
        routed_experts(nc, a, k)
        combine(nc, a, k, out)


def lay_out(inputs):
    g = {n: np.asarray(v) for n, v in inputs.items()}
    swap = np.arange(D) ^ 1
    a = {"x": g["L0_attn_X"].reshape(NTOK, D)}
    for n in range(2):
        a[f"cT{n}"] = g[f"L{n}_c"].T.reshape(KT, P, B).transpose(1, 0, 2)
        a[f"wmod{n}"] = g[f"L{n}_wmod"]
    wq, wk, wv = (g[f"L0_attn_W_{c}"] for c in "qkv")
    a["wqkv"] = np.concatenate([wq.T, wq[swap].T, wk.T, wk[swap].T, wv.T], axis=1)
    a["woT"] = g["L0_attn_W_o"].T
    a["expertT"] = g["L0_ffn_expert_w"].transpose(2, 0, 1).reshape(D, E0 * D)
    a["gateT"] = g["L0_ffn_gate_w"].T
    a["iota8"] = np.tile(np.arange(E0, dtype=np.float32) - E0, (P, 1))
    a["w_uv"] = np.concatenate([g["L1_attn_u_w"].T, g["L1_attn_v_w"].T], axis=1)
    a["b_uv"] = np.concatenate([g["L1_attn_u_b"], g["L1_attn_v_b"]]).reshape(2 * FB1, P).T
    a["o_wT"] = g["L1_attn_o_w"].T
    a["o_b"] = g["L1_attn_o_b"]
    heads = np.stack([g["L1_attn_zero"][:, 0], g["L1_attn_pos"][:, 0], g["L1_attn_neg"][:, 0]])
    a["toep"] = np.repeat(heads, F1 // heads.shape[1], axis=1).reshape(3, FB1, P).transpose(2, 0, 1)
    a["ln_w"], a["Wg"], a["bg"] = g["L1_ffn_ln_w"], g["L1_ffn_Wg"], g["L1_ffn_bg"]
    a["W1a"], a["W1b"], a["W2"], a["b2"] = g["L1_ffn_W1a"], g["L1_ffn_W1b"], g["L1_ffn_W2"], g["L1_ffn_b2"]
    b1 = np.concatenate([g["L1_ffn_b1a"], g["L1_ffn_b1b"]], axis=1)
    a["b1"] = b1.reshape(E1, 2 * FB, P).transpose(0, 2, 1)
    a["before"] = np.triu(np.ones((P, P), np.float32), 1)
    a["ones"] = np.ones((P, P), np.float32)
    a["iota_tiles"] = np.tile(np.arange(NTILES, dtype=np.float32), (P, 1))
    theta = np.power(np.float32(10000.0), np.float32(-2.0) * np.arange(DH // 2, dtype=np.float32) / np.float32(DH))
    angle = (np.arange(T, dtype=np.float32)[:, None] * theta[None, :]).T.repeat(2, axis=0)
    sign = np.where(np.arange(DH) % 2 == 0, -1, 1).astype(np.float32)[:, None]
    a["trig"] = np.stack([np.tile(np.cos(angle), (P // DH, 1)), np.tile(sign * np.sin(angle), (P // DH, 1))], axis=1)
    a["ident"] = np.eye(P, dtype=np.float32)
    later = np.triu(np.full((P, P), MASKED, np.float32), 1)
    a["masks"] = np.stack([later, later.T], axis=1)
    return {n: np.ascontiguousarray(v) for n, v in a.items()}


def kernel(**inputs):
    import concourse.bacc as bacc
    from concourse.bass_utils import run_bass_kernel_spmd

    nc = bacc.Bacc("TRN2", target_bir_lowering=False, num_devices=1)
    arrays = lay_out(inputs)
    a = {n: nc.dram_tensor(f"in_{n}", v.shape, mybir.dt.from_np(v.dtype), kind="ExternalInput").ap()
         for n, v in arrays.items()}
    out = nc.dram_tensor("out", [NTOK, D], F32, kind="ExternalOutput").ap()
    program(nc, a, out)
    r = run_bass_kernel_spmd(nc, [{f"in_{n}": v for n, v in arrays.items()}], core_ids=[0])
    return r.results[0]["out"].reshape(B, T, D)
```
